# Optimizing a Trainium2 kernel written in Bass

```python
import numpy as np
import jax
import jax.numpy as jnp

def _softmax(x, axis=-1):
    return jax.nn.softmax(x, axis=axis)

def _gelu(x):
    return jax.nn.gelu(x, approximate=True)

def _silu(x):
    return jax.nn.silu(x)

def _sigmoid(x):
    return jax.nn.sigmoid(x)

def _layernorm(x, axis=-1, eps=1e-05):
    m = jnp.mean(x, axis=axis, keepdims=True)
    v = jnp.var(x, axis=axis, keepdims=True)
    return (x - m) / jnp.sqrt(v + eps)

def _scatter_add(tgt, idx, src, axis=0):
    return tgt.at[idx].add(src)

def _segment_sum(src, seg, n):
    return jax.ops.segment_sum(src, seg, n)
kernel_name = 'mk_metaformer_d4_conv_nhwc128_r4_e77193'

def setup_inputs(seed: int=0):
    np.random.seed(seed)
    _w = jnp.asarray

    def _rec_inputs():
        import jax
        import jax.numpy as jnp
        _gk = jax.random.key(seed)
        x = -0.0002928 + 1 * jax.random.normal(jax.random.fold_in(_gk, 1), (2, 32, 32, 32), jnp.float32)
        return x
    x = _rec_inputs()

    def _L0_conv_setup():
        import jax, jax.numpy as jnp
        from jax import lax
        import numpy as np
        D_MODEL = 32
        D_INNER = 64
        D_STATE = 16
        DT_RANK = 8
        WIN = 8
        K = 4

        def _xy2d(n, x, y):
            d = 0
            s = n // 2
            while s > 0:
                rx = 1 if x & s > 0 else 0
                ry = 1 if y & s > 0 else 0
                d += s * s * (3 * rx ^ ry)
                if ry == 0:
                    if rx == 1:
                        x = s - 1 - x
                        y = s - 1 - y
                    x, y = (y, x)
                s //= 2
            return d
        _hidx = np.array([_xy2d(WIN, x, y) for y in range(WIN) for x in range(WIN)])
        SORTED_IDX = np.argsort(_hidx)
        INV_IDX = np.argsort(SORTED_IDX)

        def _forward(x, in_proj_w, conv_w, conv_b, x_proj_w, dt_projs_w, dt_projs_b, A_logs, Ds, ln_w, ln_b, out_proj_w):
            B, H, W, C = x.shape
            win = WIN
            xz = x @ in_proj_w.T
            xv, z = jnp.split(xz, 2, axis=-1)
            xc = xv.transpose(0, 3, 1, 2)
            xc = lax.conv_general_dilated(xc, conv_w, (1, 1), 'SAME', feature_group_count=D_INNER, dimension_numbers=('NCHW', 'OIHW', 'NCHW'))
            xc = jax.nn.silu(xc + conv_b[None, :, None, None])
            xw = xc.reshape(B, D_INNER, H // win, win, W // win, win)
            xw = xw.transpose(0, 2, 4, 1, 3, 5).reshape(-1, D_INNER, win, win)
            nwB = xw.shape[0]
            HW = win * win
            L = 2 * HW
            xh = xw.reshape(nwB, D_INNER, HW)[:, :, SORTED_IDX]
            xwh = xw.transpose(0, 1, 3, 2).reshape(nwB, D_INNER, HW)[:, :, SORTED_IDX]
            Bm = nwB // 2

            def merge(t):
                return jnp.stack([t[:Bm], t[Bm:]], axis=-1).reshape(Bm, D_INNER, L)
            x_hwwh = jnp.stack([merge(xh), merge(xwh)], axis=1)
            xs = jnp.concatenate([x_hwwh, x_hwwh[..., ::-1]], axis=1)
            x_dbl = jnp.einsum('bkdl,kcd->bkcl', xs, x_proj_w)
            dts, Bs, Cs = jnp.split(x_dbl, [DT_RANK, DT_RANK + D_STATE], axis=2)
            dts = jnp.einsum('bkrl,kdr->bkdl', dts, dt_projs_w)
            dts = jax.nn.softplus(dts + dt_projs_b[None, :, :, None])
            A = -jnp.exp(A_logs).reshape(K, D_INNER, D_STATE)
            Dsr = Ds.reshape(K, D_INNER)
            us = xs.transpose(3, 0, 1, 2)
            dt_t = dts.transpose(3, 0, 1, 2)
            B_t = Bs.transpose(3, 0, 1, 2)
            C_t = Cs.transpose(3, 0, 1, 2)

            def step(h, inp):
                u, dt, Bl, Cl = inp
                dA = jnp.exp(dt[..., None] * A)
                h = h * dA + (dt * u)[..., None] * Bl[:, :, None, :]
                y = jnp.einsum('bkdn,bkn->bkd', h, Cl)
                return (h, y)
            h0 = jnp.zeros((Bm, K, D_INNER, D_STATE), xs.dtype)
            _, ys = lax.scan(step, h0, (us, dt_t, B_t, C_t))
            out_y = ys.transpose(1, 2, 3, 0) + Dsr[None, :, :, None] * xs
            inv = out_y[:, 2:4][..., ::-1]

            def unmerge(t):
                return jnp.concatenate([t[:, :, 0::2], t[:, :, 1::2]], axis=0)
            wh_y = unmerge(out_y[:, 1] + inv[:, 1])
            wh_y = wh_y[:, :, INV_IDX].reshape(nwB, D_INNER, win, win).transpose(0, 1, 3, 2)
            yy = unmerge(out_y[:, 0] + inv[:, 0])
            yy = yy[:, :, INV_IDX].reshape(nwB, D_INNER, win, win)
            y = (yy + wh_y).transpose(0, 2, 3, 1)
            mu = y.mean(-1, keepdims=True)
            var = y.var(-1, keepdims=True)
            y = (y - mu) / jnp.sqrt(var + 1e-05) * ln_w + ln_b
            y = y.reshape(B, H // win, W // win, win, win, D_INNER)
            y = y.transpose(0, 1, 3, 2, 4, 5).reshape(B, H, W, D_INNER)
            y = y * jax.nn.silu(z)
            return y @ out_proj_w.T
        key = jax.random.key(seed)
        ks = jax.random.split(key, 12)
        f32 = jnp.float32
        x = jax.random.normal(ks[0], (2, 32, 32, D_MODEL), dtype=f32)
        in_proj_w = jax.random.normal(ks[1], (2 * D_INNER, D_MODEL), dtype=f32) * 0.02
        conv_w = jax.random.normal(ks[2], (D_INNER, 1, 3, 3), dtype=f32) * 0.1
        conv_b = jax.random.normal(ks[3], (D_INNER,), dtype=f32) * 0.02
        x_proj_w = jax.random.normal(ks[4], (K, DT_RANK + 2 * D_STATE, D_INNER), dtype=f32) * 0.05
        dt_projs_w = jax.random.normal(ks[5], (K, D_INNER, DT_RANK), dtype=f32) * DT_RANK ** (-0.5)
        dt_projs_b = jax.random.uniform(ks[6], (K, D_INNER), dtype=f32, minval=-5.0, maxval=-2.0)
        A_logs = jnp.tile(jnp.log(jnp.arange(1, D_STATE + 1, dtype=f32))[None, :], (K * D_INNER, 1))
        Ds = jnp.ones((K * D_INNER,), f32)
        ln_w = jnp.ones((D_INNER,), f32)
        ln_b = jnp.zeros((D_INNER,), f32)
        out_proj_w = jax.random.normal(ks[7], (D_MODEL, D_INNER), dtype=f32) * 0.02
        return {'x': x, 'in_proj_w': in_proj_w, 'conv_w': conv_w, 'conv_b': conv_b, 'x_proj_w': x_proj_w, 'dt_projs_w': dt_projs_w, 'dt_projs_b': dt_projs_b, 'A_logs': A_logs, 'Ds': Ds, 'ln_w': ln_w, 'ln_b': ln_b, 'out_proj_w': out_proj_w}
    _L0_conv_all = _L0_conv_setup()
    _L0_conv_in = {k: v for k, v in _L0_conv_all.items() if k in ('in_proj_w', 'conv_w', 'conv_b', 'x_proj_w', 'dt_projs_w', 'dt_projs_b', 'A_logs', 'Ds', 'ln_w', 'ln_b', 'out_proj_w')}
    del _L0_conv_all

    def _L0_ffn_setup():
        import jax, jax.numpy as jnp
        import numpy as np
        BN_EPS = 1e-05
        key = jax.random.key(seed)
        k1, k2, k3 = jax.random.split(key, 3)
        B, T, I, H = (16, 512, 32, 32)
        x = jax.random.normal(k1, (B, T, I), dtype=jnp.float32)
        W = jax.random.normal(k2, (H, I), dtype=jnp.float32) * (1.0 / np.sqrt(I))
        V = jnp.linalg.qr(jax.random.normal(k3, (H, H), dtype=jnp.float32))[0]
        gamma = jnp.ones((H,), dtype=jnp.float32)
        beta = jnp.zeros((H,), dtype=jnp.float32)
        return {'x': x, 'W': W, 'V': V, 'gamma': gamma, 'beta': beta}
    _L0_ffn_all = _L0_ffn_setup()
    _L0_ffn_in = {k: v for k, v in _L0_ffn_all.items() if k in ('W', 'V', 'gamma', 'beta')}
    del _L0_ffn_all

    def _L1_conv_setup():
        import jax, jax.numpy as jnp
        import numpy as np
        M_FILTERS = 5
        key = jax.random.key(seed)
        ks = jax.random.split(key, 5)
        X = jax.random.normal(ks[0], (32, 56, 56, 32), dtype=jnp.float32)
        W = jax.random.normal(ks[1], (3, 3, 32, 32), dtype=jnp.float32) * 0.1
        beta = jax.random.normal(ks[2], (3,), dtype=jnp.float32)
        v = jax.random.normal(ks[3], (3,), dtype=jnp.float32) * 0.1
        bias = jax.random.normal(ks[4], (3,), dtype=jnp.float32) * 0.1
        return {'X': X, 'W': W, 'beta': beta, 'v': v, 'bias': bias, 'stride': 1}
    _L1_conv_all = _L1_conv_setup()
    _L1_conv_in = {k: v for k, v in _L1_conv_all.items() if k in ('W', 'beta', 'v', 'bias')}
    del _L1_conv_all

    def _L1_ffn_setup():
        import jax, jax.numpy as jnp
        import numpy as np
        B, S, D, E, H, O, K = (128, 512, 32, 16, 128, 32, 8)
        key = jax.random.key(seed)
        k0, k1, k2, k3 = jax.random.split(key, 4)
        x = jax.random.normal(k0, (B, S, D), dtype=jnp.float32)
        gate_w = jax.random.normal(k1, (E, D), dtype=jnp.float32) * (1.0 / np.sqrt(D))
        gate_b = jnp.zeros((E,), dtype=jnp.float32)
        weight1 = jax.random.uniform(k2, (E, D + 1, H), dtype=jnp.float32, minval=-1.0, maxval=1.0) * (1.0 / np.sqrt(D + 1))
        weight2 = jax.random.uniform(k3, (E, H + 1, O), dtype=jnp.float32, minval=-1.0, maxval=1.0) * (1.0 / np.sqrt(H + 1))
        return {'x': x, 'gate_w': gate_w, 'gate_b': gate_b, 'weight1': weight1, 'weight2': weight2}
    _L1_ffn_all = _L1_ffn_setup()
    _L1_ffn_in = {k: v for k, v in _L1_ffn_all.items() if k in ('gate_w', 'gate_b', 'weight1', 'weight2')}
    del _L1_ffn_all

    def _L2_conv_setup():
        import jax, jax.numpy as jnp
        import numpy as np
        B, M, IN_DIM, OUT_DIM, BASIS = (4, 32, 32, 32, 15)
        NEG_SLOPE = 0.01

        def eops_2_to_2(x):
            x = jnp.transpose(x, (0, 3, 1, 2))
            m = x.shape[-1]
            shp = x.shape
            eye = jnp.eye(m, dtype=x.dtype)
            diag = jnp.diagonal(x, axis1=-2, axis2=-1)
            sum_diag = jnp.sum(diag, axis=-1, keepdims=True)
            sum_rows = jnp.sum(x, axis=-1)
            sum_cols = jnp.sum(x, axis=-2)
            sum_all = jnp.sum(sum_rows, axis=-1, keepdims=True)
            bt = lambda a: jnp.broadcast_to(a, shp)
            ops = [diag[..., :, None] * eye, sum_diag[..., None] * eye, sum_rows[..., :, None] * eye, sum_cols[..., :, None] * eye, sum_all[..., None] * eye, bt(sum_cols[..., None, :]), bt(sum_rows[..., None, :]), bt(sum_cols[..., :, None]), bt(sum_rows[..., :, None]), x, jnp.swapaxes(x, -1, -2), bt(diag[..., :, None]), bt(diag[..., None, :]), bt(sum_diag[..., None]), bt(sum_all[..., None])]
            return jnp.stack(ops, axis=2)
        key = jax.random.key(seed)
        k1, k2 = jax.random.split(key)
        inputs = jax.random.normal(k1, (B, M, M, IN_DIM), dtype=jnp.float32)
        std = np.sqrt(2.0 / (IN_DIM + OUT_DIM + BASIS)).astype(np.float32)
        coefs = jax.random.normal(k2, (IN_DIM, OUT_DIM, BASIS), dtype=jnp.float32) * std
        bias = jnp.zeros((1, 1, 1, OUT_DIM), dtype=jnp.float32)
        diag_bias = jnp.zeros((1, 1, 1, OUT_DIM), dtype=jnp.float32)
        return {'inputs': inputs, 'coefs': coefs, 'bias': bias, 'diag_bias': diag_bias}
    _L2_conv_all = _L2_conv_setup()
    _L2_conv_in = {k: v for k, v in _L2_conv_all.items() if k in ('coefs', 'bias', 'diag_bias')}
    del _L2_conv_all

    def _L2_ffn_setup():
        import jax, jax.numpy as jnp
        import numpy as np
        BN_EPS = 1e-05
        key = jax.random.key(seed)
        k1, k2, k3 = jax.random.split(key, 3)
        B, T, I, H = (16, 512, 32, 32)
        x = jax.random.normal(k1, (B, T, I), dtype=jnp.float32)
        W = jax.random.normal(k2, (H, I), dtype=jnp.float32) * (1.0 / np.sqrt(I))
        V = jnp.linalg.qr(jax.random.normal(k3, (H, H), dtype=jnp.float32))[0]
        gamma = jnp.ones((H,), dtype=jnp.float32)
        beta = jnp.zeros((H,), dtype=jnp.float32)
        return {'x': x, 'W': W, 'V': V, 'gamma': gamma, 'beta': beta}
    _L2_ffn_all = _L2_ffn_setup()
    _L2_ffn_in = {k: v for k, v in _L2_ffn_all.items() if k in ('W', 'V', 'gamma', 'beta')}
    del _L2_ffn_all

    def _L3_conv_setup():
        import jax, jax.numpy as jnp
        import numpy as np
        HEADS = 2
        DIM = 32
        DIM_HEAD = 16
        INNER = DIM_HEAD * HEADS
        SCALE = DIM_HEAD ** (-0.5)
        WS1 = (8, 8)
        WS2 = (16, 16)
        SEQ1 = WS1[0] * WS1[1]
        SEQ2 = (32 // HEADS) ** 2 * 4 // SEQ1
        SEQ3 = WS2[0] * WS2[1]
        SEQ4 = (32 // HEADS) ** 2 * 4 // SEQ3

        def _partition(t, b0, b1):
            B, H, W, c = t.shape
            t = t.reshape(B, H // b0, b0, W // b1, b1, c)
            t = t.transpose(0, 1, 3, 2, 4, 5)
            return t.reshape(B, H // b0 * (W // b1), b0 * b1, c)

        def _unpartition(t, H, W, b0, b1):
            B, n, m, c = t.shape
            t = t.reshape(B, H // b0, W // b1, b0, b1, c)
            t = t.transpose(0, 1, 3, 2, 4, 5)
            return t.reshape(B, H, W, c)

        def _window_attn(q, k, v, pos):
            B, n, m, c = q.shape
            d = c // HEADS
            qh = q.reshape(B, n, m, HEADS, d).transpose(0, 1, 3, 2, 4)
            kh = k.reshape(B, n, m, HEADS, d).transpose(0, 1, 3, 2, 4)
            vh = v.reshape(B, n, m, HEADS, d).transpose(0, 1, 3, 2, 4)
            sim = jnp.einsum('bnhid,bnhjd->bnhij', qh * SCALE, kh) + pos
            attn = jax.nn.softmax(sim, axis=-1)
            out = jnp.einsum('bnhij,bnhjd->bnhid', attn, vh)
            return out.transpose(0, 1, 3, 2, 4).reshape(B, n, m, c)
        key = jax.random.key(seed)
        ks = jax.random.split(key, 10)
        B, H, W = (8, 32, 32)
        x = jax.random.normal(ks[0], (B, H, W, DIM), dtype=jnp.float32)
        Wq = jax.random.normal(ks[1], (DIM, INNER), dtype=jnp.float32) * 0.02
        Wk = jax.random.normal(ks[2], (DIM, INNER), dtype=jnp.float32) * 0.02
        Wv = jax.random.normal(ks[3], (DIM, INNER), dtype=jnp.float32) * 0.02
        pos1 = jax.random.normal(ks[4], (1, 1, HEADS, SEQ1, SEQ1), dtype=jnp.float32)
        pos2 = jax.random.normal(ks[5], (1, 1, HEADS, SEQ2, SEQ2), dtype=jnp.float32)
        pos3 = jax.random.normal(ks[6], (1, 1, HEADS, SEQ3, SEQ3), dtype=jnp.float32)
        pos4 = jax.random.normal(ks[7], (1, 1, HEADS, SEQ4, SEQ4), dtype=jnp.float32)
        Wo = jax.random.normal(ks[8], (INNER, DIM), dtype=jnp.float32) * 0.02
        bo = jax.random.normal(ks[9], (DIM,), dtype=jnp.float32) * 0.02
        return {'x': x, 'Wq': Wq, 'Wk': Wk, 'Wv': Wv, 'pos1': pos1, 'pos2': pos2, 'pos3': pos3, 'pos4': pos4, 'Wo': Wo, 'bo': bo}
    _L3_conv_all = _L3_conv_setup()
    _L3_conv_in = {k: v for k, v in _L3_conv_all.items() if k in ('Wq', 'Wk', 'Wv', 'pos1', 'pos2', 'pos3', 'pos4', 'Wo', 'bo')}
    del _L3_conv_all

    def _L3_ffn_setup():
        import jax, jax.numpy as jnp
        import numpy as np
        B, S, D, E, H, O, K = (128, 512, 32, 16, 128, 32, 8)
        key = jax.random.key(seed)
        k0, k1, k2, k3 = jax.random.split(key, 4)
        x = jax.random.normal(k0, (B, S, D), dtype=jnp.float32)
        gate_w = jax.random.normal(k1, (E, D), dtype=jnp.float32) * (1.0 / np.sqrt(D))
        gate_b = jnp.zeros((E,), dtype=jnp.float32)
        weight1 = jax.random.uniform(k2, (E, D + 1, H), dtype=jnp.float32, minval=-1.0, maxval=1.0) * (1.0 / np.sqrt(D + 1))
        weight2 = jax.random.uniform(k3, (E, H + 1, O), dtype=jnp.float32, minval=-1.0, maxval=1.0) * (1.0 / np.sqrt(H + 1))
        return {'x': x, 'gate_w': gate_w, 'gate_b': gate_b, 'weight1': weight1, 'weight2': weight2}
    _L3_ffn_all = _L3_ffn_setup()
    _L3_ffn_in = {k: v for k, v in _L3_ffn_all.items() if k in ('gate_w', 'gate_b', 'weight1', 'weight2')}
    del _L3_ffn_all
    return {'x': x, 'L0_conv_in_proj_w': _L0_conv_in['in_proj_w'], 'L0_conv_conv_w': _L0_conv_in['conv_w'], 'L0_conv_conv_b': _L0_conv_in['conv_b'], 'L0_conv_x_proj_w': _L0_conv_in['x_proj_w'], 'L0_conv_dt_projs_w': _L0_conv_in['dt_projs_w'], 'L0_conv_dt_projs_b': _L0_conv_in['dt_projs_b'], 'L0_conv_A_logs': _L0_conv_in['A_logs'], 'L0_conv_Ds': _L0_conv_in['Ds'], 'L0_conv_ln_w': _L0_conv_in['ln_w'], 'L0_conv_ln_b': _L0_conv_in['ln_b'], 'L0_conv_out_proj_w': _L0_conv_in['out_proj_w'], 'L0_ffn_W': _L0_ffn_in['W'], 'L0_ffn_V': _L0_ffn_in['V'], 'L0_ffn_gamma': _L0_ffn_in['gamma'], 'L0_ffn_beta': _L0_ffn_in['beta'], 'L1_conv_W': _L1_conv_in['W'], 'L1_conv_beta': _L1_conv_in['beta'], 'L1_conv_v': _L1_conv_in['v'], 'L1_conv_bias': _L1_conv_in['bias'], 'L1_ffn_gate_w': _L1_ffn_in['gate_w'], 'L1_ffn_gate_b': _L1_ffn_in['gate_b'], 'L1_ffn_weight1': _L1_ffn_in['weight1'], 'L1_ffn_weight2': _L1_ffn_in['weight2'], 'L2_conv_coefs': _L2_conv_in['coefs'], 'L2_conv_bias': _L2_conv_in['bias'], 'L2_conv_diag_bias': _L2_conv_in['diag_bias'], 'L2_ffn_W': _L2_ffn_in['W'], 'L2_ffn_V': _L2_ffn_in['V'], 'L2_ffn_gamma': _L2_ffn_in['gamma'], 'L2_ffn_beta': _L2_ffn_in['beta'], 'L3_conv_Wq': _L3_conv_in['Wq'], 'L3_conv_Wk': _L3_conv_in['Wk'], 'L3_conv_Wv': _L3_conv_in['Wv'], 'L3_conv_pos1': _L3_conv_in['pos1'], 'L3_conv_pos2': _L3_conv_in['pos2'], 'L3_conv_pos3': _L3_conv_in['pos3'], 'L3_conv_pos4': _L3_conv_in['pos4'], 'L3_conv_Wo': _L3_conv_in['Wo'], 'L3_conv_bo': _L3_conv_in['bo'], 'L3_ffn_gate_w': _L3_ffn_in['gate_w'], 'L3_ffn_gate_b': _L3_ffn_in['gate_b'], 'L3_ffn_weight1': _L3_ffn_in['weight1'], 'L3_ffn_weight2': _L3_ffn_in['weight2']}

def reference(x, L0_conv_in_proj_w, L0_conv_conv_w, L0_conv_conv_b, L0_conv_x_proj_w, L0_conv_dt_projs_w, L0_conv_dt_projs_b, L0_conv_A_logs, L0_conv_Ds, L0_conv_ln_w, L0_conv_ln_b, L0_conv_out_proj_w, L0_ffn_W, L0_ffn_V, L0_ffn_gamma, L0_ffn_beta, L1_conv_W, L1_conv_beta, L1_conv_v, L1_conv_bias, L1_ffn_gate_w, L1_ffn_gate_b, L1_ffn_weight1, L1_ffn_weight2, L2_conv_coefs, L2_conv_bias, L2_conv_diag_bias, L2_ffn_W, L2_ffn_V, L2_ffn_gamma, L2_ffn_beta, L3_conv_Wq, L3_conv_Wk, L3_conv_Wv, L3_conv_pos1, L3_conv_pos2, L3_conv_pos3, L3_conv_pos4, L3_conv_Wo, L3_conv_bo, L3_ffn_gate_w, L3_ffn_gate_b, L3_ffn_weight1, L3_ffn_weight2):
    import jax
    import jax.numpy as jnp

    def _L0_conv_ref(x, in_proj_w, conv_w, conv_b, x_proj_w, dt_projs_w, dt_projs_b, A_logs, Ds, ln_w, ln_b, out_proj_w):
        import jax, jax.numpy as jnp
        from jax import lax
        import numpy as np
        D_MODEL = 32
        D_INNER = 64
        D_STATE = 16
        DT_RANK = 8
        WIN = 8
        K = 4

        def _xy2d(n, x, y):
            d = 0
            s = n // 2
            while s > 0:
                rx = 1 if x & s > 0 else 0
                ry = 1 if y & s > 0 else 0
                d += s * s * (3 * rx ^ ry)
                if ry == 0:
                    if rx == 1:
                        x = s - 1 - x
                        y = s - 1 - y
                    x, y = (y, x)
                s //= 2
            return d
        _hidx = np.array([_xy2d(WIN, x, y) for y in range(WIN) for x in range(WIN)])
        SORTED_IDX = np.argsort(_hidx)
        INV_IDX = np.argsort(SORTED_IDX)

        def _forward(x, in_proj_w, conv_w, conv_b, x_proj_w, dt_projs_w, dt_projs_b, A_logs, Ds, ln_w, ln_b, out_proj_w):
            B, H, W, C = x.shape
            win = WIN
            xz = x @ in_proj_w.T
            xv, z = jnp.split(xz, 2, axis=-1)
            xc = xv.transpose(0, 3, 1, 2)
            xc = lax.conv_general_dilated(xc, conv_w, (1, 1), 'SAME', feature_group_count=D_INNER, dimension_numbers=('NCHW', 'OIHW', 'NCHW'))
            xc = jax.nn.silu(xc + conv_b[None, :, None, None])
            xw = xc.reshape(B, D_INNER, H // win, win, W // win, win)
            xw = xw.transpose(0, 2, 4, 1, 3, 5).reshape(-1, D_INNER, win, win)
            nwB = xw.shape[0]
            HW = win * win
            L = 2 * HW
            xh = xw.reshape(nwB, D_INNER, HW)[:, :, SORTED_IDX]
            xwh = xw.transpose(0, 1, 3, 2).reshape(nwB, D_INNER, HW)[:, :, SORTED_IDX]
            Bm = nwB // 2

            def merge(t):
                return jnp.stack([t[:Bm], t[Bm:]], axis=-1).reshape(Bm, D_INNER, L)
            x_hwwh = jnp.stack([merge(xh), merge(xwh)], axis=1)
            xs = jnp.concatenate([x_hwwh, x_hwwh[..., ::-1]], axis=1)
            x_dbl = jnp.einsum('bkdl,kcd->bkcl', xs, x_proj_w)
            dts, Bs, Cs = jnp.split(x_dbl, [DT_RANK, DT_RANK + D_STATE], axis=2)
            dts = jnp.einsum('bkrl,kdr->bkdl', dts, dt_projs_w)
            dts = jax.nn.softplus(dts + dt_projs_b[None, :, :, None])
            A = -jnp.exp(A_logs).reshape(K, D_INNER, D_STATE)
            Dsr = Ds.reshape(K, D_INNER)
            us = xs.transpose(3, 0, 1, 2)
            dt_t = dts.transpose(3, 0, 1, 2)
            B_t = Bs.transpose(3, 0, 1, 2)
            C_t = Cs.transpose(3, 0, 1, 2)

            def step(h, inp):
                u, dt, Bl, Cl = inp
                dA = jnp.exp(dt[..., None] * A)
                h = h * dA + (dt * u)[..., None] * Bl[:, :, None, :]
                y = jnp.einsum('bkdn,bkn->bkd', h, Cl)
                return (h, y)
            h0 = jnp.zeros((Bm, K, D_INNER, D_STATE), xs.dtype)
            _, ys = lax.scan(step, h0, (us, dt_t, B_t, C_t))
            out_y = ys.transpose(1, 2, 3, 0) + Dsr[None, :, :, None] * xs
            inv = out_y[:, 2:4][..., ::-1]

            def unmerge(t):
                return jnp.concatenate([t[:, :, 0::2], t[:, :, 1::2]], axis=0)
            wh_y = unmerge(out_y[:, 1] + inv[:, 1])
            wh_y = wh_y[:, :, INV_IDX].reshape(nwB, D_INNER, win, win).transpose(0, 1, 3, 2)
            yy = unmerge(out_y[:, 0] + inv[:, 0])
            yy = yy[:, :, INV_IDX].reshape(nwB, D_INNER, win, win)
            y = (yy + wh_y).transpose(0, 2, 3, 1)
            mu = y.mean(-1, keepdims=True)
            var = y.var(-1, keepdims=True)
            y = (y - mu) / jnp.sqrt(var + 1e-05) * ln_w + ln_b
            y = y.reshape(B, H // win, W // win, win, win, D_INNER)
            y = y.transpose(0, 1, 3, 2, 4, 5).reshape(B, H, W, D_INNER)
            y = y * jax.nn.silu(z)
            return y @ out_proj_w.T
        return _forward(x, in_proj_w, conv_w, conv_b, x_proj_w, dt_projs_w, dt_projs_b, A_logs, Ds, ln_w, ln_b, out_proj_w)

    def _L0_ffn_ref(x, W, V, gamma, beta):
        import jax, jax.numpy as jnp
        import numpy as np
        BN_EPS = 1e-05
        B, T, H = (x.shape[0], x.shape[1], W.shape[0])
        Wx = jnp.einsum('bti,hi->bth', x, W)
        flat = Wx.reshape(B * T, H)
        mean = jnp.mean(flat, axis=0)
        var = jnp.var(flat, axis=0)
        Wx = ((flat - mean) * jax.lax.rsqrt(var + BN_EPS) * gamma + beta).reshape(B, T, H)
        Vt = V.T

        def step(yt, wx_t):
            yt = jax.nn.sigmoid(wx_t + yt @ Vt)
            return (yt, yt)
        y0 = jnp.zeros((B, H), dtype=Wx.dtype)
        _, ys = jax.lax.scan(step, y0, jnp.swapaxes(Wx, 0, 1))
        return jnp.swapaxes(ys, 0, 1)

    def _L1_conv_ref(X, W, beta, v, bias, stride):
        import jax, jax.numpy as jnp
        import numpy as np
        M_FILTERS = 5
        M = M_FILTERS
        N = beta.shape[0]
        mean = jnp.mean(W)
        std = jnp.sqrt(jnp.var(W))
        us = jnp.asarray([-1.0 + i * 2.0 / (M - 1) for i in range(M)], dtype=W.dtype)
        B = jnp.sign(W[None] - mean + us[:, None, None, None, None] * std)
        Bf = B.reshape(M, -1).T
        wf = W.reshape(-1)
        alpha = jnp.linalg.solve(Bf.T @ Bf, Bf.T @ wf)
        W_eff = jnp.einsum('m,mhwio->hwio', alpha, B)
        sum_alpha = jnp.sum(alpha)

        def conv(A):
            return jax.lax.conv_general_dilated(A, W_eff, window_strides=(stride, stride), padding='SAME', dimension_numbers=('NHWC', 'HWIO', 'NHWC'))
        out = jnp.zeros(conv(jnp.zeros_like(X)).shape, dtype=X.dtype)
        for n in range(N):
            An = jnp.sign(jnp.clip(X + v[n], 0.0, 1.0) - 0.5)
            out = out + beta[n] * (conv(An) + sum_alpha * bias[n])
        return out

    def _L1_ffn_ref(x, gate_w, gate_b, weight1, weight2):
        import jax, jax.numpy as jnp
        import numpy as np
        B, S, D, E, H, O, K = (128, 512, 32, 16, 128, 32, 8)
        Bn, Sn, Dn = x.shape
        logits = jnp.einsum('bsd,ed->bse', x, gate_w) + gate_b
        probs = jax.nn.softmax(logits, axis=1)
        vals, idx = jax.lax.top_k(probs.transpose(0, 2, 1), K)
        topv = vals.transpose(0, 2, 1)
        topi = idx.transpose(0, 2, 1)
        flat_idx = topi.reshape(Bn, K * E)
        gathered = jnp.take_along_axis(x, flat_idx[:, :, None], axis=1)
        gathered = gathered.reshape(Bn, K, E, Dn)
        pooled = jnp.einsum('bked,bke->bed', gathered, topv)
        ones = jnp.ones((E, Bn, 1), dtype=x.dtype)
        h = jnp.concatenate([pooled.transpose(1, 0, 2), ones], axis=-1)
        h = jax.nn.gelu(jnp.einsum('ebd,edh->ebh', h, weight1), approximate=False)
        h = jnp.concatenate([h, ones], axis=-1)
        out = jnp.einsum('ebh,eho->ebo', h, weight2)
        out = out.transpose(1, 0, 2)
        weighted = jnp.einsum('beo,bke->bkeo', out, topv).reshape(Bn, K * E, O)
        outputs = jnp.zeros((Bn, Sn, O), dtype=x.dtype)
        outputs = outputs.at[jnp.arange(Bn)[:, None], flat_idx].add(weighted)
        return outputs

    def _L2_conv_ref(inputs, coefs, bias, diag_bias):
        import jax, jax.numpy as jnp
        import numpy as np
        B, M, IN_DIM, OUT_DIM, BASIS = (4, 32, 32, 32, 15)
        NEG_SLOPE = 0.01

        def eops_2_to_2(x):
            x = jnp.transpose(x, (0, 3, 1, 2))
            m = x.shape[-1]
            shp = x.shape
            eye = jnp.eye(m, dtype=x.dtype)
            diag = jnp.diagonal(x, axis1=-2, axis2=-1)
            sum_diag = jnp.sum(diag, axis=-1, keepdims=True)
            sum_rows = jnp.sum(x, axis=-1)
            sum_cols = jnp.sum(x, axis=-2)
            sum_all = jnp.sum(sum_rows, axis=-1, keepdims=True)
            bt = lambda a: jnp.broadcast_to(a, shp)
            ops = [diag[..., :, None] * eye, sum_diag[..., None] * eye, sum_rows[..., :, None] * eye, sum_cols[..., :, None] * eye, sum_all[..., None] * eye, bt(sum_cols[..., None, :]), bt(sum_rows[..., None, :]), bt(sum_cols[..., :, None]), bt(sum_rows[..., :, None]), x, jnp.swapaxes(x, -1, -2), bt(diag[..., :, None]), bt(diag[..., None, :]), bt(sum_diag[..., None]), bt(sum_all[..., None])]
            return jnp.stack(ops, axis=2)
        ops = eops_2_to_2(inputs)
        out = jnp.einsum('dsb,ndbij->nijs', coefs, ops)
        diag_eye = jnp.eye(inputs.shape[1], dtype=inputs.dtype)[None, :, :, None]
        out = out + bias + diag_eye * diag_bias
        return jax.nn.leaky_relu(out, negative_slope=NEG_SLOPE)

    def _L2_ffn_ref(x, W, V, gamma, beta):
        import jax, jax.numpy as jnp
        import numpy as np
        BN_EPS = 1e-05
        B, T, H = (x.shape[0], x.shape[1], W.shape[0])
        Wx = jnp.einsum('bti,hi->bth', x, W)
        flat = Wx.reshape(B * T, H)
        mean = jnp.mean(flat, axis=0)
        var = jnp.var(flat, axis=0)
        Wx = ((flat - mean) * jax.lax.rsqrt(var + BN_EPS) * gamma + beta).reshape(B, T, H)
        Vt = V.T

        def step(yt, wx_t):
            yt = jax.nn.sigmoid(wx_t + yt @ Vt)
            return (yt, yt)
        y0 = jnp.zeros((B, H), dtype=Wx.dtype)
        _, ys = jax.lax.scan(step, y0, jnp.swapaxes(Wx, 0, 1))
        return jnp.swapaxes(ys, 0, 1)

    def _L3_conv_ref(x, Wq, Wk, Wv, pos1, pos2, pos3, pos4, Wo, bo):
        import jax, jax.numpy as jnp
        import numpy as np
        HEADS = 2
        DIM = 32
        DIM_HEAD = 16
        INNER = DIM_HEAD * HEADS
        SCALE = DIM_HEAD ** (-0.5)
        WS1 = (8, 8)
        WS2 = (16, 16)
        SEQ1 = WS1[0] * WS1[1]
        SEQ2 = (32 // HEADS) ** 2 * 4 // SEQ1
        SEQ3 = WS2[0] * WS2[1]
        SEQ4 = (32 // HEADS) ** 2 * 4 // SEQ3

        def _partition(t, b0, b1):
            B, H, W, c = t.shape
            t = t.reshape(B, H // b0, b0, W // b1, b1, c)
            t = t.transpose(0, 1, 3, 2, 4, 5)
            return t.reshape(B, H // b0 * (W // b1), b0 * b1, c)

        def _unpartition(t, H, W, b0, b1):
            B, n, m, c = t.shape
            t = t.reshape(B, H // b0, W // b1, b0, b1, c)
            t = t.transpose(0, 1, 3, 2, 4, 5)
            return t.reshape(B, H, W, c)

        def _window_attn(q, k, v, pos):
            B, n, m, c = q.shape
            d = c // HEADS
            qh = q.reshape(B, n, m, HEADS, d).transpose(0, 1, 3, 2, 4)
            kh = k.reshape(B, n, m, HEADS, d).transpose(0, 1, 3, 2, 4)
            vh = v.reshape(B, n, m, HEADS, d).transpose(0, 1, 3, 2, 4)
            sim = jnp.einsum('bnhid,bnhjd->bnhij', qh * SCALE, kh) + pos
            attn = jax.nn.softmax(sim, axis=-1)
            out = jnp.einsum('bnhij,bnhjd->bnhid', attn, vh)
            return out.transpose(0, 1, 3, 2, 4).reshape(B, n, m, c)
        B, H, W, _ = x.shape
        q = x @ Wq
        k = x @ Wk
        v = x @ Wv
        c = q.shape[-1]
        cq = c // 4
        qs = [q[..., i * cq:(i + 1) * cq] for i in range(4)]
        ks = [k[..., i * cq:(i + 1) * cq] for i in range(4)]
        vs = [v[..., i * cq:(i + 1) * cq] for i in range(4)]
        q1 = _partition(qs[0], *WS1)
        k1 = _partition(ks[0], *WS1)
        v1 = _partition(vs[0], *WS1)
        out1 = _window_attn(q1, k1, v1, pos1)
        q2 = _partition(qs[1], *WS1).transpose(0, 2, 1, 3)
        k2 = _partition(ks[1], *WS1).transpose(0, 2, 1, 3)
        v2 = _partition(vs[1], *WS1).transpose(0, 2, 1, 3)
        out2 = _window_attn(q2, k2, v2, pos2).transpose(0, 2, 1, 3)
        out_1 = jnp.concatenate([out1, out2], axis=-1)
        out_1 = _unpartition(out_1, H, W, *WS1)
        q3 = _partition(qs[2], *WS2)
        k3 = _partition(ks[2], *WS2)
        v3 = _partition(vs[2], *WS2)
        out3 = _window_attn(q3, k3, v3, pos3)
        q4 = _partition(qs[3], *WS2).transpose(0, 2, 1, 3)
        k4 = _partition(ks[3], *WS2).transpose(0, 2, 1, 3)
        v4 = _partition(vs[3], *WS2).transpose(0, 2, 1, 3)
        out4 = _window_attn(q4, k4, v4, pos4).transpose(0, 2, 1, 3)
        out_2 = jnp.concatenate([out3, out4], axis=-1)
        out_2 = _unpartition(out_2, H, W, *WS2)
        out = jnp.concatenate([out_1, out_2], axis=-1)
        return out @ Wo + bo

    def _L3_ffn_ref(x, gate_w, gate_b, weight1, weight2):
        import jax, jax.numpy as jnp
        import numpy as np
        B, S, D, E, H, O, K = (128, 512, 32, 16, 128, 32, 8)
        Bn, Sn, Dn = x.shape
        logits = jnp.einsum('bsd,ed->bse', x, gate_w) + gate_b
        probs = jax.nn.softmax(logits, axis=1)
        vals, idx = jax.lax.top_k(probs.transpose(0, 2, 1), K)
        topv = vals.transpose(0, 2, 1)
        topi = idx.transpose(0, 2, 1)
        flat_idx = topi.reshape(Bn, K * E)
        gathered = jnp.take_along_axis(x, flat_idx[:, :, None], axis=1)
        gathered = gathered.reshape(Bn, K, E, Dn)
        pooled = jnp.einsum('bked,bke->bed', gathered, topv)
        ones = jnp.ones((E, Bn, 1), dtype=x.dtype)
        h = jnp.concatenate([pooled.transpose(1, 0, 2), ones], axis=-1)
        h = jax.nn.gelu(jnp.einsum('ebd,edh->ebh', h, weight1), approximate=False)
        h = jnp.concatenate([h, ones], axis=-1)
        out = jnp.einsum('ebh,eho->ebo', h, weight2)
        out = out.transpose(1, 0, 2)
        weighted = jnp.einsum('beo,bke->bkeo', out, topv).reshape(Bn, K * E, O)
        outputs = jnp.zeros((Bn, Sn, O), dtype=x.dtype)
        outputs = outputs.at[jnp.arange(Bn)[:, None], flat_idx].add(weighted)
        return outputs

    def _gn(v, G=32, eps=1e-05):
        B_, H_, W_, C_ = v.shape
        g = v.reshape(B_, H_, W_, G, C_ // G)
        m = jnp.mean(g, axis=(1, 2, 4), keepdims=True)
        s = jnp.var(g, axis=(1, 2, 4), keepdims=True)
        return ((g - m) / jnp.sqrt(s + eps)).reshape(v.shape)

    def _ln_c(v, eps=1e-06):
        m = jnp.mean(v, axis=-1, keepdims=True)
        s = jnp.var(v, axis=-1, keepdims=True)
        return (v - m) / jnp.sqrt(s + eps)

    def _ln_t(v, eps=1e-05):
        m = jnp.mean(v, axis=-1, keepdims=True)
        s = jnp.var(v, axis=-1, keepdims=True)
        return (v - m) / jnp.sqrt(s + eps)

    def _to_tokens(v):
        B_, H_, W_, C_ = v.shape
        return v.reshape(B_, H_ * W_, C_)

    def _from_tokens(t, like):
        return t.reshape(like.shape)
    x = x + _L0_conv_ref(_ln_c(x), L0_conv_in_proj_w, L0_conv_conv_w, L0_conv_conv_b, L0_conv_x_proj_w, L0_conv_dt_projs_w, L0_conv_dt_projs_b, L0_conv_A_logs, L0_conv_Ds, L0_conv_ln_w, L0_conv_ln_b, L0_conv_out_proj_w)
    t = _to_tokens(x)
    t = t + _L0_ffn_ref(_ln_t(t), L0_ffn_W, L0_ffn_V, L0_ffn_gamma, L0_ffn_beta)
    x = _from_tokens(t, x)
    x = x + _L1_conv_ref(_ln_c(x), L1_conv_W, L1_conv_beta, L1_conv_v, L1_conv_bias, 1)
    t = _to_tokens(x)
    t = t + _L1_ffn_ref(_ln_t(t), L1_ffn_gate_w, L1_ffn_gate_b, L1_ffn_weight1, L1_ffn_weight2)
    x = _from_tokens(t, x)
    x = x + _L2_conv_ref(_ln_c(x), L2_conv_coefs, L2_conv_bias, L2_conv_diag_bias)
    t = _to_tokens(x)
    t = t + _L2_ffn_ref(_ln_t(t), L2_ffn_W, L2_ffn_V, L2_ffn_gamma, L2_ffn_beta)
    x = _from_tokens(t, x)
    x = x + _L3_conv_ref(_ln_c(x), L3_conv_Wq, L3_conv_Wk, L3_conv_Wv, L3_conv_pos1, L3_conv_pos2, L3_conv_pos3, L3_conv_pos4, L3_conv_Wo, L3_conv_bo)
    t = _to_tokens(x)
    t = t + _L3_ffn_ref(_ln_t(t), L3_ffn_gate_w, L3_ffn_gate_b, L3_ffn_weight1, L3_ffn_weight2)
    x = _from_tokens(t, x)
    return x

_drawn_inputs = setup_inputs


def setup_inputs(seed=0):
    import zlib

    import numpy as np

    out = dict(_drawn_inputs(seed))
    spreads = {'L0_conv_Ds': (1.0, 0.6),
     'L0_conv_ln_w': (1.0, 0.6),
     'L0_conv_ln_b': (0.0, 0.8),
     'L0_ffn_gamma': (1.0, 0.6),
     'L0_ffn_beta': (0.0, 0.1),
     'L1_ffn_gate_b': (0.0, 2.0),
     'L2_conv_bias': (0.0, 2.0),
     'L2_conv_diag_bias': (0.0, 2.0),
     'L2_ffn_gamma': (1.0, 0.6),
     'L2_ffn_beta': (0.0, 2.0),
     'L3_ffn_gate_b': (0.0, 0.8)}
    factors = {'L0_conv_in_proj_w': 6.319,
     'L0_conv_conv_w': 7.977,
     'L0_conv_conv_b': 8.0,
     'L0_conv_x_proj_w': 8.0,
     'L0_conv_dt_projs_w': 8.0,
     'L0_conv_dt_projs_b': 8.0,
     'L0_conv_A_logs': 8.0,
     'L0_conv_out_proj_w': 7.863,
     'L1_conv_bias': 190.448,
     'L1_ffn_gate_w': 23.508,
     'L1_ffn_weight1': 24.415,
     'L1_ffn_weight2': 8.0,
     'L2_ffn_W': 200.0,
     'L2_ffn_V': 200.0,
     'L3_conv_Wq': 64.0,
     'L3_conv_Wk': 64.0,
     'L3_conv_Wv': 64.0,
     'L3_conv_pos1': 64.0,
     'L3_conv_pos2': 64.0,
     'L3_conv_pos3': 64.0,
     'L3_conv_pos4': 64.0,
     'L3_conv_Wo': 64.0,
     'L3_conv_bo': 200.0,
     'L3_ffn_gate_w': 64.0,
     'L3_ffn_weight1': 64.0,
     'L3_ffn_weight2': 64.0}
    for name, (base, spread) in spreads.items():
        noise = np.random.default_rng([zlib.crc32(name.encode()), seed]).standard_normal(out[name].shape)
        drawn = base * np.exp(spread * noise) if base else spread * noise
        out[name] = jnp.asarray(drawn.astype(out[name].dtype))
    for name, factor in factors.items():
        out[name] = (out[name] * factor).astype(out[name].dtype)
    return out
```

```python
import numpy as np
import concourse.bass as bass
from concourse import mybir
from contextlib import ExitStack

F32 = mybir.dt.float32
BF16 = mybir.dt.bfloat16
I32 = mybir.dt.int32
ACT = mybir.ActivationFunctionType
ALU = mybir.AluOpType
AX_X = mybir.AxisListType.X

NB, SIDE, C = 2, 32, 32
T = SIDE * SIDE
R = NB * C
D = 64
NS = 16
WIN = 8
NW = (SIDE // WIN) ** 2
POS = WIN * WIN
L = NB * POS
RANK = 8
BANK = 512
E, HID, TOPK = 16, 128, 8
NLEV = 5
NACT = 3
NBASIS = 15
HC_SCALE = 0.25
MASKED = -1e30


class Signals(dict):

    def __init__(self, nc, ctx):
        super().__init__()
        self.nc, self.ctx = nc, ctx

    def __missing__(self, name):
        self[name] = self.ctx.enter_context(self.nc.semaphore(name))
        return self[name]


class Chain:

    def __init__(self, eng, sem):
        self.eng, self.sem, self.n = eng, sem, 0

    def __call__(self, ins):
        self.n += 1
        ins.then_inc(self.sem, 1)
        self.eng.wait_ge(self.sem, self.n)


def build_program(nc, io):
    with ExitStack() as ctx:
        sig = Signals(nc, ctx)
        chain_n = {"dve": 0, "act": 0, "pool": 0}

        def sb(name, shape, dt=F32, stack=ctx):
            return stack.enter_context(nc.sbuf_tensor(name, shape, dt))

        def ps(name, shape, dt=F32, stack=ctx):
            return stack.enter_context(nc.psum_tensor(name, shape, dt))

        def chain(eng, name):
            c = Chain(eng, sig["chain_" + name])
            c.n = chain_n[name]
            return c

        def unchain(c, name):
            chain_n[name] = c.n

        ident = sb("ident", [128, 128])
        ones64 = sb("ones64", [R, R])
        eps6 = sb("eps6", [128, 1])
        eps5 = sb("eps5", [128, 1])
        x = sb("x", [R, T])
        xn = sb("xn", [R, T])
        xn_tok = sb("xn_tok", [128, T // 128, R])
        ln_sq = sb("ln_sq", [128, 2, 4 * R])
        ln_stat = sb("ln_stat", [128, 2, 5, 4 * NB])
        ln_warm = sb("ln_warm", [128, 1])

        ln_uses = [0]

        class Norm:

            def __init__(self, p_tok, p_back, eps, apart=False, k=None):
                if k is None:
                    k = ln_uses[0]
                    ln_uses[0] += 1
                self.k, self.eps, self.apart = k, eps, apart
                bank = (lambda h: 0) if apart else (lambda h: h * BANK)
                self.turned = [p_tok[:, bank(h):bank(h) + 4 * R] for h in range(2)]
                self.back = [p_back[:, bank(h):bank(h) + BANK] for h in range(2)]

            def at(self, name, h):
                return sig[name], 2 * self.k + h + 1

            def step(self, i, h):
                return sig["ln_step"], 10 * self.k + (5 * h + i if self.apart else 2 * i + h) + 1

            def turn(self, pe, h, j):
                t = (4 * h + j) * 128
                ins = pe.transpose(self.turned[h][:, j * R:(j + 1) * R], x[:, t:t + 128], ident[0:R, 0:R])
                if j == 3:
                    ins.then_inc(sig["ln_turned"], 1)

            def turn_back(self, pe, h, j):
                if j == 0:
                    pe.wait_ge(*self.at("ln_scaled", h))
                ins = pe.transpose(self.back[h][:, j * 128:(j + 1) * 128], xn_tok[:, 4 * h + j], ident[:])
                if j == 3:
                    ins.then_inc(sig["ln_back"], 1)

            def pe(self, pe):
                for move in (self.turn, self.turn_back):
                    for h in range(2):
                        for j in range(4):
                            move(pe, h, j)

            def dve(self, dve, hs=(0, 1)):
                by_token = lambda t: t.rearrange("p (g c) -> p g c", c=C)
                spread = lambda t: t.rearrange("p (g a) -> p g a", a=1).broadcast_to([128, 4 * NB, C])
                tok = lambda h: xn_tok[:, 4 * h:4 * h + 4].rearrange("p j r -> p (j r)")
                for h in hs:
                    dve.wait_ge(*self.at("ln_turned", h))
                    dve.tensor_reduce(ln_stat[:, h, 0], by_token(self.turned[h]), AX_X, ALU.add).then_inc(sig["ln_step"], 1)
                for h in hs:
                    dve.wait_ge(*self.step(0, h))
                    dve.tensor_scalar(ln_stat[:, h, 1], ln_stat[:, h, 0], 1.0 / C, None, ALU.mult).then_inc(sig["ln_step"], 1)
                for h in hs:
                    dve.wait_ge(*self.step(1, h))
                    dve.tensor_tensor(by_token(tok(h)), by_token(self.turned[h]), spread(ln_stat[:, h, 1]), ALU.subtract).then_inc(sig["ln_step"], 1)
                for h in hs:
                    dve.wait_ge(*self.step(2, h))
                    dve.tensor_tensor(ln_sq[:, h], tok(h), tok(h), ALU.mult).then_inc(sig["ln_step"], 1)
                for h in hs:
                    dve.wait_ge(*self.step(3, h))
                    dve.tensor_reduce(ln_stat[:, h, 2], by_token(ln_sq[:, h]), AX_X, ALU.add).then_inc(sig["ln_square"], 1)
                for h in hs:
                    dve.wait_ge(*self.at("ln_sd", h))
                    dve.reciprocal(ln_stat[:, h, 4], ln_stat[:, h, 3]).then_inc(sig["ln_step"], 1)
                    dve.wait_ge(*self.step(4, h))
                    dve.tensor_tensor(by_token(tok(h)), by_token(tok(h)), spread(ln_stat[:, h, 4]), ALU.mult).then_inc(sig["ln_scaled"], 1)
                if self.apart:
                    for h in hs:
                        dve.wait_ge(*self.at("ln_back", h))
                        dve.tensor_copy(xn[:, h * BANK:(h + 1) * BANK], self.back[h]).then_inc(sig["ln_out"], 1)

            def act_roots(self, act, h):
                act.wait_ge(*self.at("ln_square", h))
                act.activation(ln_stat[:, h, 3], ln_stat[:, h, 2], ACT.Sqrt, bias=self.eps[:, 0:1], scale=1.0 / C).then_inc(sig["ln_sd"], 1)

            def act(self, act):
                act.activation(ln_warm[:], self.eps[:], ACT.Sqrt)
                for h in range(2):
                    self.act_roots(act, h)
                for h in range(2):
                    act.wait_ge(*self.at("ln_back", h))
                    act.copy(xn[:, h * BANK:(h + 1) * BANK], self.back[h]).then_inc(sig["ln_out"], 1)

            def wait_out(self, eng, h=1):
                eng.wait_ge(sig["ln_out"], 2 * self.k + h + 1)

            def wait_tokens(self, eng):
                eng.wait_ge(sig["ln_scaled"], 2 * self.k + 2)

        with ExitStack() as st:
            x_tok = sb("x_tok", [128, T // 128, NB, C], stack=st)
            p_x = ps("p_x", [R, T], stack=st)
            with nc.Block() as block:
                @block.sync
                def _(sp):
                    sp.dma_start(ident[:], io["ident"]).then_inc(sig["load_const"], 16)
                    for b in range(NB):
                        sp.dma_start(x_tok[:, :, b, :], io["x"][b].rearrange("(j p) c -> p j c", p=128)).then_inc(sig["load_x"], 16)
                    sp.wait_ge(sig["load_const"], 16)

                @block.gpsimd
                def _(pool):
                    pool.memset(eps6[:], 1e-6)
                    pool.memset(eps5[:], 1e-5)
                    pool.memset(ones64[:], 1.0)

                @block.tensor
                def _(pe):
                    pe.wait_ge(sig["load_x"], 32)
                    pe.wait_ge(sig["load_const"], 16)
                    for j in range(T // 128):
                        last = pe.transpose(p_x[:, j * 128:(j + 1) * 128], x_tok[:, j].rearrange("p b c -> p (b c)"), ident[:])
                    last.then_inc(sig["x_turned"], 1)

                @block.vector
                def _(dve):
                    dve.wait_ge(sig["x_turned"], 1)
                    dve.tensor_copy(x[:], p_x[:])

        with ExitStack() as st:
            z_gate = sb("z_gate", [128, T], stack=st)
            seq = sb("seq", [128, 2, NW, L], stack=st)
            conv = sb("conv", [128, NW, POS], stack=st)
            w_out = sb("w_out", [128, R], stack=st)
            ln_w = sb("ln_w", [128, 1], stack=st)
            ln_b = sb("ln_b", [128, 1], stack=st)
            skip = sb("skip", [128, 2], stack=st)
            unperm = sb("unperm", [L, 4, L], stack=st)
            step = sb("step", [128, 2, NW * L], stack=st)
            drive = sb("drive", [128, 2, NW * L], stack=st)
            b_parts = sb("b_parts", [96, 2, NW * L], BF16, stack=st)
            c_parts = sb("c_parts", [96, 2, NW * L], BF16, stack=st)
            decay = sb("decay", [128, 2, NS], stack=st)
            pick = sb("pick", [96, NS, 128], BF16, stack=st)
            y_seq = sb("y_seq", [128, 2, NW * L], stack=st)

            with ExitStack() as s2:
                w_in = sb("w_in", [R, 2, 128], stack=s2)
                w_conv = sb("w_conv", [128, 9], stack=s2)
                b_conv = sb("b_conv", [128, 1], stack=s2)
                w_bc = sb("w_bc", [128, 2, D], stack=s2)
                xw = sb("xw", [RANK, 4, D], stack=s2)
                dtw = sb("dtw", [RANK, 4, D], stack=s2)
                b_dt = sb("b_dt", [128, 2], stack=s2)
                w_dt = sb("w_dt", [128, 2, 128], stack=s2)
                perm = sb("perm", [L, 4, L], stack=s2)
                padded = sb("padded", [128, SIDE + 2, SIDE + 2], stack=s2)
                acc = sb("acc", [128, SIDE, SIDE], stack=s2)
                pick_f = y_seq[0:96, 0].rearrange("p (n m) -> p n m", n=NS)
                tok = sb("tok", [L, NW, D], stack=s2)
                with ExitStack() as s3:
                    p_a = ps("p_a", [128, T], stack=s3)
                    p_b = ps("p_b", [R, T], stack=s3)
                    p_v = ps("p_v", [128, T], stack=s3)
                    p_z = ps("p_z", [128, T], stack=s3)
                    norm = Norm(p_a, p_b, eps6)
                    with nc.Block() as block:
                        @block.sync
                        def _(sp):
                            for t, n in ((w_in, "w_in"), (w_conv, "w_conv"), (b_conv, "b_conv"), (decay, "a_log")):
                                sp.dma_start(t[:], io[n]).then_inc(sig["load_in"], 16)
                            for t, n in ((w_bc, "w_bc"), (xw, "xw"), (dtw, "dtw"), (b_dt, "b_dt"), (perm, "perm"),
                                         (skip, "skip"), (pick_f, "pick"), (w_out, "w_out"),
                                         (ln_w, "ln_w"), (ln_b, "ln_b"), (unperm, "unperm")):
                                sp.dma_start(t[:] if t is not pick_f else t, io[n]).then_inc(sig["load_scan"], 16)
                            sp.wait_ge(sig["load_scan"], 16 * 11)

                        @block.gpsimd
                        def _(pool):
                            pool.memset(padded[:], 0.0).then_inc(sig["border_zero"], 1)
                            pool.memset(w_dt[:], 0.0)
                            pool.wait_ge(sig["load_scan"], 16 * 11)
                            pool.tensor_copy(pick[:], pick_f)

                        @block.tensor
                        def _(pe):
                            norm.pe(pe)
                            pe.wait_ge(sig["load_in"], 64)
                            for h in range(2):
                                c = slice(h * BANK, (h + 1) * BANK)
                                norm.wait_out(pe, h)
                                pe.matmul(p_v[:, c], w_in[:, 0], xn[:, c], start=True, stop=True).then_inc(sig["xv"], 1)
                                pe.matmul(p_z[:, c], w_in[:, 1], xn[:, c], start=True, stop=True).then_inc(sig["z"], 1)

                        @block.vector
                        def _(dve):
                            link = chain(dve, "dve")
                            norm.dve(dve)
                            dve.wait_ge(sig["load_in"], 64)
                            dve.wait_ge(sig["padded_in"], 2)
                            for k in range(9):
                                src = padded[:, k // 3:k // 3 + SIDE, k % 3:k % 3 + SIDE]
                                if k == 0:
                                    link(dve.tensor_scalar(acc[:], src, w_conv[:, 0:1], None, ALU.mult))
                                else:
                                    ins = dve.scalar_tensor_tensor(acc[:], src, w_conv[:, k:k + 1], acc[:], ALU.mult, ALU.add)
                                    if k < 8:
                                        link(ins)
                            ins.then_inc(sig["conv_sum"], 1)
                            unchain(link, "dve")

                        @block.scalar
                        def _(act):
                            link = chain(act, "act")
                            norm.act(act)
                            act.wait_ge(sig["border_zero"], 1)
                            for h in range(2):
                                act.wait_ge(sig["xv"], h + 1)
                                act.activation(padded[:, 1 + 16 * h:17 + 16 * h, 1:1 + SIDE],
                                               p_v[:, h * BANK:(h + 1) * BANK].rearrange("p (y x) -> p y x", y=16),
                                               ACT.Copy).then_inc(sig["padded_in"], 1)
                            act.wait_ge(sig["z"], 2)
                            act.activation(z_gate[:], p_z[:], ACT.Silu)
                            act.wait_ge(sig["conv_sum"], 1)
                            for wy in range(SIDE // WIN):
                                dst = conv[:, 4 * wy:4 * wy + 4].rearrange("p w (y x) -> p y w x", y=WIN)
                                src = acc[:, WIN * wy:WIN * wy + WIN].rearrange("p y (w x) -> p y w x", w=4)
                                act.activation(dst, src, ACT.Silu, bias=b_conv[:, 0:1])
                            act.wait_ge(sig["load_in"], 64)
                            link(act.activation(decay[:], decay[:], ACT.Exp))
                            act.activation(decay[:], decay[:], ACT.Copy, scale=-1.0)
                            unchain(link, "act")

                with ExitStack() as s3:
                    p_t = ps("p_t", [L, NW * D], stack=s3)
                    p_w = ps("p_w", [128, 128], stack=s3)
                    p_s = ps("p_s", [128, 4, BANK], stack=s3)
                    NPAIR = NW // 2
                    with nc.Block() as block:
                        @block.tensor
                        def _(pe):
                            for w in range(NW):
                                for b in range(NB):
                                    rows = slice(b * D, (b + 1) * D)
                                    last = pe.matmul(p_t[b * POS:(b + 1) * POS, w * D:(w + 1) * D], conv[rows, w], ident[rows, rows],
                                                     start=True, stop=True)
                                if w % 8 == 7:
                                    last.then_inc(sig["tok_turned"], 1)
                            for k in range(4):
                                back, kl = k // 2, k % 2
                                last = pe.matmul(p_w[back * D:(back + 1) * D, kl * D:(kl + 1) * D], xw[:, k], dtw[:, k], start=True, stop=True)
                            last.then_inc(sig["step_weight"], 1)
                            for i in range(NPAIR):
                                pe.wait_ge(sig["tok_copied"], i // 4 + 1)
                                if i >= 4:
                                    pe.wait_ge(sig["seq_copied_even" if i % 2 == 0 else "seq_copied_odd"], (i - 4) // 2 + 1)
                                for j in range(2):
                                    w = 2 * i + j
                                    for back in range(2):
                                        last = pe.matmul(p_s[back * D:(back + 1) * D, i % 4, 256 * j:256 * j + 256], tok[:, w],
                                                         perm[:, 2 * back:2 * back + 2].rearrange("p k l -> p (k l)"), start=True, stop=True)
                                last.then_inc(sig["seq_made"], 1)

                        def copy_seq(i, copy):
                            return copy(seq[:, :, 2 * i:2 * i + 2].rearrange("p k w l -> p w k l"),
                                        p_s[:, i % 4].rearrange("p (w k l) -> p w k l", w=2, k=2))

                        @block.vector
                        def _(dve):
                            for h in range(2):
                                dve.wait_ge(sig["tok_turned"], h + 1)
                                dve.tensor_copy(tok[:, 8 * h:8 * h + 8].rearrange("p w d -> p (w d)"), p_t[:, h * BANK:(h + 1) * BANK]).then_inc(sig["tok_copied"], 1)
                            dve.wait_ge(sig["step_weight"], 1)
                            for back in range(2):
                                rows = slice(back * D, (back + 1) * D)
                                dve.tensor_copy(w_dt[rows, :, back * D:(back + 1) * D],
                                                p_w[rows, :].rearrange("p (k d) -> p k d", k=2))
                            for i in range(0, NPAIR, 2):
                                dve.wait_ge(sig["seq_made"], i + 1)
                                copy_seq(i, dve.tensor_copy).then_inc(sig["seq_copied_even"], 1)

                        @block.scalar
                        def _(act):
                            for i in range(1, NPAIR, 2):
                                act.wait_ge(sig["seq_made"], i + 1)
                                copy_seq(i, act.copy).then_inc(sig["seq_copied_odd"], 1)

                with ExitStack() as s3:
                    p_bc = ps("p_bc", [R, 2, BANK], stack=s3)
                    p_d = ps("p_d", [128, 2, BANK], stack=s3)
                    part = [sb(f"part{i}", [64, 2, NW * L], BF16, stack=s3) for i in range(3)]
                    rest = sb("rest", [64, 2, NW * L], stack=s3)
                    zd = sb("zd", [128, 2, NW * L], stack=s3)
                    ex = sb("ex", [128, 2, NW * L], stack=s3)
                    ln_one = sb("ln_one", [128, 1], stack=s3)
                    NCH = 8
                    def cols(i):
                        return i // 4, slice((i % 4) * BANK, (i % 4 + 1) * BANK)
                    seqf = seq[:].rearrange("p k w l -> p k (w l)")
                    with nc.Block() as block:
                        @block.tensor
                        def _(pe):
                            for i in range(NCH):
                                k, c = cols(i)
                                if i >= 2:
                                    pe.wait_ge(sig["step_read"], i - 1)
                                pe.matmul(p_d[:, i % 2], w_dt[:, k], seqf[:, k, c], start=True, stop=True).then_inc(sig["step_made"], 1)
                                if i >= 2:
                                    pe.wait_ge(sig["bc_read"], i - 1)
                                pe.matmul(p_bc[:, i % 2], w_bc[:, k], seqf[:, k, c], start=True, stop=True).then_inc(sig["bc_made"], 1)

                        @block.scalar
                        def _(act):
                            for i in range(NCH):
                                k, c = cols(i)
                                act.wait_ge(sig["step_made"], i + 1)
                                act.activation(zd[:, k, c], p_d[:, i % 2], ACT.Identity, bias=b_dt[:, k:k + 1]).then_inc(sig["step_read"], 1)
                                act.wait_ge(sig["bc_made"], i + 1)
                                act.activation(part[0][:, k, c], p_bc[:, i % 2], ACT.Copy).then_inc(sig["part_hi"], 1)
                            for i in range(NCH):
                                k, c = cols(i)
                                act.wait_ge(sig["neg_abs"], i + 2)
                                act.activation(ex[:, k, c], ex[:, k, c], ACT.Exp).then_inc(sig["exp_neg"], 1)
                            act.wait_ge(sig["exp_neg"], NCH)
                            act.activation(ln_one[:], ln_one[:], ACT.Ln, bias=1.0).then_inc(sig["ln_one"], 1)
                            for i in range(NCH):
                                k, c = cols(i)
                                act.activation(step[:, k, c], ex[:, k, c], ACT.Ln, bias=1.0).then_inc(sig["log1"], 1)

                        @block.vector
                        def _(dve):
                            dve.memset(ln_one[:], 0.0).then_inc(sig["neg_abs"], 1)
                            for i in range(NCH):
                                k, c = cols(i)
                                dve.wait_ge(sig["part_hi"], i + 1)
                                dve.tensor_tensor(rest[:, k, c], p_bc[:, i % 2], part[0][:, k, c], ALU.subtract).then_inc(sig["bc_read"], 1)
                                dve.wait_ge(sig["step_read"], i + 1)
                                dve.scalar_tensor_tensor(ex[:, k, c], zd[:, k, c], -1.0, zd[:, k, c], ALU.mult, ALU.min).then_inc(sig["neg_abs"], 1)
                            dve.wait_ge(sig["bc_read"], NCH)
                            dve.tensor_copy(part[1][:], rest[:]).then_inc(sig["part_mid"], 1)
                            for i in range(NCH):
                                k, c = cols(i)
                                dve.wait_ge(sig["exp_neg"], i + 1)
                                dve.tensor_scalar(drive[:, k, c], ex[:, k, c], 1.0, -1.0, ALU.add, ALU.add).then_inc(sig["kept"], 1)
                            dve.wait_ge(sig["part_mid"], 1)
                            dve.tensor_tensor(part[2][:], rest[:], part[1][:], ALU.subtract).then_inc(sig["part_lo"], 1)
                            for i in range(NCH):
                                k, c = cols(i)
                                dve.wait_ge(sig["ln_one"], 1)
                                dve.wait_ge(sig["lost"], i + 1)
                                dve.wait_ge(sig["log1"], i + 1)
                                dve.scalar_tensor_tensor(step[:, k, c], step[:, k, c], ln_one[:, 0:1], drive[:, k, c],
                                                         ALU.subtract, ALU.add).then_inc(sig["log1p"], 1)
                            for i in range(NCH):
                                k, c = cols(i)
                                dve.wait_ge(sig["log1p"], i + 1)
                                dve.scalar_tensor_tensor(step[:, k, c], zd[:, k, c], 0.0, step[:, k, c], ALU.max, ALU.add).then_inc(sig["softplus"], 1)
                            for i in range(0, NCH, 2):
                                k, c = cols(i)
                                dve.wait_ge(sig["softplus"], i + 1)
                                dve.tensor_tensor(drive[:, k, c], step[:, k, c], seqf[:, k, c], ALU.mult)

                        @block.gpsimd
                        def _(pool):
                            for i in range(NCH):
                                k, c = cols(i)
                                pool.wait_ge(sig["kept"], i + 1)
                                pool.tensor_tensor(drive[:, k, c], ex[:, k, c], drive[:, k, c], ALU.subtract).then_inc(sig["lost"], 1)
                            for i in range(1, NCH, 2):
                                k, c = cols(i)
                                pool.wait_ge(sig["softplus"], i + 1)
                                pool.tensor_tensor(drive[:, k, c], step[:, k, c], seqf[:, k, c], ALU.mult)

                        @block.sync
                        def _(sp):
                            for i, s in enumerate(("part_hi", "part_mid", "part_lo")):
                                sp.wait_ge(sig[s], NCH if i == 0 else 1)
                                for dst, row in ((b_parts, 0), (c_parts, 32)):
                                    sp.dma_start(dst[32 * i:32 * i + 32], part[i][row:row + 32]).then_inc(sig["parts_stacked"], 16)
                            sp.wait_ge(sig["parts_stacked"], 96)

            with ExitStack() as s2:
                UC = NW * L // 2
                RING = 3
                p_bb = ps("p_bb", [128, 2, UC], stack=s2)
                p_cb = ps("p_cb", [128, UC], stack=s2)
                p_y = ps("p_y", [128, UC], stack=s2)
                d_a = sb("d_a", [128, 2, UC], stack=s2)
                d_bu = sb("d_bu", [128, RING, UC], stack=s2)
                hs = sb("hs", [128, RING, UC], stack=s2)
                cb = sb("cb", [128, RING, UC], stack=s2)
                hc = sb("hc", [128, RING, UC], stack=s2)
                NU = 4 * NS
                def unit(u):
                    g, n = divmod(u, NS)
                    return g // 2, (g % 2) * UC, n
                with nc.Block() as block:
                    @block.tensor
                    def _(pe):
                        for u in range(NU + RING):
                            if u < NU:
                                k, c0, n = unit(u)
                                if u >= 2:
                                    pe.wait_ge(sig["d_bu"], u - 1)
                                for h in range(2):
                                    c = slice(c0 + h * BANK, c0 + (h + 1) * BANK)
                                    last = pe.matmul(p_bb[:, u % 2, h * BANK:(h + 1) * BANK], pick[:, n], b_parts[:, k, c], start=True, stop=True)
                                last.then_inc(sig["b_spread"], 1)
                                if u >= 1:
                                    pe.wait_ge(sig["c_copied"], u)
                                for h in range(2):
                                    c = slice(c0 + h * BANK, c0 + (h + 1) * BANK)
                                    last = pe.matmul(p_cb[:, h * BANK:(h + 1) * BANK], pick[:, n], c_parts[:, k, c], start=True, stop=True)
                                last.then_inc(sig["c_spread"], 1)
                            if u >= RING:
                                v = u - RING
                                n = v % NS
                                if n == 0 and v:
                                    pe.wait_ge(sig["y_read"], v // NS)
                                pe.wait_ge(sig["hc"], v + 1)
                                for h in range(2):
                                    c = slice(h * BANK, (h + 1) * BANK)
                                    last = pe.matmul(p_y[:, c], ident[:], hc[:, v % RING, c], start=(n == 0), stop=(n == NS - 1))
                                last.then_inc(sig["y_summed"], 1)

                    @block.scalar
                    def _(act):
                        act.wait_ge(sig["first_decay_zero"], 1)
                        for u in range(NU):
                            k, c0, n = unit(u)
                            if u >= 2:
                                act.wait_ge(sig["scanned"], u - 1)
                            src = step[:, k, c0:c0 + UC].rearrange("p (w l) -> p w l", l=L)
                            dst = d_a[:, u % 2].rearrange("p (w l) -> p w l", l=L)
                            act.activation(dst[:, :, 1:L], src[:, :, 1:L], ACT.Exp, scale=decay[:, k, n:n + 1]).then_inc(sig["d_a"], 1)
                            act.wait_ge(sig["c_spread"], u + 1)
                            if u >= RING:
                                act.wait_ge(sig["hc"], u - RING + 1)
                            act.activation(cb[:, u % RING], p_cb[:], ACT.Copy).then_inc(sig["c_copied"], 1)

                    @block.vector
                    def _(dve):
                        def read_y(g):
                            k, c0, _ = unit(g * NS)
                            dve.wait_ge(sig["y_summed"], (g + 1) * NS)
                            dve.scalar_tensor_tensor(y_seq[:, k, c0:c0 + UC], seqf[:, k, c0:c0 + UC], skip[:, k:k + 1], p_y[:],
                                                     ALU.mult, ALU.add).then_inc(sig["y_read"], 1)
                        for u in range(NU + 1):
                            if u < NU:
                                k, c0, n = unit(u)
                                dve.wait_ge(sig["b_spread"], u + 1)
                                if u >= RING:
                                    dve.wait_ge(sig["scanned"], u - RING + 1)
                                dve.tensor_tensor(d_bu[:, u % RING], drive[:, k, c0:c0 + UC], p_bb[:, u % 2], ALU.mult).then_inc(sig["d_bu"], 1)
                            if u >= 1:
                                v = u - 1
                                dve.wait_ge(sig["d_bu"], v + 1)
                                dve.wait_ge(sig["d_a"], v + 1)
                                if v >= RING:
                                    dve.wait_ge(sig["hc"], v - RING + 1)
                                dve.tensor_tensor_scan(hs[:, v % RING], d_a[:, v % 2], d_bu[:, v % RING], 0.0, ALU.mult, ALU.add).then_inc(sig["scanned"], 1)
                                if v >= NS and v % NS == 1:
                                    read_y(v // NS - 1)
                        read_y(3)

                    @block.gpsimd
                    def _(pool):
                        pool.memset(d_a[:], 0.0).then_inc(sig["first_decay_zero"], 1)
                        for u in range(NU):
                            pool.wait_ge(sig["scanned"], u + 1)
                            pool.wait_ge(sig["c_copied"], u + 1)
                            if u >= RING:
                                pool.wait_ge(sig["y_summed"], u - RING + 1)
                            pool.tensor_tensor(hc[:, u % RING], hs[:, u % RING], cb[:, u % RING], ALU.mult).then_inc(sig["hc"], 1)

            with ExitStack() as s2:
                y_l = sb("y_l", [L, 4, NW, D], stack=s2)
                y_tok = sb("y_tok", [L, NW, D], stack=s2)
                y_sq = sb("y_sq", [L, NW, D], stack=s2)
                stat = sb("stat", [L, 3, NW], stack=s2)
                y_img = sb("y_img", [128, SIDE, SIDE], stack=s2)
                p_tr = ps("p_tr", [128, 4, BANK], stack=s2)
                p_tok = ps("p_tok", [L, NW * D], stack=s2)
                p_o = ps("p_o", [R, T], stack=s2)
                yv = y_seq[:].rearrange("p k (w l) -> p k w l", l=L)
                NTR = 2 * NW // 4
                p_img = p_tr[:, 0:2].rearrange("p h n -> p (h n)")
                with nc.Block() as block:
                    @block.tensor
                    def _(pe):
                        for i in range(NTR):
                            if i >= 4:
                                pe.wait_ge(sig["yl_copied_even" if i % 2 == 0 else "yl_copied_odd"], (i - 4) // 2 + 1)
                            for j in range(4):
                                k, w = divmod(4 * i + j, NW)
                                last = pe.transpose(p_tr[:, i % 4, j * 128:(j + 1) * 128], yv[:, k, w], ident[:])
                            last.then_inc(sig["yl_turned"], 1)
                        pe.wait_ge(sig["yl_copied_even"], NTR // 2)
                        pe.wait_ge(sig["yl_copied_odd"], NTR // 2)
                        for h in range(2):
                            for k in range(4):
                                last = pe.matmul(p_tok[:, h * BANK:(h + 1) * BANK], unperm[:, k],
                                                 y_l[:, k, 8 * h:8 * h + 8].rearrange("p w d -> p (w d)"), start=(k == 0), stop=(k == 3))
                            last.then_inc(sig["y_in_order"], 1)
                        pe.wait_ge(sig["y_normed"], 1)
                        for w in range(NW):
                            for b in range(NB):
                                rows = slice(b * POS, (b + 1) * POS)
                                last = pe.matmul(p_img[b * D:(b + 1) * D, w * POS:(w + 1) * POS], y_tok[rows, w], ident[rows, rows], start=True, stop=True)
                            if w % 8 == 7:
                                last.then_inc(sig["y_turned"], 1)
                        for h in range(2):
                            pe.wait_ge(sig["y_gated"], h + 1)
                            pe.matmul(p_o[:, h * BANK:(h + 1) * BANK], w_out[:], y_img[:, 16 * h:16 * h + 16].rearrange("p y x -> p (y x)"),
                                      start=True, stop=True).then_inc(sig["mixed"], 1)

                    def copy_yl(i, copy):
                        k, w = divmod(4 * i, NW)
                        return copy(y_l[:].rearrange("p (b k) w d -> p k w b d", b=2)[:, k, w:w + 4],
                                    p_tr[:, i % 4].rearrange("p (w b d) -> p w b d", w=4, b=2))

                    @block.vector
                    def _(dve):
                        link = chain(dve, "dve")
                        for i in range(0, NTR, 2):
                            dve.wait_ge(sig["yl_turned"], i + 1)
                            copy_yl(i, dve.tensor_copy).then_inc(sig["yl_copied_even"], 1)
                        dve.wait_ge(sig["y_in_order"], 2)
                        pt = p_tok[:].rearrange("p (w d) -> p w d", d=D)
                        link(dve.tensor_reduce(stat[:, 0], pt, AX_X, ALU.add))
                        link(dve.tensor_scalar(stat[:, 0], stat[:, 0], 1.0 / D, None, ALU.mult))
                        mean = stat[:, 0].rearrange("p (w a) -> p w a", a=1).broadcast_to([L, NW, D])
                        dve.tensor_tensor(y_tok[:], pt, mean, ALU.subtract).then_inc(sig["y_centred"], 1)
                        dve.wait_ge(sig["y_squared"], 1)
                        dve.tensor_reduce(stat[:, 1], y_sq[:], AX_X, ALU.add).then_inc(sig["y_sqsum"], 1)
                        dve.wait_ge(sig["y_sd"], 1)
                        link(dve.reciprocal(stat[:, 2], stat[:, 2]))
                        rsd = stat[:, 2].rearrange("p (w a) -> p w a", a=1).broadcast_to([L, NW, D])
                        dve.tensor_tensor(y_tok[:], y_tok[:], rsd, ALU.mult).then_inc(sig["y_normed"], 1)
                        for h in range(2):
                            dve.wait_ge(sig["y_scaled"], 2 * h + 2)
                            v = y_img[:, 16 * h:16 * h + 16]
                            dve.tensor_tensor(v, v, z_gate[:, h * BANK:(h + 1) * BANK].rearrange("p (y x) -> p y x", y=16), ALU.mult).then_inc(sig["y_gated"], 1)
                        for h in range(2):
                            c = slice(h * BANK, (h + 1) * BANK)
                            dve.wait_ge(sig["mixed"], h + 1)
                            dve.tensor_tensor(x[:, c], x[:, c], p_o[:, c], ALU.add)
                        unchain(link, "dve")

                    @block.scalar
                    def _(act):
                        for i in range(1, NTR, 2):
                            act.wait_ge(sig["yl_turned"], i + 1)
                            copy_yl(i, act.copy).then_inc(sig["yl_copied_odd"], 1)
                        act.wait_ge(sig["y_centred"], 1)
                        act.activation(y_sq[:], y_tok[:], ACT.Square).then_inc(sig["y_squared"], 1)
                        act.wait_ge(sig["y_sqsum"], 1)
                        act.activation(stat[:, 2], stat[:, 1], ACT.Sqrt, bias=eps5[:, 0:1], scale=1.0 / D).then_inc(sig["y_sd"], 1)
                        for wy in range(SIDE // WIN):
                            act.wait_ge(sig["y_turned"], wy // 2 + 1)
                            src = p_img[:, 4 * wy * POS:(4 * wy + 4) * POS].rearrange("p (w y x) -> p y w x", w=4, y=WIN)
                            dst = y_img[:, WIN * wy:WIN * wy + WIN].rearrange("p y (w x) -> p y w x", w=4)
                            act.activation(dst, src, ACT.Identity, bias=ln_b[:, 0:1], scale=ln_w[:, 0:1]).then_inc(sig["y_scaled"], 1)
        more(nc, io, locals())


def more(nc, io, loc):
    ctx, sig, sb, ps, chain, unchain, Norm = (loc[k] for k in ("ctx", "sig", "sb", "ps", "chain", "unchain", "Norm"))
    x, xn, ident, eps5, eps6, ones64, xn_tok = (loc[k] for k in ("x", "xn", "ident", "eps5", "eps6", "ones64", "xn_tok"))

    def halves():
        return [(h, slice(h * BANK, (h + 1) * BANK)) for h in range(2)]

    def add_half(dve, by_batch, h):
        c = slice(h * BANK, (h + 1) * BANK)
        states = slice(h * BANK + 1, (h + 1) * BANK + 1)
        dve.tensor_copy(xn[C:R, c], by_batch[0:C, states, 1]).then_inc(sig["half_added"], 1)
        dve.tensor_tensor(x[0:C, c], x[0:C, c], by_batch[0:C, states, 0], ALU.add).then_inc(sig["half_added"], 1)
        dve.wait_ge(sig["half_added"], 3 * h + 1)
        dve.tensor_tensor(x[C:R, c], x[C:R, c], xn[C:R, c], ALU.add).then_inc(sig["half_added"], 1)

    def recurrent(tag, swept, use, beside=None):
        per_use = {"load": 48, "wx": NB}
        s = lambda name: sig["rec_" + name] if name not in ("state", "preact") else sig[tag + name]
        at = lambda name, n: (s(name), use * per_use.get(name, 1) + n)
        with ExitStack() as st:
            yx = sb(tag + "yx", [2 * C, NB * (T + 17)], stack=st)
            by_batch = yx[:].rearrange("p (t b) -> p t b", b=NB)
            w = sb(tag + "w", [R, C], stack=st)
            v = sb(tag + "v", [2 * C, 128], stack=st)
            gb = sb(tag + "gb", [2 * C, 2], stack=st)
            bn = sb(tag + "bn", [2 * C, NB, 2, 6], stack=st)
            mv = sb(tag + "mv", [2 * C, 8], stack=st)
            hi = slice(C, 2 * C)
            with ExitStack() as s2:
                p_a = ps(tag + "p_a", [128, T], stack=s2)
                p_b = ps(tag + "p_b", [R, T], stack=s2)
                p_w = ps(tag + "p_w", [2 * C, NB, T], stack=s2)
                norm = Norm(p_a, p_b, eps5)
                with nc.Block() as block:
                    @block.sync
                    def _(sp):
                        for t, src in ((w, io[tag + "_W"]), (v, io[tag + "_V"]), (gb, io[tag + "_gb"])):
                            sp.dma_start(t[:], src).then_inc(s("load"), 16)
                        if swept:
                            beside.load(sp)
                        sp.wait_ge(*at("load", 48))

                    @block.tensor
                    def _(pe):
                        norm.pe(pe)
                        pe.wait_ge(*at("load", 48))
                        norm.wait_out(pe, 1)
                        for b in range(NB):
                            rows = slice(b * C, (b + 1) * C)
                            for h, c in halves():
                                last = pe.matmul(p_w[hi, b, c], w[rows], xn[rows, c], start=True, stop=True)
                            last.then_inc(s("wx"), 1)
                            if swept and b == 0:
                                beside.pe_sum(pe, p_a)
                        if swept:
                            beside.pe_square_sum(pe, p_a)

                    @block.vector
                    def _(dve):
                        link = chain(dve, "dve")
                        norm.dve(dve)
                        if swept:
                            beside.dve_spread(dve, link, p_a)
                        for b in range(NB):
                            dve.wait_ge(*at("wx", b + 1))
                            for h, c in halves():
                                link(dve.bn_stats(bn[hi, b, h], p_w[hi, b, c]))
                        dve.bn_aggr(mv[hi, 0:2], bn[hi].rearrange("p b h s -> p (b h s)")).then_inc(s("stats"), 1)
                        dve.wait_ge(*at("sd", 1))
                        dve.wait_ge(*at("load", 48))
                        link(dve.reciprocal(mv[hi, 5:6], mv[hi, 4:5]))
                        link(dve.tensor_tensor(mv[hi, 5:6], mv[hi, 5:6], gb[hi, 0:1], ALU.mult))
                        link(dve.tensor_tensor(mv[hi, 6:7], mv[hi, 5:6], mv[hi, 0:1], ALU.mult))
                        dve.tensor_tensor(mv[hi, 6:7], gb[hi, 1:2], mv[hi, 6:7], ALU.subtract).then_inc(s("shift"), 1)
                        dve.wait_ge(*at("shift", 1))
                        dve.tensor_scalar(by_batch[hi, 0:T, 1], p_w[hi, 1], mv[hi, 5:6], mv[hi, 6:7], ALU.mult, ALU.add)
                        unchain(link, "dve")

                    @block.scalar
                    def _(act):
                        norm.act(act)
                        act.wait_ge(*at("stats", 1))
                        act.activation(mv[hi, 4:5], mv[hi, 1:2], ACT.Sqrt, bias=eps5[hi, 0:1]).then_inc(s("sd"), 1)
                        if swept:
                            beside.act_root(act, p_a)
                        act.wait_ge(*at("shift", 1))
                        act.activation(by_batch[hi, 0:T, 0], p_w[hi, 0], ACT.Identity, bias=mv[hi, 6:7], scale=mv[hi, 5:6])

                    @block.gpsimd
                    def _(pool):
                        pool.memset(yx[0:C, 0:NB * T], 0.0)

            with ExitStack() as s2:
                p_z = ps(tag + "p_z", [128, 2, BANK], stack=s2)
                if not swept:
                    HALF, ROOTS = T // 2, T // 2 + 24
                    first = beside(s2)
                    with nc.Block() as block:
                        @block.tensor
                        def _(pe):
                            others = first.pe(pe)
                            for t in range(T):
                                if t:
                                    pe.wait_ge(s("state"), t)
                                pe.matmul(p_z[0:C, t % 2, 0:NB], v[:, 0:C], yx[:, NB * t:NB * (t + 1)], start=True, stop=True).then_inc(s("preact"), 1)
                                if t > HALF + 4:
                                    next(others, None)
                            for _ in others:
                                pass

                        @block.scalar
                        def _(act):
                            for t in range(T):
                                act.wait_ge(s("preact"), t + 1)
                                act.activation(yx[0:C, NB * (t + 1):NB * (t + 2)], p_z[0:C, t % 2, 0:NB], ACT.Sigmoid).then_inc(s("state"), 1)
                                if t == ROOTS:
                                    first.roots(act)

                        @block.vector
                        def _(dve):
                            dve.wait_ge(s("state"), HALF)
                            add_half(dve, by_batch, 0)
                            first.dve(dve)

                        @block.gpsimd
                        def _(pool):
                            first.pool(pool)
                    second = beside(s2)
                    with nc.Block() as block:
                        @block.tensor
                        def _(pe):
                            for _ in second.pe(pe):
                                pass

                        @block.scalar
                        def _(act):
                            second.roots(act)
                            second.act(act)

                        @block.vector
                        def _(dve):
                            add_half(dve, by_batch, 1)
                            second.dve(dve)

                        @block.gpsimd
                        def _(pool):
                            second.pool(pool)
                else:
                    p_f = ps(tag + "p_f", [C, BANK], stack=s2)
                    p_g = ps(tag + "p_g", [R, BANK], stack=s2)
                    SEG = 16
                    NSEG = T // SEG
                    SWEEPS = 3
                    UNROLL = 16
                    guess = sb(tag + "guess", [C, NSEG - 1, NB], stack=s2)
                    differ = sb(tag + "differ", [C, NSEG - 1, NB], stack=s2)
                    count = sb(tag + "count", [C, 1], stack=s2)
                    flag = sb(tag + "flag", [1, 1], I32, stack=s2)
                    ends = by_batch[0:C, SEG:T:SEG]
                    with nc.Block() as block:
                        @block.tensor
                        def _(pe):
                            for i in range(SWEEPS * SEG):
                                n = NSEG - SWEEPS + 1 + i // SEG
                                at = i % SEG
                                if i:
                                    pe.wait_ge(s("state"), i)
                                if i == 2 * SEG - 4:
                                    beside.pe_gram(pe, p_g)
                                pe.matmul(p_z[0:C, i % 2, 0:NB * n], v[:, 0:C], by_batch[:, at:at + SEG * (n - 1) + 1:SEG], start=True, stop=True).then_inc(s("preact"), 1)
                            pe.wait_ge(s("differ"), 1)
                            pe.matmul(p_f[:, 0:1], ones64[0:C, 0:C], count[:], start=True, stop=True).then_inc(s("differs"), 1)
                            pe.wait_ge(s("flag"), 1)
                            again = pe.value_load(flag[0:1, 0:1], min_val=0, max_val=1)
                            with pe.If(again != 0):
                                with pe.Fori(0, T, UNROLL) as t0:
                                    for u in range(UNROLL):
                                        pe.wait_ge(s("state_again"), t0 + u + 1)
                                        pe.matmul(p_z[:, u % 2, 0:NB], v[:], yx[:, bass.ds(NB * t0 + NB * u, NB)], start=True, stop=True).then_inc(s("preact_again"), 1)

                        @block.scalar
                        def _(act):
                            for i in range(SWEEPS * SEG):
                                n = NSEG - SWEEPS + 1 + i // SEG
                                at = i % SEG + 1
                                act.wait_ge(s("preact"), i + 1)
                                if i == SWEEPS * SEG - 1:
                                    act.wait_ge(s("guess"), 1)
                                act.activation(by_batch[0:C, at:at + SEG * (n - 1) + 1:SEG], p_z[0:C, i % 2, 0:NB * n].rearrange("p (n b) -> p n b", b=NB), ACT.Sigmoid).then_inc(s("state"), 1)
                                if 4 <= i < 4 + NLEV:
                                    beside.act_sign(act, i - 4)
                            act.wait_ge(s("flag"), 1)
                            again = act.value_load(flag[0:1, 0:1], min_val=0, max_val=1)
                            with act.If(again != 0):
                                with act.Fori(0, T, UNROLL) as t0:
                                    for u in range(UNROLL):
                                        act.wait_ge(s("preact_again"), t0 + u + 1)
                                        act.activation(yx[0:C, bass.ds(NB * t0 + NB * (u + 1), NB)], p_z[0:C, u % 2, 0:NB], ACT.Sigmoid).then_inc(s("state_again"), 1)

                        @block.vector
                        def _(dve):
                            link = chain(dve, "dve")
                            dve.memset(count[:], 0.0).then_inc(s("state_again"), 1)
                            dve.wait_ge(s("state_again"), 1)
                            beside.dve_solve(dve, link, p_g)
                            dve.wait_ge(s("state"), (SWEEPS - 1) * SEG)
                            dve.tensor_copy(guess[:], ends).then_inc(s("guess"), 1)
                            dve.wait_ge(s("guess"), 1)
                            dve.wait_ge(s("state"), SWEEPS * SEG)
                            link(dve.tensor_tensor(differ[:], guess[:], ends, ALU.not_equal))
                            dve.tensor_reduce(count[:], differ[:].rearrange("p n b -> p (n b)"), AX_X, ALU.max).then_inc(s("differ"), 1)
                            dve.wait_ge(s("differs"), 1)
                            dve.tensor_scalar(flag[:], p_f[0:1, 0:1], 1.0, None, ALU.min).then_inc(s("flag"), 1)
                            unchain(link, "dve")
            if not swept:
                return
            with nc.Block() as block:
                @block.vector
                def _(dve):
                    dve.tensor_tensor(x[0:C], x[0:C], by_batch[0:C, 1:T + 1, 0], ALU.add)
                    dve.wait_ge(*at("moved", 1))
                    dve.tensor_tensor(x[C:R], x[C:R], xn[C:R], ALU.add)

                @block.scalar
                def _(act):
                    act.activation(xn[C:R], by_batch[0:C, 1:T + 1, 1], ACT.Copy).then_inc(s("moved"), 1)

    with ExitStack() as st:
        NT, K1 = 9, 3
        NPAIRS = 2 * K1
        wf = sb("wf", [R, NT * C], stack=st)
        sc = sb("sc", [R, 3 * NACT], stack=st)
        beta = lambda n: sc[:, n:n + 1]
        shift = lambda n: sc[:, NACT + n:NACT + n + 1]
        junk = sb("junk", [R, NT * C], stack=st)
        lev = sb("lev", [R, NLEV, NT * C], stack=st)
        weff = sb("weff", [R, NT * C], stack=st)
        wc = sb("wc", [128, NPAIRS, R], stack=st)
        pad1 = sb("pad1", [128, SIDE + 2, SIDE + 2], stack=st)
        sm = sb("sm", [R, 16], stack=st)
        gram = sb("gram", [R, NLEV, NLEV + 1], stack=st)
        tmp = sb("tmp", [R, NLEV, NLEV + 1], stack=st)
        row = sb("row", [R, NLEV + 1], stack=st)
        N_ALL = float(NB * C * NT * C)

        class Filter:

            def load(self, sp):
                sp.dma_start(wf[:], io["bin_w"]).then_inc(sig["load_bin"], 16)
                sp.dma_start(sc[:], io["bin_s"]).then_inc(sig["load_bin"], 16)
                sp.wait_ge(sig["load_bin"], 32)

            def pe_sum(self, pe, p):
                pe.wait_ge(sig["w_sum"], 1)
                pe.matmul(p[0:R, BANK - 1:BANK], ones64[:], sm[:, 0:1], start=True, stop=True).then_inc(sig["w_total"], 1)

            def pe_square_sum(self, pe, p):
                pe.wait_ge(sig["w_sqsum"], 1)
                pe.matmul(p[0:R, T - 1:T], ones64[:], sm[:, 2:3], start=True, stop=True).then_inc(sig["w_sqtotal"], 1)

            def dve_spread(self, dve, link, p):
                dve.wait_ge(sig["load_bin"], 32)
                dve.tensor_reduce(sm[:, 0:1], wf[:], AX_X, ALU.add).then_inc(sig["w_sum"], 1)
                dve.wait_ge(sig["w_total"], 1)
                link(dve.tensor_scalar(sm[:, 1:2], p[0:R, BANK - 1:BANK], 1.0 / N_ALL, None, ALU.mult))
                link(dve.tensor_scalar(weff[:], wf[:], sm[:, 1:2], None, ALU.subtract))
                dve.tensor_tensor_reduce(junk[:], weff[:], weff[:], 1.0, 0.0, ALU.mult, ALU.add, sm[:, 2:3]).then_inc(sig["w_sqsum"], 1)

            def act_root(self, act, p):
                act.wait_ge(sig["w_sqtotal"], 1)
                act.activation(sm[:, 3:4], p[0:R, T - 1:T], ACT.Sqrt, scale=1.0 / N_ALL).then_inc(sig["w_sd"], 1)

            def act_sign(self, act, m):
                act.wait_ge(sig["levels"], 1)
                act.activation(lev[:, m], lev[:, m], ACT.Sign).then_inc(sig["lev_signs"], 1)

            def pe_gram(self, pe, p):
                pe.wait_ge(sig["gram_rows"], 1)
                pe.matmul(p[:, 0:30], ones64[:], gram[:].rearrange("p a b -> p (a b)"), start=True, stop=True).then_inc(sig["gram"], 1)

            def dve_solve(self, dve, link, p):
                dve.wait_ge(sig["w_sd"], 1)
                for m in range(NLEV):
                    link(dve.tensor_scalar(sm[:, 4 + m:5 + m], sm[:, 3:4], -1.0 + 2.0 * m / (NLEV - 1), None, ALU.mult))
                for m in range(NLEV):
                    ins = dve.tensor_scalar(lev[:, m], weff[:], sm[:, 4 + m:5 + m], None, ALU.add)
                ins.then_inc(sig["levels"], 1)
                dve.wait_ge(sig["lev_signs"], NLEV)
                for a in range(NLEV):
                    for b in range(a, NLEV + 1):
                        other = lev[:, b] if b < NLEV else wf[:]
                        link(dve.tensor_tensor_reduce(junk[:], lev[:, a], other, 1.0, 0.0, ALU.mult, ALU.add, gram[:, a, b:b + 1]))
                for a in range(NLEV - 1):
                    ins = dve.tensor_copy(gram[:, a + 1:NLEV, a], gram[:, a, a + 1:NLEV])
                ins.then_inc(sig["gram_rows"], 1)
                dve.wait_ge(sig["gram"], 1)
                link(dve.tensor_scalar(gram[:].rearrange("p a b -> p (a b)"), p[:, 0:30], 0.5, None, ALU.mult))
                for k in range(NLEV):
                    link(dve.reciprocal(sm[:, 10:11], gram[:, k, k:k + 1]))
                    link(dve.tensor_scalar(row[:], gram[:, k], sm[:, 10:11], None, ALU.mult))
                    col = gram[:, :, k:k + 1].broadcast_to([R, NLEV, NLEV + 1])
                    rows = row[:].rearrange("p (a b) -> p a b", a=1).broadcast_to([R, NLEV, NLEV + 1])
                    link(dve.tensor_tensor(tmp[:], col, rows, ALU.mult))
                    link(dve.tensor_tensor(gram[:], gram[:], tmp[:], ALU.subtract))
                    link(dve.tensor_copy(gram[:, k], row[:]))
                for m in range(NLEV):
                    if m == 0:
                        link(dve.tensor_scalar(weff[:], lev[:, 0], gram[:, 0, NLEV:NLEV + 1], None, ALU.mult))
                    else:
                        link(dve.scalar_tensor_tensor(weff[:], lev[:, m], gram[:, m, NLEV:NLEV + 1], weff[:], ALU.mult, ALU.add))
                link(dve.memset(wc[:], 0.0))
                taps = weff[:].rearrange("p (y x c) -> p y x c", y=K1, x=K1)
                for b in range(NB):
                    rr = slice(b * C, (b + 1) * C)
                    dve.tensor_copy(wc[rr, 0:K1, rr], taps[rr, :, 0])
                    dve.tensor_copy(wc[rr, K1:NPAIRS, rr], taps[rr, :, 2])
                    dve.tensor_copy(wc[R + b * C:R + (b + 1) * C, 0:K1, rr], taps[rr, :, 1])
                link(dve.tensor_reduce(sm[:, 11:12], gram[:, :, NLEV], AX_X, ALU.add))
                link(dve.tensor_tensor_reduce(junk[:, 0:NACT], sc[:, 0:NACT], sc[:, 2 * NACT:3 * NACT], 1.0, 0.0, ALU.mult, ALU.add, sm[:, 12:13]))
                link(dve.tensor_tensor(sm[:, 13:14], sm[:, 11:12], sm[:, 12:13], ALU.mult))

        recurrent("L0", True, 0, Filter())

        sg = sb("sg", [R, NACT, T], stack=st)
        p_a = ps("b1p_a", [128, T], stack=st)
        p_b = ps("b1p_b", [R, T], stack=st)
        p_c = ps("b1p_c", [R, T], stack=st)
        norm = Norm(p_a, p_b, eps6)
        inner = pad1[0:R, 1:1 + SIDE, 1:1 + SIDE]
        further = pad1[R:2 * R, 1:1 + SIDE, 0:SIDE]
        img = lambda t: t.rearrange("p (y x) -> p y x", x=SIDE)
        with nc.Block() as block:
            @block.gpsimd
            def _(pool):
                pool.memset(pad1[:], 0.0).then_inc(sig["bin_zero"], 1)

            @block.tensor
            def _(pe):
                norm.pe(pe)
                pe.wait_ge(sig["acts"], 1)
                pe.wait_ge(sig["acts_further"], 1)
                for h, c in halves():
                    for k in range(NPAIRS):
                        y0 = 16 * h + k % K1
                        x0 = 0 if k < K1 else 2
                        last = pe.matmul(p_c[:, c], wc[:, k], pad1[:, y0:y0 + 16, x0:x0 + SIDE], start=(k == 0), stop=(k == NPAIRS - 1))
                    last.then_inc(sig["bin_conv"], 1)

            @block.scalar
            def _(act):
                norm.act(act)
                for n in range(NACT):
                    act.wait_ge(sig["act_in"], n + 1)
                    act.activation(sg[:, n], sg[:, n], ACT.Sign).then_inc(sig["act_sign"], 1)
                act.wait_ge(sig["acts"], 1)
                act.copy(further, inner).then_inc(sig["acts_further"], 1)

            @block.vector
            def _(dve):
                link = chain(dve, "dve")
                norm.dve(dve)
                norm.wait_out(dve)
                for n in range(NACT):
                    dve.tensor_scalar(sg[:, n], xn[:], shift(n), -0.5, ALU.add, ALU.add).then_inc(sig["act_in"], 1)
                dve.wait_ge(sig["bin_zero"], 1)
                for n in range(NACT):
                    dve.wait_ge(sig["act_sign"], n + 1)
                    if n == 0:
                        link(dve.tensor_scalar(inner, img(sg[:, 0]), beta(0), None, ALU.mult))
                    else:
                        ins = dve.scalar_tensor_tensor(inner, img(sg[:, n]), beta(n), inner, ALU.mult, ALU.add)
                        if n < NACT - 1:
                            link(ins)
                ins.then_inc(sig["acts"], 1)
                for h, c in halves():
                    dve.wait_ge(sig["bin_conv"], h + 1)
                    dve.scalar_tensor_tensor(x[:, c], p_c[:, c], sm[:, 13:14], x[:, c], ALU.add, ALU.add)
                unchain(link, "dve")

    def experts(tag, use):
        per_use = {"load": 96, "logits": 2, "biased_logits": 2, "spread": 2}
        s = lambda name: sig["moe_" + name]
        at = lambda name, n: (s(name), use * per_use.get(name, 1) + n)
        G = NB * E
        NTG = T // 128
        with ExitStack() as st:
            gate = sb(tag + "gate", [R, G], stack=st)
            gate_b = sb(tag + "gate_b", [G, 1], stack=st)
            w1 = sb(tag + "w1", [C + 1, E, HID], stack=st)
            w2 = sb(tag + "w2", [HID, E, C], stack=st)
            b2 = sb(tag + "b2", [C, E], stack=st)
            own = sb(tag + "own", [G, NB], stack=st)
            lg = sb(tag + "lg", [G, T], stack=st)
            pr = sb(tag + "pr", [G, T], stack=st)
            left = sb(tag + "left", [G, T], stack=st)
            wt = sb(tag + "wt", [G, T], stack=st)
            top = sb(tag + "top", [G, 8], stack=st)
            small = sb(tag + "small", [G, 4], stack=st)
            wt_tok = sb(tag + "wt_tok", [128, NTG, G], stack=st)
            pooled = sb(tag + "pooled", [C + 1, E, NB], stack=st)
            hid = sb(tag + "hid", [HID, G], stack=st)
            outs = sb(tag + "outs", [C, NB, E], stack=st)
            outb = sb(tag + "outb", [G, NB, C], stack=st)
            p_a = ps(tag + "p_a", [128, T], stack=st)
            p_b = ps(tag + "p_b", [R, T], stack=st)
            p_l2 = ps(tag + "p_l", [R, T], stack=st)
            p_l = p_l2[0:G]
            p_t = ps(tag + "p_t", [128, 2, BANK], stack=st)
            norm = Norm(p_a, p_b, eps5)
            p_pool, p_e, p_r = p_a[0:R, 0:G], p_b[0:C, BANK:BANK + G], p_a[0:G, BANK:BANK + C]
            p_x = p_l2
            with nc.Block() as block:
                @block.sync
                def _(sp):
                    for t, n in ((gate, tag + "_gate"), (gate_b, tag + "_gate_b"), (w1, tag + "_w1"), (w2, tag + "_w2"), (b2, tag + "_b2"), (own, "own")):
                        sp.dma_start(t[:], io[n]).then_inc(s("load"), 16)
                    sp.wait_ge(*at("load", 96))

                @block.gpsimd
                def _(pool):
                    pool.memset(pooled[:], 1.0).then_inc(s("ones"), 1)

                @block.tensor
                def _(pe):
                    norm.pe(pe)
                    pe.wait_ge(*at("load", 96))
                    for h, c in halves():
                        norm.wait_out(pe, h)
                        pe.matmul(p_l[:, c], gate[:], xn[:, c], start=True, stop=True).then_inc(s("logits"), 1)
                    pe.wait_ge(*at("weights", 1))
                    for j in range(NTG):
                        last = pe.transpose(p_t[:, 1, j * G:(j + 1) * G], wt[:, j * 128:(j + 1) * 128], ident[0:G, 0:G])
                    last.then_inc(s("w_turned"), 1)
                    pe.wait_ge(*at("w_tok", 1))
                    for j in range(NTG):
                        last = pe.matmul(p_pool, xn_tok[:, j], wt_tok[:, j], start=(j == 0), stop=(j == NTG - 1))
                    last.then_inc(s("pooled"), 1)
                    pe.wait_ge(*at("pool_read", 1))
                    for e in range(E):
                        last = pe.matmul(p_t[:, 0, 2 * e:2 * e + 2], w1[:, e], pooled[:, e], start=True, stop=True)
                    last.then_inc(s("hidden"), 1)
                    pe.wait_ge(*at("gelu", 1))
                    for e in range(E):
                        last = pe.matmul(p_e[:, 2 * e:2 * e + 2], w2[:, e], hid[:, 2 * e:2 * e + 2], start=True, stop=True)
                    last.then_inc(s("expert_out"), 1)
                    pe.wait_ge(*at("biased", 1))
                    pe.transpose(p_r, outs[:].rearrange("p b e -> p (b e)"), ident[0:C, 0:C]).then_inc(s("out_turned"), 1)
                    pe.wait_ge(*at("outb", 1))
                    for h, c in halves():
                        pe.matmul(p_x[:, c], outb[:].rearrange("p b c -> p (b c)"), wt[:, c], start=True, stop=True).then_inc(s("spread"), 1)

                @block.scalar
                def _(act):
                    norm.act(act)
                    act.wait_ge(*at("load", 96))
                    for h, c in halves():
                        act.wait_ge(*at("logits", h + 1))
                        act.activation(lg[:, c], p_l[:, c], ACT.Identity, bias=gate_b[:, 0:1]).then_inc(s("biased_logits"), 1)
                    act.wait_ge(*at("neg_max", 1))
                    act.activation(pr[:], lg[:], ACT.Exp, bias=small[:, 0:1], accum_out=small[:, 1:2]).then_inc(s("exp"), 1)
                    act.wait_ge(*at("hidden", 1))
                    act.activation(hid[:], p_t[:, 0, 0:G], ACT.Gelu).then_inc(s("gelu"), 1)

                @block.vector
                def _(dve):
                    link = chain(dve, "dve")
                    norm.dve(dve)
                    dve.wait_ge(*at("biased_logits", 2))
                    link(dve.max(top[:], lg[:]))
                    dve.tensor_scalar(small[:, 0:1], top[:, 0:1], -1.0, None, ALU.mult).then_inc(s("neg_max"), 1)
                    dve.wait_ge(*at("exp", 1))
                    link(dve.reciprocal(small[:, 2:3], small[:, 1:2]))
                    link(dve.tensor_scalar(pr[:], pr[:], small[:, 2:3], None, ALU.mult))
                    link(dve.max(top[:], pr[:]))
                    link(dve.match_replace(left[:], top[:], pr[:], 0.0))
                    dve.tensor_tensor(wt[:], pr[:], left[:], ALU.subtract).then_inc(s("weights"), 1)
                    dve.wait_ge(*at("w_turned", 1))
                    dve.tensor_copy(wt_tok[:].rearrange("p j r -> p (j r)"), p_t[:, 1, 0:NTG * G]).then_inc(s("w_tok"), 1)
                    dve.wait_ge(*at("pooled", 1))
                    dve.wait_ge(*at("ones", 1))
                    for b in range(NB):
                        ins = dve.tensor_copy(pooled[0:C, :, b], p_pool[b * C:(b + 1) * C, b * E:(b + 1) * E])
                    ins.then_inc(s("pool_read"), 1)
                    dve.wait_ge(*at("expert_out", 1))
                    dve.wait_ge(*at("load", 96))
                    dve.tensor_tensor(outs[:], p_e.rearrange("p (e b) -> p b e", b=NB),
                                      b2[:].rearrange("p (a e) -> p a e", a=1).broadcast_to([C, NB, E]), ALU.add).then_inc(s("biased"), 1)
                    dve.wait_ge(*at("out_turned", 1))
                    for b in range(NB):
                        ins = dve.tensor_scalar(outb[:, b], p_r, own[:, b:b + 1], None, ALU.mult)
                    ins.then_inc(s("outb"), 1)
                    for h, c in halves():
                        dve.wait_ge(*at("spread", h + 1))
                        dve.tensor_tensor(x[:, c], x[:, c], p_x[:, c], ALU.add)
                    unchain(link, "dve")

    experts("L1", 0)

    with ExitStack() as st:
        ew = sb("ew", [R, NBASIS, R], stack=st)
        eb = sb("eb", [R, 2], stack=st)
        sr = sb("sr", [R, SIDE], stack=st)
        scl = sb("scl", [R, SIDE], stack=st)
        dg = sb("dg", [R, SIDE], stack=st)
        tot = sb("tot", [R, 2], stack=st)
        rc = sb("rc", [R, 3, SIDE], stack=st)
        acc = sb("eacc", [R, SIDE, SIDE], stack=st)
        low = sb("elow", [R, SIDE, SIDE], stack=st)
        p_a = ps("e2p_a", [128, T], stack=st)
        p_b = ps("e2p_b", [R, T], stack=st)
        p_c = ps("e2p_c", [R, T], stack=st)
        p_r = ps("e2p_r", [R, 2, BANK], stack=st)
        norm = Norm(p_a, p_b, eps6)
        xi = xn[:].rearrange("p (i j) -> p i j", j=SIDE)
        with nc.Block() as block:
            @block.sync
            def _(sp):
                sp.dma_start(ew[:], io["eq_w"]).then_inc(sig["load_eq"], 16)
                sp.dma_start(eb[:], io["eq_b"]).then_inc(sig["load_eq"], 16)
                sp.wait_ge(sig["load_eq"], 32)

            @block.tensor
            def _(pe):
                norm.pe(pe)
                pe.wait_ge(sig["load_eq"], 32)
                norm.wait_out(pe)
                turned = xn[:].rearrange("p (i j) -> p j i", j=SIDE)
                for h, c in halves():
                    pe.matmul(p_c[:, c], ew[:, 9], xn[:, c], start=True, stop=False)
                    pe.matmul(p_c[:, c], ew[:, 10], turned[:, 16 * h:16 * h + 16], start=False, stop=True).then_inc(sig["eq_full"], 1)
                pe.wait_ge(sig["eq_sums"], 1)
                sd = tot[:, 0:1].broadcast_to([R, SIDE])
                sa = tot[:, 1:2].broadcast_to([R, SIDE])
                groups = [[(8, sr[:]), (7, scl[:]), (11, dg[:]), (13, sd), (14, sa)],
                          [(5, scl[:]), (6, sr[:]), (12, dg[:])],
                          [(0, dg[:]), (1, sd), (2, sr[:]), (3, scl[:]), (4, sa)]]
                for g, terms in enumerate(groups):
                    for n, (k, src) in enumerate(terms):
                        last = pe.matmul(p_r[:, g % 2, (g // 2) * SIDE:(g // 2) * SIDE + SIDE], ew[:, k], src, start=(n == 0), stop=(n == len(terms) - 1))
                    last.then_inc(sig["eq_lines"], 1)

            @block.scalar
            def _(act):
                norm.act(act)

            @block.vector
            def _(dve):
                link = chain(dve, "dve")
                norm.dve(dve)
                norm.wait_out(dve)
                dve.tensor_reduce(scl[:], xn[:].rearrange("p (i j) -> p j i", j=SIDE), AX_X, ALU.add)
                link(dve.tensor_reduce(sr[:], xi, AX_X, ALU.add))
                link(dve.tensor_copy(dg[:], xn[:, 0:T:SIDE + 1]))
                link(dve.tensor_reduce(tot[:, 0:1], dg[:], AX_X, ALU.add))
                dve.tensor_reduce(tot[:, 1:2], sr[:], AX_X, ALU.add).then_inc(sig["eq_sums"], 1)
                dve.wait_ge(sig["eq_lines"], 3)
                dve.wait_ge(sig["load_eq"], 32)
                link(dve.tensor_scalar(rc[:, 0], p_r[:, 0, 0:SIDE], eb[:, 0:1], None, ALU.add))
                link(dve.tensor_copy(rc[:, 1], p_r[:, 1, 0:SIDE]))
                link(dve.tensor_scalar(rc[:, 2], p_r[:, 0, SIDE:2 * SIDE], eb[:, 1:2], None, ALU.add))
                dve.wait_ge(sig["eq_full"], 2)
                along = rc[:, 0].rearrange("p (i a) -> p i a", a=1).broadcast_to([R, SIDE, SIDE])
                down = rc[:, 1].rearrange("p (a j) -> p a j", a=1).broadcast_to([R, SIDE, SIDE])
                link(dve.tensor_tensor(acc[:], p_c[:].rearrange("p (i j) -> p i j", j=SIDE), along, ALU.add))
                link(dve.tensor_tensor(acc[:], acc[:], down, ALU.add))
                diag = acc[:].rearrange("p i j -> p (i j)")[:, 0:T:SIDE + 1]
                link(dve.tensor_tensor(diag, diag, rc[:, 2], ALU.add))
                link(dve.scalar_tensor_tensor(low[:], acc[:], 0.01, acc[:], ALU.mult, ALU.max))
                dve.tensor_tensor(x[:], x[:], low[:].rearrange("p i j -> p (i j)"), ALU.add)
                unchain(link, "dve")

    with ExitStack() as st:
        NTG = T // 128
        HEADS = 2
        HC = C // 4 // HEADS
        JC = NB * HEADS * HC
        W1, W3 = (SIDE // 8) ** 2, (SIDE // 16) ** 2
        WITHIN = {2: 0, 0: 1}
        aq = sb("aq", [R, 2, 128], stack=st)
        ak = sb("ak", [R, 2, 128], stack=st)
        av = sb("av", [R, 2, JC], stack=st)
        ae1 = sb("ae1", [R, NB, 3 * HEADS * HC], stack=st)
        ae3 = sb("ae3", [R, NB * 3 * HEADS * HC], stack=st)
        ao = sb("ao", [128, 4, BANK], stack=st)
        abo = sb("abo", [1, R], stack=st)
        one_row = sb("one_row", [1, BANK], stack=st)
        pos1 = sb("pos1", [128, 2, 128], stack=st)
        pos3 = sb("pos3", [128, 2, 2, 256], stack=st)
        pos2 = sb("pos2", [128, HEADS * W1 * W1], stack=st)
        pos4 = sb("pos4", [128, HEADS * W3 * W3], stack=st)
        EC = 3 * BANK // 4
        xo = sb("xo", [R, 4, T], stack=st)
        q = sb("q", [128, 2, T], stack=st)
        kk = sb("kk", [128, 2, T], stack=st)
        vv = sb("vv", [128, 2, NTG, JC], stack=st)
        units = [(g, j, range(t, t + n)) for h, quarters in ((0, (2, 0)), (1, (0, 2))) for g in quarters for n in (2 if g == 2 else 4,)
                 for t in range(4 * h, 4 * h + 4, n) for j in range(4)]
        NU, EARLY = len(units), len(units) // 2
        scored = sb("scored", [128, EARLY, BANK], stack=st)
        mx = sb("amx", [128, NU, 4], stack=st)
        nmx = sb("anmx", [128, NU, 4], stack=st)
        den = sb("aden", [128, 2, NTG, 4], stack=st)
        e1 = sb("e1", [128, W1, 3, HEADS, HC], stack=st)
        e3 = sb("e3", [128, 2, W3, NB, 3, HEADS, HC], stack=st)

        def arranged(g, whole, image, half):
            side = 8 if g < 2 else 16
            n = SIDE // side
            src = image.rearrange("p (u y v x) -> p u y v x", u=n, y=side, v=n)
            for u in range(half * n // 2, (half + 1) * n // 2):
                if g % 2 == 0:
                    dst = whole.rearrange("p (u v y x) -> p u v y x", u=n, v=n, y=side)[:, u]
                    yield dst, src[:, u].rearrange("p y v x -> p v y x")
                else:
                    dst = whole.rearrange("p (y x u v) -> p u y x v", u=n, v=n, y=side)[:, u]
                    yield dst, src[:, u].rearrange("p y v x -> p y x v")

        def entries(u):
            g, j, ts = units[u]
            nk = BANK // len(ts)
            for e, t in enumerate(ts):
                yield e, t, nk, slice(e * nk, (e + 1) * nk)

        def score(pe, dst, u, e, t, part, width):
            g, j, _ = units[u]
            nk = BANK // len(units[u][2])
            k0 = (t * 128 if nk == 128 else (t // 2) * 256) + part * width
            rr = slice(32 * j, 32 * j + 4)
            c = e * nk + part * width
            return pe.matmul(dst[:, c:c + width], q[rr, WITHIN[g], t * 128:(t + 1) * 128], kk[rr, WITHIN[g], k0:k0 + width],
                             start=True, stop=True, tile_position=(32 * j, 0))

        def biased(dve, src, i):
            g, j, ts = units[i]
            h = j % 2
            dve.wait_ge(sig["at_scores"], i + 1)
            if i >= EARLY:
                dve.wait_ge(sig["at_turned"], i - EARLY + 1)
            for e, t, nk, c in entries(i):
                bias = pos3[:, t % 2, h] if g == 2 else pos1[:, h]
                last = dve.tensor_tensor_reduce(scored[:, i % EARLY, c], src[:, c], bias, 1.0, -3e38, ALU.add, ALU.max, mx[:, i, e:e + 1])
            last.then_inc(sig["at_max"], 1)
            dve.wait_ge(sig["at_max"], i + 1)
            n = len(ts)
            dve.tensor_scalar(nmx[:, i, 0:n], mx[:, i, 0:n], -1.0, None, ALU.mult).then_inc(sig["at_nmax"], 1)

        def exponentials(act, i):
            g, j, _ = units[i]
            act.wait_ge(sig["at_nmax"], i + 1)
            for e, t, nk, c in entries(i):
                row = scored[:, i % EARLY, c]
                last = act.activation(row, row, ACT.Exp, bias=nmx[:, i, e:e + 1], accum_out=den[:, WITHIN[g], t, j:j + 1])
            last.then_inc(sig["at_exp"], 1)

        class Front:
            made = 0

            def __init__(self, stack):
                self.half = h = Front.made
                Front.made += 1
                if h == 0:
                    Front.banks = [ps("atp_tok", [128, BANK], stack=stack), ps("atp_back", [R, BANK], stack=stack),
                                   ps("atp_q", [128, 2, BANK], stack=stack), ps("atp_e", [128, 2, BANK], stack=stack)]
                p_tok, p_back, self.p_q, self.p_e = Front.banks
                self.norm = Norm(p_tok, p_back, eps6, apart=True, k=None if h == 0 else Front.k)
                Front.k = self.norm.k

            def pe(self, pe):
                half, norm, p_q, p_e = self.half, self.norm, self.p_q, self.p_e
                width = BANK if half else 32
                pe.wait_ge(sig["half_added"], 3 * half + 3)
                for j in range(4):
                    norm.turn(pe, half, j)
                    yield
                for _ in range(28):
                    yield
                for j in range(4):
                    norm.turn_back(pe, half, j)
                    yield
                for _ in range(20):
                    yield
                pe.wait_ge(sig["load_at"], 16 * 11)
                made = 4 * half
                for g in (2, 0):
                    pe.wait_ge(sig[f"arranged{g}"], half + 1)
                    for m, wgt in enumerate((aq, ak)):
                        if made >= 2:
                            pe.wait_ge(sig["qk_read"], made - 1)
                        if half and g == 2:
                            pe.wait_ge(sig["at_max"], EARLY)
                        for c in range(0, BANK, width):
                            ins = pe.matmul(p_q[:, m, c:c + width], wgt[:, WITHIN[g]], xo[:, g, half * BANK + c:half * BANK + c + width],
                                            start=True, stop=True)
                            if c + width == BANK:
                                ins.then_inc(sig["qk_made"], 1)
                            yield
                        made += 1
                        for _ in range(8):
                            yield
                for slot, g in enumerate((2, 0)):
                    for t in range(4 * half, 4 * half + 4):
                        pe.matmul(p_e[:, slot, EC + t * JC:EC + (t + 1) * JC], xo[:, g, t * 128:(t + 1) * 128], av[:, slot], start=True, stop=True)
                        yield
                pe.wait_ge(sig["arranged3"], half + 1)
                cols = NB * 3 * HEADS * HC
                for f in range(2):
                    for w in range(2 * half, 2 * half + 2):
                        n = f * W3 + w
                        start = f * 128 * W3 + w
                        last = pe.matmul(p_e[:, 0, n * cols:(n + 1) * cols], xo[:, 3, start:start + 127 * W3 + 1:W3], ae3[:], start=True, stop=True)
                        if (f, w) == (1, 2 * half + 1):
                            last.then_inc(sig["e_made"], 1)
                        yield
                pe.wait_ge(sig["arranged1"], half + 1)
                cols = 3 * HEADS * HC
                for w in range(8 * half, 8 * half + 8):
                    for b in range(NB):
                        last = pe.matmul(p_e[b * 64:(b + 1) * 64, 1, w * cols:(w + 1) * cols], xo[:, 1, w:w + 63 * W1 + 1:W1], ae1[:, b], start=True, stop=True)
                        if (w, b) == (8 * half + 7, 1):
                            last.then_inc(sig["e_made"], 1)
                        yield
                if half == 0:
                    pe.wait_ge(sig["qk_read"], 4)
                    for u in range(EARLY):
                        if u >= 2:
                            pe.wait_ge(sig["at_max"], u - 1)
                        for n in range(BANK // width):
                            e, part = divmod(n, BANK // width // len(units[u][2]))
                            ins = score(pe, p_q[:, u % 2], u, e, units[u][2][e], part, width)
                            if n == BANK // width - 1:
                                ins.then_inc(sig["at_scores"], 1)
                            yield

            def roots(self, act):
                self.norm.act_roots(act, self.half)

            def act(self, act):
                for i in range(EARLY):
                    exponentials(act, i)

            def pool(self, pool):
                if self.half == 0:
                    pool.memset(one_row[:], 1.0)
                self.norm.wait_out(pool, self.half)
                for g in (0, 3):
                    for dst, src in arranged(g, xo[:, g], xn[:], self.half):
                        last = pool.tensor_copy(dst, src)
                    last.then_inc(sig[f"arranged{g}"], 1)

            def dve(self, dve):
                half, p_q, p_e = self.half, self.p_q, self.p_e
                self.norm.dve(dve, (half,))
                self.norm.wait_out(dve, half)
                for g in (2, 1):
                    for dst, src in arranged(g, xo[:, g], xn[:], half):
                        last = dve.tensor_copy(dst, src)
                    last.then_inc(sig[f"arranged{g}"], 1)
                c = slice(half * BANK, (half + 1) * BANK)
                n = 4 * half
                for g in (2, 0):
                    dve.wait_ge(sig["qk_made"], n + 1)
                    dve.tensor_scalar(q[:, WITHIN[g], c], p_q[:, 0], HC_SCALE, None, ALU.mult).then_inc(sig["qk_read"], 1)
                    dve.wait_ge(sig["qk_made"], n + 2)
                    dve.tensor_copy(kk[:, WITHIN[g], c], p_q[:, 1]).then_inc(sig["qk_read"], 1)
                    n += 2
                groups, own = slice(4 * half, 4 * half + 4), slice(EC + 4 * half * JC, EC + (4 * half + 4) * JC)
                dve.wait_ge(sig["e_made"], 2 * half + 1)
                dve.tensor_copy(vv[:, 0, groups].rearrange("p t n -> p (t n)"), p_e[:, 0, own])
                w = slice(2 * half, 2 * half + 2)
                dve.tensor_copy(e3[:, :, w].rearrange("p f w b n h c -> p f (w b n h c)"),
                                p_e[:, 0, 0:EC].rearrange("p (f w n) -> p f w n", f=2, w=W3)[:, :, w].rearrange("p f w n -> p f (w n)"))
                dve.wait_ge(sig["e_made"], 2 * half + 2)
                dve.tensor_copy(vv[:, 1, groups].rearrange("p t n -> p (t n)"), p_e[:, 1, own])
                w = slice(8 * half, 8 * half + 8)
                dve.tensor_copy(e1[:, w].rearrange("p w n h c -> p (w n h c)"),
                                p_e[:, 1, 0:EC].rearrange("p (w n) -> p w n", w=W1)[:, w].rearrange("p w n -> p (w n)"))
                if half == 0:
                    for u in range(EARLY):
                        biased(dve, p_q[:, u % 2], u)

        with nc.Block() as block:
            @block.sync
            def _(sp):
                loads = [(aq, "at_q"), (ak, "at_k"), (av, "at_v"), (ae1, "at_e1"), (ae3, "at_e3"), (pos1, "pos1"), (pos2, "pos2"),
                         (pos3, "pos3"), (pos4, "pos4"), (abo, "at_bo"), (ao, "at_o")]
                for t, n in loads:
                    sp.dma_start(t[:], io[n]).then_inc(sig["load_at"], 16)

        recurrent("L2", False, 1, Front)

        with ExitStack() as s2:
            END0 = NU - 8
            p_s = ps("atp_s", [128, 2, BANK], stack=s2)
            p_t = ps("atp_t", [128, 2, BANK], stack=s2)
            p_bank = ps("atp_bank", [128, 2, BANK], stack=s2)
            p_o = p_bank[:, :, 0:128].rearrange("p s (t n) -> p s t n", t=NTG)
            p_x = ps("atp_x", [R, T], stack=s2)
            pt = sb("apt", [128, 2, BANK], stack=s2)
            rden = sb("arden", [128, 2, NTG, 4], stack=s2)
            o_tok = sb("ato_tok", [128, 4, 128], stack=s2)
            o_chan = sb("ato_chan", [128, 4, 128], stack=s2)
            prod1 = sb("prod1", [128, HEADS, W1 * W1 * HC], stack=s2)
            pv1 = sb("pv1", [128, HEADS, W1 * W1 * HC], stack=s2)
            sc1 = sb("sc1", [128, HEADS * W1, W1], stack=s2)
            st1 = sb("st1", [128, 3, HEADS * W1], stack=s2)
            NC3 = 2 * NB * HEADS
            prod3 = sb("prod3", [128, NC3, W3 * W3 * HC], stack=s2)
            pv3 = sb("pv3", [128, NC3, W3 * W3 * HC], stack=s2)
            sc3 = sb("sc3", [128, NC3 * W3, W3], stack=s2)
            st3 = sb("st3", [128, 3, NC3 * W3], stack=s2)
            MIX = (3, 1, 0, 2)

            def turned(g):
                k = 1 if g == MIX[-1] else 1 + MIX.index(g)
                return p_bank[:, WITHIN[MIX[-1] if g == MIX[-1] else MIX[-2]], k * 128:(k + 1) * 128]

            with nc.Block() as block:
                @block.tensor
                def _(pe):
                    def turn_out(nth, quarters):
                        pe.wait_ge(sig["at_norm"], nth)
                        for g in quarters:
                            last = pe.transpose(turned(g), o_tok[:, g], ident[:])
                        last.then_inc(sig["at_turned_out"], 1)

                    def mix(g):
                        pe.wait_ge(sig["at_chan"], 2 if g == MIX[-1] else 1)
                        image = p_x[:].rearrange("p (u y v x) -> p u v y x", y=8 if g < 2 else 16, x=8 if g < 2 else 16, v=4 if g < 2 else 2)
                        if g == 1:
                            for w in range(W1):
                                for b in range(NB):
                                    last = pe.matmul(image[b * C:(b + 1) * C, w // 4, w % 4], ao[:, g, w * C:(w + 1) * C], o_chan[:, g, b * 64:(b + 1) * 64],
                                                     start=False, stop=False)
                        else:
                            for t in range(NTG):
                                if g == 0:
                                    dst = image[:, t // 2, 2 * (t % 2):2 * (t % 2) + 2]
                                elif g == 2:
                                    dst = image[:, t // 4, t // 2 % 2, 8 * (t % 2):8 * (t % 2) + 8]
                                else:
                                    dst = image[:, t % 4 // 2, t % 2, 8 * (t // 4):8 * (t // 4) + 8]
                                last = pe.matmul(dst, ao[:, g, t * R:(t + 1) * R], o_chan[:, g], start=False, stop=(g == MIX[-1] and t % 4 == 3))
                        last.then_inc(sig["at_mixed"], 1)

                    for h, c in halves():
                        pe.matmul(p_x[:, c], abo[:], one_row[:], start=True, stop=False)
                    for i in range(2, NU + 3):
                        if EARLY <= i < NU:
                            if i >= EARLY + 2:
                                pe.wait_ge(sig["at_max"], i - 1)
                            for e, t, nk, c in entries(i):
                                last = score(pe, p_s[:, i % 2], i, e, t, 0, nk)
                            last.then_inc(sig["at_scores"], 1)
                        if i < NU + 2:
                            u = i - 2
                            pe.wait_ge(sig["at_exp"], u + 1)
                            if u >= 2:
                                pe.wait_ge(sig["at_pt"], u - 1)
                            for n in range(4):
                                last = pe.transpose(p_t[:, u % 2, n * 128:(n + 1) * 128], scored[:, u % EARLY, n * 128:(n + 1) * 128], ident[:])
                            last.then_inc(sig["at_turned"], 1)
                        if i >= 3:
                            u = i - 3
                            g, j, _ = units[u]
                            pe.wait_ge(sig["at_pt"], u + 1)
                            for e, t, nk, c in entries(u):
                                nkb = nk // 128
                                for kb in range(nkb):
                                    kt = t if nkb == 1 else (t // 2) * 2 + kb
                                    last = pe.matmul(p_o[:, WITHIN[g], t, j * HC:(j + 1) * HC], pt[:, u % 2, c.start + kb * 128:c.start + (kb + 1) * 128],
                                                     vv[:, WITHIN[g], kt, j * HC:(j + 1) * HC], start=(kb == 0), stop=(kb == nkb - 1))
                            last.then_inc(sig["at_out"], 1)
                        if i == END0 + 4:
                            turn_out(3, MIX[:3])
                        if END0 + 6 <= i < END0 + 9:
                            mix(MIX[i - END0 - 6])
                    turn_out(4, MIX[3:])
                    mix(MIX[3])

                @block.vector
                def _(dve):
                    link = chain(dve, "dve")

                    def scores(dst, stat, prod, pos_, scale, nth, lead):
                        rows, keys = dst.shape[1], dst.shape[2]
                        flat = dst[:].rearrange("p r k -> p (r k)")
                        dve.wait_ge(sig["at_prod"], nth)
                        link(dve.tensor_reduce(flat, prod[:].rearrange("p n (m c) -> p (n m) c", c=HC), AX_X, ALU.add))
                        folded = flat.rearrange("p (a m) -> p a m", a=lead)
                        bias = pos_[:].rearrange("p (a m) -> p a m", a=1).broadcast_to([128, lead, pos_.shape[1]])
                        link(dve.scalar_tensor_tensor(folded, folded, scale, bias, ALU.mult, ALU.add))
                        link(dve.tensor_reduce(stat[:, 0], dst[:], AX_X, ALU.max))
                        dve.tensor_tensor(dst[:], dst[:], stat[:, 0].rearrange("p (r a) -> p r a", a=1).broadcast_to([128, rows, keys]),
                                          ALU.subtract).then_inc(sig["at_shifted"], 1)

                    def sums(src, stat, nth):
                        dve.wait_ge(sig["at_exp_across"], nth)
                        link(dve.tensor_reduce(stat[:, 1], src[:], AX_X, ALU.add))
                        link(dve.reciprocal(stat[:, 2], stat[:, 1]))

                    def finish3():
                        sums(sc3, st3, 1)
                        dve.wait_ge(sig["at_prod"], 3)
                        link(dve.tensor_reduce(prod3[:].rearrange("p n m -> p (n m)")[:, 0:NC3 * W3 * HC], pv3[:].rearrange("p n (m j) -> p (n m) j", j=W3), AX_X, ALU.add))
                        made = prod3[:].rearrange("p n m -> p (n m)")[:, 0:NC3 * W3 * HC].rearrange("p (f x w c) -> p f x w c", f=2, w=W3, c=HC)
                        over = st3[:, 2].rearrange("p (f x w a) -> p f x w a", f=2, w=W3, a=1)
                        dst = o_tok[:, 3].rearrange("p (f w x c) -> p f x w c", f=2, w=W3, c=HC)
                        for f in range(2):
                            last = dve.tensor_tensor(dst[:, f], made[:, f], over[:, f].broadcast_to([128, NB * HEADS, W3, HC]), ALU.mult)
                        last.then_inc(sig["at_norm"], 1)

                    def finish1():
                        sums(sc1, st1, 2)
                        dve.wait_ge(sig["at_prod"], 4)
                        flat = prod1[:].rearrange("p n m -> p (n m)")[:, 0:HEADS * W1 * HC]
                        link(dve.tensor_reduce(flat, pv1[:].rearrange("p n (m j) -> p (n m) j", j=W1), AX_X, ALU.add))
                        made = flat.rearrange("p (h w c) -> p h w c", h=HEADS, w=W1)
                        over = st1[:, 2].rearrange("p (h w a) -> p h w a", h=HEADS, a=1)
                        dst = o_tok[:, 1].rearrange("p (w h c) -> p h w c", w=W1, h=HEADS)
                        dve.tensor_tensor(dst, made, over.broadcast_to([128, HEADS, W1, HC]), ALU.mult).then_inc(sig["at_norm"], 1)

                    def finish_within(g, units_done):
                        slot = WITHIN[g]
                        dve.wait_ge(sig["at_exp"], units_done)
                        over = rden[:, slot].rearrange("p t j -> p (t j)")
                        link(dve.reciprocal(over, den[:, slot].rearrange("p t j -> p (t j)")))
                        dve.wait_ge(sig["at_out"], units_done)
                        dve.tensor_tensor(o_tok[:, g].rearrange("p (n c) -> p n c", c=HC), p_o[:, slot].rearrange("p t (j c) -> p (t j) c", c=HC),
                                          over.rearrange("p (n a) -> p n a", a=1).broadcast_to([128, NTG * 4, HC]), ALU.mult).then_inc(sig["at_norm"], 1)

                    scores(sc3, st3, prod3, pos4, HC_SCALE, 1, 2 * NB)
                    scores(sc1, st1, prod1, pos2, HC_SCALE, 2, 1)
                    for i in range(EARLY, NU):
                        biased(dve, p_s[:, i % 2], i)
                        if i == EARLY:
                            finish3()
                        if i == EARLY + 2:
                            finish1()
                        if i == END0 + 4:
                            finish_within(0, END0)
                    finish_within(2, NU)
                    dve.wait_ge(sig["at_mixed"], 4)
                    dve.tensor_tensor(x[:], x[:], p_x[:], ALU.add)
                    unchain(link, "dve")

                @block.scalar
                def _(act):
                    def turned_out(nth, quarters):
                        act.wait_ge(sig["at_turned_out"], nth)
                        for g in quarters:
                            last = act.copy(o_chan[:, g], turned(g))
                        last.then_inc(sig["at_chan"], 1)

                    for i in range(2, NU + 2):
                        if EARLY <= i < NU:
                            exponentials(act, i)
                        u = i - 2
                        act.wait_ge(sig["at_turned"], u + 1)
                        if u >= 2:
                            act.wait_ge(sig["at_out"], u - 1)
                        act.copy(pt[:, u % 2], p_t[:, u % 2]).then_inc(sig["at_pt"], 1)
                        if i == 5:
                            act.wait_ge(sig["at_shifted"], 1)
                            act.activation(sc3[:], sc3[:], ACT.Exp).then_inc(sig["at_exp_across"], 1)
                        if i == 8:
                            act.wait_ge(sig["at_shifted"], 2)
                            act.activation(sc1[:], sc1[:], ACT.Exp).then_inc(sig["at_exp_across"], 1)
                        if i == END0 + 4:
                            turned_out(1, MIX[:3])
                    turned_out(2, MIX[3:])

                @block.gpsimd
                def _(pool):
                    for n in range(NC3):
                        f, b, h = n // 4, n // 2 % 2, n % 2
                        ours = e3[:, f, :, b, 0, h].rearrange("p (i a) c -> p i a c", a=1).broadcast_to([128, W3, W3, HC])
                        theirs = e3[:, f, :, b, 1, h].rearrange("p (a j) c -> p a j c", a=1).broadcast_to([128, W3, W3, HC])
                        last = pool.tensor_tensor(prod3[:, n].rearrange("p (i j c) -> p i j c", i=W3, j=W3), ours, theirs, ALU.mult)
                    last.then_inc(sig["at_prod"], 1)
                    for h in range(HEADS):
                        ours = e1[:, :, 0, h].rearrange("p (i a) c -> p i a c", a=1).broadcast_to([128, W1, W1, HC])
                        theirs = e1[:, :, 1, h].rearrange("p (a j) c -> p a j c", a=1).broadcast_to([128, W1, W1, HC])
                        last = pool.tensor_tensor(prod1[:, h].rearrange("p (i j c) -> p i j c", i=W1, j=W1), ours, theirs, ALU.mult)
                    last.then_inc(sig["at_prod"], 1)
                    pool.wait_ge(sig["at_exp_across"], 1)
                    for n in range(NC3):
                        f, b, h = n // 4, n // 2 % 2, n % 2
                        weight = sc3[:, n * W3:(n + 1) * W3].rearrange("p i (a j) -> p i a j", a=1).broadcast_to([128, W3, HC, W3])
                        value = e3[:, f, :, b, 2, h].rearrange("p j (a c) -> p a c j", a=1).broadcast_to([128, W3, HC, W3])
                        last = pool.tensor_tensor(pv3[:, n].rearrange("p (i c j) -> p i c j", i=W3, c=HC), weight, value, ALU.mult)
                    last.then_inc(sig["at_prod"], 1)
                    pool.wait_ge(sig["at_exp_across"], 2)
                    for h in range(HEADS):
                        weight = sc1[:, h * W1:(h + 1) * W1].rearrange("p i (a j) -> p i a j", a=1).broadcast_to([128, W1, HC, W1])
                        value = e1[:, :, 2, h].rearrange("p j (a c) -> p a c j", a=1).broadcast_to([128, W1, HC, W1])
                        last = pool.tensor_tensor(pv1[:, h].rearrange("p (i c j) -> p i c j", i=W1, c=HC), weight, value, ALU.mult)
                    last.then_inc(sig["at_prod"], 1)

    experts("L3", 1)

    with ExitStack() as st:
        o_tok = sb("o_tok", [128, T // 128, NB, C], stack=st)
        p_o = ps("fp_o", [128, T // 128 * R], stack=st)
        with nc.Block() as block:
            @block.tensor
            def _(pe):
                for j in range(T // 128):
                    last = pe.transpose(p_o[:, j * R:(j + 1) * R], x[:, j * 128:(j + 1) * 128], ident[0:R, 0:R])
                last.then_inc(sig["out_turned"], 1)

            @block.vector
            def _(dve):
                dve.wait_ge(sig["out_turned"], 1)
                dve.tensor_copy(o_tok[:].rearrange("p j b c -> p (j b c)"), p_o[:]).then_inc(sig["out_tok"], 1)

            @block.sync
            def _(sp):
                sp.wait_ge(sig["out_tok"], 1)
                for b in range(NB):
                    sp.dma_start(io["out"][b].rearrange("(j p) c -> p j c", p=128), o_tok[:, :, b, :]).then_inc(sig["stored"], 16)
                sp.wait_ge(sig["stored"], 32)
def scan_orders():
    def curve(n, px, py):
        d, s = 0, n // 2
        while s > 0:
            rx = 1 if px & s > 0 else 0
            ry = 1 if py & s > 0 else 0
            d += s * s * (3 * rx ^ ry)
            if ry == 0:
                if rx == 1:
                    px, py = s - 1 - px, s - 1 - py
                px, py = py, px
            s //= 2
        return d

    along = np.argsort(np.array([curve(WIN, i, j) for j in range(WIN) for i in range(WIN)]))
    rows = [(b, int(q)) for q in along for b in range(NB)]
    cols = [(b, int(q) % WIN * WIN + int(q) // WIN) for q in along for b in range(NB)]
    return [rows, cols, rows[::-1], cols[::-1]]


def constants():
    perm = np.zeros((L, 4, L), np.float32)
    for k, order in enumerate(scan_orders()):
        for l, (b, pos) in enumerate(order):
            perm[b * POS + pos, k, l] = 1.0
    pick = np.zeros((3, 2, NS, NS, 2, D), np.float32)
    for n in range(NS):
        for back in range(2):
            pick[:, back, n, n, back, :] = 1.0
    own = np.zeros((NB * E, NB), np.float32)
    for b in range(NB):
        own[b * E:(b + 1) * E, b] = 1.0
    return {
        "ident": np.eye(128, dtype=np.float32),
        "perm": perm,
        "unperm": np.ascontiguousarray(perm.transpose(2, 1, 0)),
        "pick": pick.reshape(96, NS, 128),
        "own": own,
    }


def two(w):
    k, m = w.shape[0], w.shape[-1]
    out = np.zeros((2, k) + w.shape[1:-1] + (2, m), np.float32)
    out[0, ..., 0, :] = w
    out[1, ..., 1, :] = w
    return out.reshape((2 * k,) + w.shape[1:-1] + (2 * m,))


def twice(v):
    return np.concatenate([v, v], axis=0)


def column(v, rows):
    return np.ascontiguousarray(np.broadcast_to(np.reshape(v, (1, -1)), (rows, np.size(v))))


def pack(i):
    a = dict(constants())
    a["x"] = i["x"].reshape(NB, T, C)
    p = "L0_conv_"
    w_in = i[p + "in_proj_w"]
    a["w_in"] = np.stack([two(w_in[:D].T), two(w_in[D:].T)], axis=1)
    a["w_conv"] = twice(i[p + "conv_w"].reshape(D, 9))
    a["b_conv"] = twice(i[p + "conv_b"].reshape(D, 1))
    xp = i[p + "x_proj_w"]
    w_bc = np.zeros((2, D, 2, 2, 2, NS), np.float32)
    for back in range(2):
        for kl in range(2):
            for t in range(2):
                w_bc[back, :, kl, t, back, :] = xp[2 * back + kl, RANK + t * NS:RANK + (t + 1) * NS].T
    a["w_bc"] = w_bc.reshape(2 * D, 2, 4 * NS)
    a["xw"] = xp[:, :RANK].transpose(1, 0, 2)
    a["dtw"] = i[p + "dt_projs_w"].transpose(2, 0, 1)
    a["b_dt"] = i[p + "dt_projs_b"].reshape(2, 2, D).transpose(0, 2, 1).reshape(128, 2)
    a["a_log"] = i[p + "A_logs"].reshape(2, 2, D, NS).transpose(0, 2, 1, 3).reshape(128, 2, NS)
    a["skip"] = i[p + "Ds"].reshape(2, 2, D).transpose(0, 2, 1).reshape(128, 2)
    a["w_out"] = two(i[p + "out_proj_w"].T)
    a["ln_w"] = twice(i[p + "ln_w"].reshape(D, 1))
    a["ln_b"] = twice(i[p + "ln_b"].reshape(D, 1))
    for l in ("L0", "L2"):
        a[l + "_W"] = twice(i[l + "_ffn_W"].T)
        v = np.zeros((2 * C, 128), np.float32)
        v[:C, :C] = i[l + "_ffn_V"].T
        v[C:, :C] = np.eye(C, dtype=np.float32)
        a[l + "_V"] = v
        gb = np.zeros((2 * C, 2), np.float32)
        gb[C:, 0] = i[l + "_ffn_gamma"]
        gb[C:, 1] = i[l + "_ffn_beta"]
        a[l + "_gb"] = gb
    a["bin_w"] = twice(i["L1_conv_W"].transpose(2, 0, 1, 3).reshape(C, 9 * C))
    a["bin_s"] = column(np.concatenate([i["L1_conv_beta"], i["L1_conv_v"], i["L1_conv_bias"]]), R)
    for l in ("L1", "L3"):
        a[l + "_gate"] = two(i[l + "_ffn_gate_w"].T)
        a[l + "_gate_b"] = twice(i[l + "_ffn_gate_b"].reshape(E, 1))
        a[l + "_w1"] = i[l + "_ffn_weight1"].transpose(1, 0, 2)
        a[l + "_w2"] = i[l + "_ffn_weight2"][:, :HID].transpose(1, 0, 2)
        a[l + "_b2"] = i[l + "_ffn_weight2"][:, HID].T
    cf = i["L2_conv_coefs"]
    a["eq_w"] = two(cf.transpose(0, 2, 1))
    a["eq_b"] = twice(np.stack([i["L2_conv_bias"].reshape(C), i["L2_conv_diag_bias"].reshape(C)], axis=1))
    w = {n: i["L3_conv_W" + n].reshape(C, 4, 2, 4) for n in "qkv"}
    for n in "qk":
        o = np.zeros((2, C, 2, 2, 2, 32), np.float32)
        for b in range(2):
            o[b, :, :, b, :, :4] = w[n][:, [2, 0]]
        a["at_" + n] = o.reshape(2 * C, 2, 128)
    o = np.zeros((2, C, 2, 2, 8), np.float32)
    e1 = np.zeros((2, C, 2, 3, 8), np.float32)
    for b in range(2):
        o[b, :, :, b] = w["v"][:, [2, 0]].reshape(C, 2, 8)
        for t, n in enumerate("qkv"):
            e1[b, :, b, t] = w[n][:, 1].reshape(C, 8)
    a["at_v"] = o.reshape(2 * C, 2, 16)
    a["at_e1"] = e1.reshape(2 * C, 2, 24)
    e3 = np.zeros((2, C, 2, 3, 8), np.float32)
    for b in range(2):
        for t, n in enumerate("qkv"):
            e3[b, :, b, t] = w[n][:, 3].reshape(C, 8)
    a["at_e3"] = e3.reshape(2 * C, 48)
    wo = i["L3_conv_Wo"].reshape(4, 8, C)
    o = np.zeros((4, 128, 512), np.float32)
    for g in range(4):
        if g == 1:
            for n in range(16):
                o[g, n * 8:(n + 1) * 8, n * C:(n + 1) * C] = wo[g]
        else:
            for n in range(8):
                for b in range(2):
                    o[g, n * 16 + b * 8:n * 16 + b * 8 + 8, n * 2 * C + b * C:n * 2 * C + (b + 1) * C] = wo[g]
    a["at_o"] = o.transpose(1, 0, 2)
    a["at_bo"] = twice(i["L3_conv_bo"].reshape(C, 1)).reshape(1, 2 * C)
    pos = i["L3_conv_pos1"].reshape(2, 64, 64)
    o = np.full((128, 2, 128), MASKED, np.float32)
    for s in range(2):
        o[s * 64:(s + 1) * 64, :, s * 64:(s + 1) * 64] = pos.transpose(1, 0, 2)
    a["pos1"] = o
    a["pos2"] = column(i["L3_conv_pos2"], 128)
    a["pos3"] = i["L3_conv_pos3"].reshape(2, 2, 128, 256).transpose(2, 1, 0, 3)
    a["pos4"] = column(i["L3_conv_pos4"], 128)
    return {k: np.ascontiguousarray(v) for k, v in a.items()}


def kernel(**inputs):
    import concourse.bacc as bacc
    from concourse.bass_utils import run_bass_kernel_spmd

    nc = bacc.Bacc("TRN2", target_bir_lowering=False, num_devices=1)
    arrays = pack({k: np.asarray(v) for k, v in inputs.items()})
    io = {n: nc.dram_tensor(f"in_{n}", a.shape, mybir.dt.from_np(a.dtype), kind="ExternalInput").ap()
          for n, a in arrays.items()}
    io["out"] = nc.dram_tensor("out_x", (NB, T, C), F32, kind="ExternalOutput").ap()
    build_program(nc, io)
    r = run_bass_kernel_spmd(nc, [{f"in_{n}": a for n, a in arrays.items()}], core_ids=[0])
    return r.results[0]["out_x"].reshape(NB, SIDE, SIDE, C)
```

```python
import numpy as np
import concourse.bass as bass
from concourse import mybir
from contextlib import ExitStack

F32 = mybir.dt.float32
BF16 = mybir.dt.bfloat16
I32 = mybir.dt.int32
ACT = mybir.ActivationFunctionType
ALU = mybir.AluOpType
AX_X = mybir.AxisListType.X

NB, SIDE, C = 2, 32, 32
T = SIDE * SIDE
R = NB * C
D = 64
NS = 16
WIN = 8
NW = (SIDE // WIN) ** 2
POS = WIN * WIN
L = NB * POS
RANK = 8
BANK = 512
E, HID, TOPK = 16, 128, 8
MARK = -3e38
NLEV = 5
NACT = 3
NBASIS = 15
HC_SCALE = 0.25
MASKED = -1e30


class Signals(dict):

    def __init__(self, nc, ctx):
        super().__init__()
        self.nc, self.ctx = nc, ctx

    def __missing__(self, name):
        self[name] = self.ctx.enter_context(self.nc.semaphore(name))
        return self[name]


class Chain:

    def __init__(self, eng, sem):
        self.eng, self.sem, self.n = eng, sem, 0

    def __call__(self, ins):
        self.n += 1
        ins.then_inc(self.sem, 1)
        self.eng.wait_ge(self.sem, self.n)


def build_program(nc, io):
    with ExitStack() as ctx:
        sig = Signals(nc, ctx)
        chain_n = {"dve": 0, "act": 0, "pool": 0}

        def sb(name, shape, dt=F32, stack=ctx):
            return stack.enter_context(nc.sbuf_tensor(name, shape, dt))

        def ps(name, shape, dt=F32, stack=ctx):
            return stack.enter_context(nc.psum_tensor(name, shape, dt))

        def chain(eng, name):
            c = Chain(eng, sig["chain_" + name])
            c.n = chain_n[name]
            return c

        def unchain(c, name):
            chain_n[name] = c.n

        ident = sb("ident", [128, 128])
        ones64 = sb("ones64", [R, R])
        eps6 = sb("eps6", [128, 1])
        eps5 = sb("eps5", [128, 1])
        x = sb("x", [R, T])
        xn = sb("xn", [R, T])
        xn_tok = sb("xn_tok", [128, T // 128, R])
        ln_sq = sb("ln_sq", [128, 2, 4 * R])
        ln_stat = sb("ln_stat", [128, 2, 5, 4 * NB])
        ln_warm = sb("ln_warm", [128, 1])

        ln_uses = [0]

        class Norm:

            def __init__(self, p_tok, p_back, eps, apart=False, k=None):
                if k is None:
                    k = ln_uses[0]
                    ln_uses[0] += 1
                self.k, self.eps, self.apart = k, eps, apart
                bank = (lambda h: 0) if apart else (lambda h: h * BANK)
                self.turned = [p_tok[:, bank(h):bank(h) + 4 * R] for h in range(2)]
                self.back = [p_back[:, bank(h):bank(h) + BANK] for h in range(2)]

            def at(self, name, h):
                return sig[name], 2 * self.k + h + 1

            def step(self, i, h):
                return sig["ln_step"], 10 * self.k + (5 * h + i if self.apart else 2 * i + h) + 1

            def turn(self, pe, h, j):
                t = (4 * h + j) * 128
                ins = pe.transpose(self.turned[h][:, j * R:(j + 1) * R], x[:, t:t + 128], ident[0:R, 0:R])
                if j == 3:
                    ins.then_inc(sig["ln_turned"], 1)

            def turn_back(self, pe, h, j):
                if j == 0:
                    pe.wait_ge(*self.at("ln_scaled", h))
                ins = pe.transpose(self.back[h][:, j * 128:(j + 1) * 128], xn_tok[:, 4 * h + j], ident[:])
                if j == 3:
                    ins.then_inc(sig["ln_back"], 1)

            def pe(self, pe):
                for move in (self.turn, self.turn_back):
                    for h in range(2):
                        for j in range(4):
                            move(pe, h, j)

            def dve(self, dve, hs=(0, 1)):
                by_token = lambda t: t.rearrange("p (g c) -> p g c", c=C)
                spread = lambda t: t.rearrange("p (g a) -> p g a", a=1).broadcast_to([128, 4 * NB, C])
                tok = lambda h: xn_tok[:, 4 * h:4 * h + 4].rearrange("p j r -> p (j r)")
                for h in hs:
                    dve.wait_ge(*self.at("ln_turned", h))
                    dve.tensor_reduce(ln_stat[:, h, 0], by_token(self.turned[h]), AX_X, ALU.add).then_inc(sig["ln_step"], 1)
                for h in hs:
                    dve.wait_ge(*self.step(0, h))
                    dve.tensor_scalar(ln_stat[:, h, 1], ln_stat[:, h, 0], 1.0 / C, None, ALU.mult).then_inc(sig["ln_step"], 1)
                for h in hs:
                    dve.wait_ge(*self.step(1, h))
                    dve.tensor_tensor(by_token(tok(h)), by_token(self.turned[h]), spread(ln_stat[:, h, 1]), ALU.subtract).then_inc(sig["ln_step"], 1)
                for h in hs:
                    dve.wait_ge(*self.step(2, h))
                    dve.tensor_tensor(ln_sq[:, h], tok(h), tok(h), ALU.mult).then_inc(sig["ln_step"], 1)
                for h in hs:
                    dve.wait_ge(*self.step(3, h))
                    dve.tensor_reduce(ln_stat[:, h, 2], by_token(ln_sq[:, h]), AX_X, ALU.add).then_inc(sig["ln_square"], 1)
                for h in hs:
                    dve.wait_ge(*self.at("ln_sd", h))
                    dve.reciprocal(ln_stat[:, h, 4], ln_stat[:, h, 3]).then_inc(sig["ln_step"], 1)
                    dve.wait_ge(*self.step(4, h))
                    dve.tensor_tensor(by_token(tok(h)), by_token(tok(h)), spread(ln_stat[:, h, 4]), ALU.mult).then_inc(sig["ln_scaled"], 1)
                if self.apart:
                    for h in hs:
                        dve.wait_ge(*self.at("ln_back", h))
                        dve.tensor_copy(xn[:, h * BANK:(h + 1) * BANK], self.back[h]).then_inc(sig["ln_out"], 1)

            def act_roots(self, act, h):
                act.wait_ge(*self.at("ln_square", h))
                act.activation(ln_stat[:, h, 3], ln_stat[:, h, 2], ACT.Sqrt, bias=self.eps[:, 0:1], scale=1.0 / C).then_inc(sig["ln_sd"], 1)

            def act(self, act):
                act.activation(ln_warm[:], self.eps[:], ACT.Sqrt)
                for h in range(2):
                    self.act_roots(act, h)
                for h in range(2):
                    act.wait_ge(*self.at("ln_back", h))
                    act.copy(xn[:, h * BANK:(h + 1) * BANK], self.back[h]).then_inc(sig["ln_out"], 1)

            def wait_out(self, eng, h=1):
                eng.wait_ge(sig["ln_out"], 2 * self.k + h + 1)

            def wait_tokens(self, eng):
                eng.wait_ge(sig["ln_scaled"], 2 * self.k + 2)

        with ExitStack() as st:
            x_tok = sb("x_tok", [128, T // 128, NB, C], stack=st)
            p_x = ps("p_x", [R, T], stack=st)
            with nc.Block() as block:
                @block.sync
                def _(sp):
                    sp.dma_start(ident[:], io["ident"]).then_inc(sig["load_const"], 16)
                    for b in range(NB):
                        sp.dma_start(x_tok[:, :, b, :], io["x"][b].rearrange("(j p) c -> p j c", p=128)).then_inc(sig["load_x"], 16)
                    sp.wait_ge(sig["load_const"], 16)

                @block.gpsimd
                def _(pool):
                    pool.memset(eps6[:], 1e-6)
                    pool.memset(eps5[:], 1e-5)
                    pool.memset(ones64[:], 1.0)

                @block.tensor
                def _(pe):
                    pe.wait_ge(sig["load_x"], 32)
                    pe.wait_ge(sig["load_const"], 16)
                    for j in range(T // 128):
                        last = pe.transpose(p_x[:, j * 128:(j + 1) * 128], x_tok[:, j].rearrange("p b c -> p (b c)"), ident[:])
                    last.then_inc(sig["x_turned"], 1)

                @block.vector
                def _(dve):
                    dve.wait_ge(sig["x_turned"], 1)
                    dve.tensor_copy(x[:], p_x[:])

        with ExitStack() as st:
            z_gate = sb("z_gate", [128, T], stack=st)
            seq = sb("seq", [128, 2, NW, L], stack=st)
            conv = sb("conv", [128, NW, POS], stack=st)
            w_out = sb("w_out", [128, R], stack=st)
            ln_w = sb("ln_w", [128, 1], stack=st)
            ln_b = sb("ln_b", [128, 1], stack=st)
            skip = sb("skip", [128, 2], stack=st)
            unperm = sb("unperm", [L, 4, L], stack=st)
            step = sb("step", [128, 2, NW * L], stack=st)
            drive = sb("drive", [128, 2, NW * L], stack=st)
            b_parts = sb("b_parts", [96, 2, NW * L], BF16, stack=st)
            c_parts = sb("c_parts", [96, 2, NW * L], BF16, stack=st)
            decay = sb("decay", [128, 2, NS], stack=st)
            pick = sb("pick", [96, NS, 128], BF16, stack=st)
            y_seq = sb("y_seq", [128, 2, NW * L], stack=st)

            with ExitStack() as s2:
                w_in = sb("w_in", [R, 2, 128], stack=s2)
                w_conv = sb("w_conv", [128, 9], stack=s2)
                b_conv = sb("b_conv", [128, 1], stack=s2)
                w_bc = sb("w_bc", [128, 2, D], stack=s2)
                xw = sb("xw", [RANK, 4, D], stack=s2)
                dtw = sb("dtw", [RANK, 4, D], stack=s2)
                b_dt = sb("b_dt", [128, 2], stack=s2)
                w_dt = sb("w_dt", [128, 2, 128], stack=s2)
                perm = sb("perm", [L, 4, L], stack=s2)
                padded = sb("padded", [128, SIDE + 2, SIDE + 2], stack=s2)
                acc = sb("acc", [128, SIDE, SIDE], stack=s2)
                pick_f = y_seq[0:96, 0].rearrange("p (n m) -> p n m", n=NS)
                tok = sb("tok", [L, NW, D], stack=s2)
                with ExitStack() as s3:
                    p_a = ps("p_a", [128, T], stack=s3)
                    p_b = ps("p_b", [R, T], stack=s3)
                    p_v = ps("p_v", [128, T], stack=s3)
                    p_z = ps("p_z", [128, T], stack=s3)
                    norm = Norm(p_a, p_b, eps6)
                    tap = lambda k: padded[:, k // 3:k // 3 + SIDE, k % 3:k % 3 + SIDE]
                    AWAY = 3
                    tap_out = [step[:, n // 2, n % 2 * T:(n % 2 + 1) * T].rearrange("p (y x) -> p y x", y=SIDE) for n in range(AWAY)]
                    with nc.Block() as block:
                        @block.sync
                        def _(sp):
                            for t, n in ((w_in, "w_in"), (w_conv, "w_conv"), (b_conv, "b_conv"), (decay, "a_log")):
                                sp.dma_start(t[:], io[n]).then_inc(sig["load_in"], 16)
                            for t, n in ((w_bc, "w_bc"), (xw, "xw"), (dtw, "dtw"), (b_dt, "b_dt"), (perm, "perm"),
                                         (skip, "skip"), (pick_f, "pick"), (w_out, "w_out"),
                                         (ln_w, "ln_w"), (ln_b, "ln_b"), (unperm, "unperm")):
                                sp.dma_start(t[:] if t is not pick_f else t, io[n]).then_inc(sig["load_scan"], 16)
                            sp.wait_ge(sig["load_scan"], 16 * 11)

                        @block.gpsimd
                        def _(pool):
                            pool.memset(padded[:], 0.0).then_inc(sig["border_zero"], 1)
                            pool.memset(w_dt[:], 0.0)
                            for n in range(1, AWAY):
                                pool.wait_ge(sig["tap_made"], n + 1)
                                if n > 1:
                                    pool.wait_ge(sig["tap_added"], n - 1)
                                pool.tensor_tensor(tap_out[0], tap_out[0], tap_out[n], ALU.add).then_inc(sig["tap_added"], 1)

                        @block.tensor
                        def _(pe):
                            norm.pe(pe)
                            pe.wait_ge(sig["load_in"], 64)
                            for h in range(2):
                                c = slice(h * BANK, (h + 1) * BANK)
                                norm.wait_out(pe, h)
                                pe.matmul(p_v[:, c], w_in[:, 0], xn[:, c], start=True, stop=True).then_inc(sig["xv"], 1)
                            for h in range(2):
                                c = slice(h * BANK, (h + 1) * BANK)
                                pe.matmul(p_z[:, c], w_in[:, 1], xn[:, c], start=True, stop=True).then_inc(sig["z"], 1)

                        @block.vector
                        def _(dve):
                            link = chain(dve, "dve")
                            norm.dve(dve)
                            dve.wait_ge(sig["load_in"], 64)
                            dve.wait_ge(sig["padded_in"], 2)
                            link(dve.tensor_scalar(acc[:], tap(0), w_conv[:, 0:1], None, ALU.mult))
                            for k in range(1, 9 - AWAY):
                                link(dve.scalar_tensor_tensor(acc[:], tap(k), w_conv[:, k:k + 1], acc[:], ALU.mult, ALU.add))
                            dve.wait_ge(sig["tap_added"], AWAY - 1)
                            dve.tensor_tensor(acc[:], acc[:], tap_out[0], ALU.add).then_inc(sig["conv_sum"], 1)
                            unchain(link, "dve")

                        @block.scalar
                        def _(act):
                            link = chain(act, "act")
                            norm.act(act)
                            act.wait_ge(sig["border_zero"], 1)
                            for h in range(2):
                                act.wait_ge(sig["xv"], h + 1)
                                act.activation(padded[:, 1 + 16 * h:17 + 16 * h, 1:1 + SIDE],
                                               p_v[:, h * BANK:(h + 1) * BANK].rearrange("p (y x) -> p y x", y=16),
                                               ACT.Copy).then_inc(sig["padded_in"], 1)
                            act.wait_ge(sig["load_in"], 64)
                            act.wait_ge(sig["padded_in"], 2)
                            for n in range(AWAY):
                                act.activation(tap_out[n], tap(9 - AWAY + n), ACT.Copy, scale=w_conv[:, 9 - AWAY + n:10 - AWAY + n]).then_inc(sig["tap_made"], 1)
                            link(act.activation(decay[:], decay[:], ACT.Exp))
                            act.activation(decay[:], decay[:], ACT.Copy, scale=-1.0)
                            act.wait_ge(sig["z"], 2)
                            act.activation(z_gate[:], p_z[:], ACT.Silu)
                            act.wait_ge(sig["conv_sum"], 1)
                            for wy in range(SIDE // WIN):
                                dst = conv[:, 4 * wy:4 * wy + 4].rearrange("p w (y x) -> p y w x", y=WIN)
                                src = acc[:, WIN * wy:WIN * wy + WIN].rearrange("p y (w x) -> p y w x", w=4)
                                act.activation(dst, src, ACT.Silu, bias=b_conv[:, 0:1])
                            unchain(link, "act")

                with ExitStack() as s3:
                    p_t = ps("p_t", [L, NW * D], stack=s3)
                    p_w = ps("p_w", [128, 128], stack=s3)
                    p_s = ps("p_s", [128, 4, BANK], stack=s3)
                    NPAIR = NW // 2
                    with nc.Block() as block:
                        @block.gpsimd
                        def _(pool):
                            pool.tensor_copy(pick[:], pick_f)

                        @block.tensor
                        def _(pe):
                            for w in range(NW):
                                for b in range(NB):
                                    rows = slice(b * D, (b + 1) * D)
                                    last = pe.matmul(p_t[b * POS:(b + 1) * POS, w * D:(w + 1) * D], conv[rows, w], ident[rows, rows],
                                                     start=True, stop=True)
                                if w % 8 == 7:
                                    last.then_inc(sig["tok_turned"], 1)
                            for k in range(4):
                                back, kl = k // 2, k % 2
                                last = pe.matmul(p_w[back * D:(back + 1) * D, kl * D:(kl + 1) * D], xw[:, k], dtw[:, k], start=True, stop=True)
                            last.then_inc(sig["step_weight"], 1)
                            for i in range(NPAIR):
                                pe.wait_ge(sig["tok_copied"], i // 4 + 1)
                                if i >= 4:
                                    pe.wait_ge(sig["seq_copied_even" if i % 2 == 0 else "seq_copied_odd"], (i - 4) // 2 + 1)
                                for j in range(2):
                                    w = 2 * i + j
                                    for back in range(2):
                                        last = pe.matmul(p_s[back * D:(back + 1) * D, i % 4, 256 * j:256 * j + 256], tok[:, w],
                                                         perm[:, 2 * back:2 * back + 2].rearrange("p k l -> p (k l)"), start=True, stop=True)
                                last.then_inc(sig["seq_made"], 1)

                        def copy_seq(i, copy):
                            return copy(seq[:, :, 2 * i:2 * i + 2].rearrange("p k w l -> p w k l"),
                                        p_s[:, i % 4].rearrange("p (w k l) -> p w k l", w=2, k=2))

                        @block.vector
                        def _(dve):
                            for h in range(2):
                                dve.wait_ge(sig["tok_turned"], h + 1)
                                dve.tensor_copy(tok[:, 8 * h:8 * h + 8].rearrange("p w d -> p (w d)"), p_t[:, h * BANK:(h + 1) * BANK]).then_inc(sig["tok_copied"], 1)
                            dve.wait_ge(sig["step_weight"], 1)
                            for back in range(2):
                                rows = slice(back * D, (back + 1) * D)
                                dve.tensor_copy(w_dt[rows, :, back * D:(back + 1) * D],
                                                p_w[rows, :].rearrange("p (k d) -> p k d", k=2))
                            for i in range(0, NPAIR, 2):
                                dve.wait_ge(sig["seq_made"], i + 1)
                                copy_seq(i, dve.tensor_copy).then_inc(sig["seq_copied_even"], 1)

                        @block.scalar
                        def _(act):
                            for i in range(1, NPAIR, 2):
                                act.wait_ge(sig["seq_made"], i + 1)
                                copy_seq(i, act.copy).then_inc(sig["seq_copied_odd"], 1)

                with ExitStack() as s3:
                    p_bc = ps("p_bc", [R, 2, BANK], stack=s3)
                    p_d = ps("p_d", [128, 2, BANK], stack=s3)
                    part = [sb(f"part{i}", [64, 2, NW * L], BF16, stack=s3) for i in range(3)]
                    rest = sb("rest", [64, 2, NW * L], stack=s3)
                    zd = sb("zd", [128, 2, NW * L], stack=s3)
                    ex = sb("ex", [128, 2, NW * L], stack=s3)
                    ln_one = sb("ln_one", [128, 1], stack=s3)
                    NCH = 8
                    def cols(i):
                        return i // 4, slice((i % 4) * BANK, (i % 4 + 1) * BANK)
                    seqf = seq[:].rearrange("p k w l -> p k (w l)")
                    with nc.Block() as block:
                        @block.tensor
                        def _(pe):
                            for i in range(NCH):
                                k, c = cols(i)
                                if i >= 2:
                                    pe.wait_ge(sig["step_read"], i - 1)
                                pe.matmul(p_d[:, i % 2], w_dt[:, k], seqf[:, k, c], start=True, stop=True).then_inc(sig["step_made"], 1)
                                if i >= 2:
                                    pe.wait_ge(sig["bc_read"], i - 1)
                                pe.matmul(p_bc[:, i % 2], w_bc[:, k], seqf[:, k, c], start=True, stop=True).then_inc(sig["bc_made"], 1)

                        @block.scalar
                        def _(act):
                            for i in range(NCH):
                                k, c = cols(i)
                                act.wait_ge(sig["step_made"], i + 1)
                                act.activation(zd[:, k, c], p_d[:, i % 2], ACT.Identity, bias=b_dt[:, k:k + 1]).then_inc(sig["step_read"], 1)
                                act.wait_ge(sig["bc_made"], i + 1)
                                act.activation(part[0][:, k, c], p_bc[:, i % 2], ACT.Copy).then_inc(sig["part_hi"], 1)
                            for i in range(NCH):
                                k, c = cols(i)
                                act.wait_ge(sig["neg_abs"], i + 2)
                                act.activation(ex[:, k, c], ex[:, k, c], ACT.Exp).then_inc(sig["exp_neg"], 1)
                            act.wait_ge(sig["exp_neg"], NCH)
                            act.activation(ln_one[:], ln_one[:], ACT.Ln, bias=1.0).then_inc(sig["ln_one"], 1)
                            for i in range(NCH):
                                k, c = cols(i)
                                act.activation(step[:, k, c], ex[:, k, c], ACT.Ln, bias=1.0).then_inc(sig["log1"], 1)

                        @block.vector
                        def _(dve):
                            dve.memset(ln_one[:], 0.0).then_inc(sig["neg_abs"], 1)
                            for i in range(NCH):
                                k, c = cols(i)
                                dve.wait_ge(sig["part_hi"], i + 1)
                                dve.tensor_tensor(rest[:, k, c], p_bc[:, i % 2], part[0][:, k, c], ALU.subtract).then_inc(sig["bc_read"], 1)
                                dve.wait_ge(sig["step_read"], i + 1)
                                dve.scalar_tensor_tensor(ex[:, k, c], zd[:, k, c], -1.0, zd[:, k, c], ALU.mult, ALU.min).then_inc(sig["neg_abs"], 1)
                                dve.wait_ge(sig["bc_read"], i + 1)
                                dve.tensor_copy(part[1][:, k, c], rest[:, k, c]).then_inc(sig["part_mid"], 1)
                            for i in range(NCH):
                                k, c = cols(i)
                                dve.wait_ge(sig["exp_neg"], i + 1)
                                dve.tensor_scalar(drive[:, k, c], ex[:, k, c], 1.0, -1.0, ALU.add, ALU.add).then_inc(sig["kept"], 1)
                            for i in range(NCH):
                                k, c = cols(i)
                                dve.wait_ge(sig["ln_one"], 1)
                                dve.wait_ge(sig["lost"], i + 1)
                                dve.wait_ge(sig["log1"], i + 1)
                                dve.scalar_tensor_tensor(step[:, k, c], step[:, k, c], ln_one[:, 0:1], drive[:, k, c],
                                                         ALU.subtract, ALU.add).then_inc(sig["log1p"], 1)
                            for i in range(NCH):
                                k, c = cols(i)
                                dve.wait_ge(sig["log1p"], i + 1)
                                dve.scalar_tensor_tensor(step[:, k, c], zd[:, k, c], 0.0, step[:, k, c], ALU.max, ALU.add).then_inc(sig["softplus"], 1)
                            for i in range(0, NCH, 2):
                                k, c = cols(i)
                                dve.wait_ge(sig["softplus"], i + 1)
                                dve.tensor_tensor(drive[:, k, c], step[:, k, c], seqf[:, k, c], ALU.mult)

                        @block.gpsimd
                        def _(pool):
                            for i in range(NCH):
                                k, c = cols(i)
                                pool.wait_ge(sig["part_mid"], i + 1)
                                pool.tensor_tensor(part[2][:, k, c], rest[:, k, c], part[1][:, k, c], ALU.subtract).then_inc(sig["part_lo"], 1)
                            for i in range(NCH):
                                k, c = cols(i)
                                pool.wait_ge(sig["kept"], i + 1)
                                pool.tensor_tensor(drive[:, k, c], ex[:, k, c], drive[:, k, c], ALU.subtract).then_inc(sig["lost"], 1)
                            for i in range(1, NCH, 2):
                                k, c = cols(i)
                                pool.wait_ge(sig["softplus"], i + 1)
                                pool.tensor_tensor(drive[:, k, c], step[:, k, c], seqf[:, k, c], ALU.mult)

                        @block.sync
                        def _(sp):
                            for i, s in enumerate(("part_hi", "part_mid", "part_lo")):
                                sp.wait_ge(sig[s], NCH)
                                for dst, row in ((b_parts, 0), (c_parts, 32)):
                                    sp.dma_start(dst[32 * i:32 * i + 32], part[i][row:row + 32]).then_inc(sig["parts_stacked"], 16)
                            sp.wait_ge(sig["parts_stacked"], 96)

            with ExitStack() as s2:
                UC = NW * L // 2
                RING = 3
                p_bb = ps("p_bb", [128, 2, UC], stack=s2)
                p_cb = ps("p_cb", [128, UC], stack=s2)
                p_y = ps("p_y", [128, UC], stack=s2)
                d_a = sb("d_a", [128, 2, UC], stack=s2)
                d_bu = sb("d_bu", [128, RING, UC], stack=s2)
                hs = sb("hs", [128, RING, UC], stack=s2)
                cb = sb("cb", [128, RING, UC], stack=s2)
                hc = sb("hc", [128, RING, UC], stack=s2)
                NU = 4 * NS
                def unit(u):
                    g, n = divmod(u, NS)
                    return g // 2, (g % 2) * UC, n
                with nc.Block() as block:
                    @block.tensor
                    def _(pe):
                        for u in range(NU + RING):
                            if u < NU:
                                k, c0, n = unit(u)
                                if u >= 2:
                                    pe.wait_ge(sig["d_bu"], u - 1)
                                for h in range(2):
                                    c = slice(c0 + h * BANK, c0 + (h + 1) * BANK)
                                    last = pe.matmul(p_bb[:, u % 2, h * BANK:(h + 1) * BANK], pick[:, n], b_parts[:, k, c], start=True, stop=True)
                                last.then_inc(sig["b_spread"], 1)
                                if u >= 1:
                                    pe.wait_ge(sig["c_copied"], u)
                                for h in range(2):
                                    c = slice(c0 + h * BANK, c0 + (h + 1) * BANK)
                                    last = pe.matmul(p_cb[:, h * BANK:(h + 1) * BANK], pick[:, n], c_parts[:, k, c], start=True, stop=True)
                                last.then_inc(sig["c_spread"], 1)
                            if u >= RING:
                                v = u - RING
                                n = v % NS
                                if n == 0 and v:
                                    pe.wait_ge(sig["y_read"], v // NS)
                                pe.wait_ge(sig["hc"], v + 1)
                                for h in range(2):
                                    c = slice(h * BANK, (h + 1) * BANK)
                                    last = pe.matmul(p_y[:, c], ident[:], hc[:, v % RING, c], start=(n == 0), stop=(n == NS - 1))
                                last.then_inc(sig["y_summed"], 1)

                    @block.scalar
                    def _(act):
                        act.wait_ge(sig["first_decay_zero"], 1)
                        for u in range(NU):
                            k, c0, n = unit(u)
                            if u >= 2:
                                act.wait_ge(sig["scanned"], u - 1)
                            src = step[:, k, c0:c0 + UC].rearrange("p (w l) -> p w l", l=L)
                            dst = d_a[:, u % 2].rearrange("p (w l) -> p w l", l=L)
                            act.activation(dst[:, :, 1:L], src[:, :, 1:L], ACT.Exp, scale=decay[:, k, n:n + 1]).then_inc(sig["d_a"], 1)
                            act.wait_ge(sig["c_spread"], u + 1)
                            if u >= RING:
                                act.wait_ge(sig["hc"], u - RING + 1)
                            act.activation(cb[:, u % RING], p_cb[:], ACT.Copy).then_inc(sig["c_copied"], 1)

                    @block.vector
                    def _(dve):
                        def read_y(g):
                            k, c0, _ = unit(g * NS)
                            dve.wait_ge(sig["y_summed"], (g + 1) * NS)
                            dve.scalar_tensor_tensor(y_seq[:, k, c0:c0 + UC], seqf[:, k, c0:c0 + UC], skip[:, k:k + 1], p_y[:],
                                                     ALU.mult, ALU.add).then_inc(sig["y_read"], 1)
                        for u in range(NU + 1):
                            if u < NU:
                                k, c0, n = unit(u)
                                dve.wait_ge(sig["b_spread"], u + 1)
                                if u >= RING:
                                    dve.wait_ge(sig["scanned"], u - RING + 1)
                                dve.tensor_tensor(d_bu[:, u % RING], drive[:, k, c0:c0 + UC], p_bb[:, u % 2], ALU.mult).then_inc(sig["d_bu"], 1)
                            if u >= 1:
                                v = u - 1
                                dve.wait_ge(sig["d_bu"], v + 1)
                                dve.wait_ge(sig["d_a"], v + 1)
                                if v >= RING:
                                    dve.wait_ge(sig["hc"], v - RING + 1)
                                dve.tensor_tensor_scan(hs[:, v % RING], d_a[:, v % 2], d_bu[:, v % RING], 0.0, ALU.mult, ALU.add).then_inc(sig["scanned"], 1)
                                if v >= NS and v % NS == 1:
                                    read_y(v // NS - 1)
                        read_y(3)

                    @block.gpsimd
                    def _(pool):
                        pool.memset(d_a[:], 0.0).then_inc(sig["first_decay_zero"], 1)
                        for u in range(NU):
                            pool.wait_ge(sig["scanned"], u + 1)
                            pool.wait_ge(sig["c_copied"], u + 1)
                            if u >= RING:
                                pool.wait_ge(sig["y_summed"], u - RING + 1)
                            pool.tensor_tensor(hc[:, u % RING], hs[:, u % RING], cb[:, u % RING], ALU.mult).then_inc(sig["hc"], 1)

            with ExitStack() as s2:
                y_l = sb("y_l", [L, 4, NW, D], stack=s2)
                y_tok = sb("y_tok", [L, NW, D], stack=s2)
                y_sq = sb("y_sq", [L, NW, D], stack=s2)
                stat = sb("stat", [L, 3, NW], stack=s2)
                y_img = sb("y_img", [128, SIDE, SIDE], stack=s2)
                p_tr = ps("p_tr", [128, 4, BANK], stack=s2)
                p_tok = ps("p_tok", [L, NW * D], stack=s2)
                p_o = ps("p_o", [R, T], stack=s2)
                yv = y_seq[:].rearrange("p k (w l) -> p k w l", l=L)
                NTR = 2 * NW // 4
                p_img = p_tr[:, 0:2].rearrange("p h n -> p (h n)")
                with nc.Block() as block:
                    def group(i):
                        return i % 4 // 2, 8 * (i // 4) + 4 * (i % 2)

                    @block.tensor
                    def _(pe):
                        for i in range(NTR):
                            k, w0 = group(i)
                            if i >= 4:
                                pe.wait_ge(sig["yl_copied_even" if i % 2 == 0 else "yl_copied_odd"], (i - 4) // 2 + 1)
                            for j in range(4):
                                last = pe.transpose(p_tr[:, i % 4, j * 128:(j + 1) * 128], yv[:, k, w0 + j], ident[:])
                            last.then_inc(sig["yl_turned"], 1)
                        for h in range(2):
                            pe.wait_ge(sig["yl_copied_even"], NTR // 4 * (h + 1))
                            pe.wait_ge(sig["yl_copied_odd"], NTR // 4 * (h + 1))
                            for k in range(4):
                                last = pe.matmul(p_tok[:, h * BANK:(h + 1) * BANK], unperm[:, k],
                                                 y_l[:, k, 8 * h:8 * h + 8].rearrange("p w d -> p (w d)"), start=(k == 0), stop=(k == 3))
                            last.then_inc(sig["y_in_order"], 1)
                        for w in range(NW):
                            if w % 8 == 0:
                                pe.wait_ge(sig["y_normed"], w // 8 + 1)
                            for b in range(NB):
                                rows = slice(b * POS, (b + 1) * POS)
                                last = pe.matmul(p_img[b * D:(b + 1) * D, w * POS:(w + 1) * POS], y_tok[rows, w], ident[rows, rows], start=True, stop=True)
                            if w % 8 == 7:
                                last.then_inc(sig["y_turned"], 1)
                        for h in range(2):
                            pe.wait_ge(sig["y_gated"], h + 1)
                            pe.matmul(p_o[:, h * BANK:(h + 1) * BANK], w_out[:], y_img[:, 16 * h:16 * h + 16].rearrange("p y x -> p (y x)"),
                                      start=True, stop=True).then_inc(sig["mixed"], 1)

                    def copy_yl(i, copy):
                        k, w = group(i)
                        return copy(y_l[:].rearrange("p (b k) w d -> p k w b d", b=2)[:, k, w:w + 4],
                                    p_tr[:, i % 4].rearrange("p (w b d) -> p w b d", w=4, b=2))

                    @block.vector
                    def _(dve):
                        link = chain(dve, "dve")
                        for i in range(0, NTR, 2):
                            dve.wait_ge(sig["yl_turned"], i + 1)
                            copy_yl(i, dve.tensor_copy).then_inc(sig["yl_copied_even"], 1)
                        in_half = [slice(8 * h, 8 * h + 8) for h in range(2)]
                        pt = p_tok[:].rearrange("p (w d) -> p w d", d=D)
                        spread = lambda n, w: stat[:, n, w].rearrange("p (w a) -> p w a", a=1).broadcast_to([L, NW // 2, D])
                        for h, w in enumerate(in_half):
                            dve.wait_ge(sig["y_in_order"], h + 1)
                            link(dve.tensor_reduce(stat[:, 0, w], pt[:, w], AX_X, ALU.add))
                            link(dve.tensor_scalar(stat[:, 0, w], stat[:, 0, w], 1.0 / D, None, ALU.mult))
                            dve.tensor_tensor(y_tok[:, w], pt[:, w], spread(0, w), ALU.subtract).then_inc(sig["y_centred"], 1)
                        for h, w in enumerate(in_half):
                            dve.wait_ge(sig["y_squared"], h + 1)
                            dve.tensor_reduce(stat[:, 1, w], y_sq[:, w], AX_X, ALU.add).then_inc(sig["y_sqsum"], 1)
                        for h, w in enumerate(in_half):
                            dve.wait_ge(sig["y_sd"], h + 1)
                            link(dve.reciprocal(stat[:, 2, w], stat[:, 2, w]))
                            dve.tensor_tensor(y_tok[:, w], y_tok[:, w], spread(2, w), ALU.mult).then_inc(sig["y_normed"], 1)
                        for h in range(2):
                            dve.wait_ge(sig["y_scaled"], 2 * h + 2)
                            v = y_img[:, 16 * h:16 * h + 16]
                            dve.tensor_tensor(v, v, z_gate[:, h * BANK:(h + 1) * BANK].rearrange("p (y x) -> p y x", y=16), ALU.mult).then_inc(sig["y_gated"], 1)
                        for h in range(2):
                            c = slice(h * BANK, (h + 1) * BANK)
                            dve.wait_ge(sig["mixed"], h + 1)
                            dve.tensor_tensor(x[:, c], x[:, c], p_o[:, c], ALU.add)
                        unchain(link, "dve")

                    @block.scalar
                    def _(act):
                        for i in range(1, NTR, 2):
                            act.wait_ge(sig["yl_turned"], i + 1)
                            copy_yl(i, act.copy).then_inc(sig["yl_copied_odd"], 1)
                        act.activation(ln_warm[:], eps5[:], ACT.Sqrt)
                        for h in range(2):
                            w = slice(8 * h, 8 * h + 8)
                            act.wait_ge(sig["y_centred"], h + 1)
                            act.activation(y_sq[:, w], y_tok[:, w], ACT.Square).then_inc(sig["y_squared"], 1)
                        for h in range(2):
                            w = slice(8 * h, 8 * h + 8)
                            act.wait_ge(sig["y_sqsum"], h + 1)
                            act.activation(stat[:, 2, w], stat[:, 1, w], ACT.Sqrt, bias=eps5[:, 0:1], scale=1.0 / D).then_inc(sig["y_sd"], 1)
                        for wy in range(SIDE // WIN):
                            act.wait_ge(sig["y_turned"], wy // 2 + 1)
                            src = p_img[:, 4 * wy * POS:(4 * wy + 4) * POS].rearrange("p (w y x) -> p y w x", w=4, y=WIN)
                            dst = y_img[:, WIN * wy:WIN * wy + WIN].rearrange("p y (w x) -> p y w x", w=4)
                            act.activation(dst, src, ACT.Identity, bias=ln_b[:, 0:1], scale=ln_w[:, 0:1]).then_inc(sig["y_scaled"], 1)
        more(nc, io, locals())


def more(nc, io, loc):
    ctx, sig, sb, ps, chain, unchain, Norm = (loc[k] for k in ("ctx", "sig", "sb", "ps", "chain", "unchain", "Norm"))
    x, xn, ident, eps5, eps6, ones64, xn_tok = (loc[k] for k in ("x", "xn", "ident", "eps5", "eps6", "ones64", "xn_tok"))

    def halves():
        return [(h, slice(h * BANK, (h + 1) * BANK)) for h in range(2)]

    def add_half(dve, by_batch, h):
        c = slice(h * BANK, (h + 1) * BANK)
        states = slice(h * BANK + 1, (h + 1) * BANK + 1)
        dve.tensor_copy(xn[C:R, c], by_batch[0:C, states, 1]).then_inc(sig["half_added"], 1)
        dve.tensor_tensor(x[0:C, c], x[0:C, c], by_batch[0:C, states, 0], ALU.add).then_inc(sig["half_added"], 1)
        dve.wait_ge(sig["half_added"], 3 * h + 1)
        dve.tensor_tensor(x[C:R, c], x[C:R, c], xn[C:R, c], ALU.add).then_inc(sig["half_added"], 1)

    def recurrent(tag, swept, use, beside):
        per_use = {"load": 48, "wx": NB}
        s = lambda name: sig["rec_" + name] if name not in ("state", "preact") else sig[tag + name]
        at = lambda name, n: (s(name), use * per_use.get(name, 1) + n)
        with ExitStack() as st:
            yx = sb(tag + "yx", [2 * C, NB * (T + 17)], stack=st)
            by_batch = yx[:].rearrange("p (t b) -> p t b", b=NB)
            w = sb(tag + "w", [R, C], stack=st)
            v = sb(tag + "v", [2 * C, 128], stack=st)
            gb = sb(tag + "gb", [2 * C, 2], stack=st)
            bn = sb(tag + "bn", [2 * C, NB, 2, 6], stack=st)
            mv = sb(tag + "mv", [2 * C, 8], stack=st)
            hi = slice(C, 2 * C)
            with ExitStack() as s2:
                p_a = ps(tag + "p_a", [128, T], stack=s2)
                p_b = ps(tag + "p_b", [R, T], stack=s2)
                p_w = ps(tag + "p_w", [2 * C, NB, T], stack=s2)
                norm = Norm(p_a, p_b, eps5)
                with nc.Block() as block:
                    @block.sync
                    def _(sp):
                        for t, src in ((w, io[tag + "_W"]), (v, io[tag + "_V"]), (gb, io[tag + "_gb"])):
                            sp.dma_start(t[:], src).then_inc(s("load"), 16)
                        beside.load(sp)
                        sp.wait_ge(*at("load", 48))

                    @block.tensor
                    def _(pe):
                        norm.pe(pe)
                        pe.wait_ge(*at("load", 48))
                        norm.wait_out(pe, 1)
                        for b in range(NB):
                            rows = slice(b * C, (b + 1) * C)
                            for h, c in halves():
                                last = pe.matmul(p_w[hi, b, c], w[rows], xn[rows, c], start=True, stop=True)
                            last.then_inc(s("wx"), 1)
                            if swept and b == 0:
                                beside.pe_sum(pe, p_a)
                        if swept:
                            beside.pe_square_sum(pe, p_a)

                    @block.vector
                    def _(dve):
                        link = chain(dve, "dve")
                        norm.dve(dve)
                        if swept:
                            beside.dve_spread(dve, link, p_a)
                        for b in range(NB):
                            dve.wait_ge(*at("wx", b + 1))
                            for h, c in halves():
                                link(dve.bn_stats(bn[hi, b, h], p_w[hi, b, c]))
                        dve.bn_aggr(mv[hi, 0:2], bn[hi].rearrange("p b h s -> p (b h s)")).then_inc(s("stats"), 1)
                        dve.wait_ge(*at("sd", 1))
                        dve.wait_ge(*at("load", 48))
                        link(dve.reciprocal(mv[hi, 5:6], mv[hi, 4:5]))
                        link(dve.tensor_tensor(mv[hi, 5:6], mv[hi, 5:6], gb[hi, 0:1], ALU.mult))
                        link(dve.tensor_tensor(mv[hi, 6:7], mv[hi, 5:6], mv[hi, 0:1], ALU.mult))
                        dve.tensor_tensor(mv[hi, 6:7], gb[hi, 1:2], mv[hi, 6:7], ALU.subtract).then_inc(s("shift"), 1)
                        dve.wait_ge(*at("shift", 1))
                        dve.tensor_scalar(by_batch[hi, 0:T, 1], p_w[hi, 1], mv[hi, 5:6], mv[hi, 6:7], ALU.mult, ALU.add)
                        unchain(link, "dve")

                    @block.scalar
                    def _(act):
                        norm.act(act)
                        act.wait_ge(*at("stats", 1))
                        act.activation(mv[hi, 4:5], mv[hi, 1:2], ACT.Sqrt, bias=eps5[hi, 0:1]).then_inc(s("sd"), 1)
                        if swept:
                            beside.act_root(act, p_a)
                        act.wait_ge(*at("shift", 1))
                        act.activation(by_batch[hi, 0:T, 0], p_w[hi, 0], ACT.Identity, bias=mv[hi, 6:7], scale=mv[hi, 5:6])

                    @block.gpsimd
                    def _(pool):
                        pool.memset(yx[0:C, 0:NB * T], 0.0)

            with ExitStack() as s2:
                p_z = ps(tag + "p_z", [128, 2, BANK], stack=s2)
                if not swept:
                    HALF, ROOTS = T // 2, T // 2 + 24
                    first = beside(s2)
                    with nc.Block() as block:
                        @block.tensor
                        def _(pe):
                            others = first.pe(pe)
                            for t in range(T):
                                if t:
                                    pe.wait_ge(s("state"), t)
                                pe.matmul(p_z[0:C, t % 2, 0:NB], v[:, 0:C], yx[:, NB * t:NB * (t + 1)], start=True, stop=True).then_inc(s("preact"), 1)
                                if t > HALF + 4:
                                    next(others, None)
                            for _ in others:
                                pass

                        @block.scalar
                        def _(act):
                            for t in range(T):
                                act.wait_ge(s("preact"), t + 1)
                                act.activation(yx[0:C, NB * (t + 1):NB * (t + 2)], p_z[0:C, t % 2, 0:NB], ACT.Sigmoid).then_inc(s("state"), 1)
                                if t == ROOTS:
                                    first.roots(act)

                        @block.vector
                        def _(dve):
                            dve.wait_ge(s("state"), HALF)
                            add_half(dve, by_batch, 0)
                            first.dve(dve)

                        @block.gpsimd
                        def _(pool):
                            first.pool(pool)
                    second = beside(s2)
                    with nc.Block() as block:
                        @block.tensor
                        def _(pe):
                            for _ in second.pe(pe):
                                pass

                        @block.scalar
                        def _(act):
                            second.roots(act)
                            second.act(act)

                        @block.vector
                        def _(dve):
                            add_half(dve, by_batch, 1)
                            second.dve(dve)

                        @block.gpsimd
                        def _(pool):
                            second.pool(pool)
                else:
                    p_f = ps(tag + "p_f", [C, BANK], stack=s2)
                    p_g = ps(tag + "p_g", [R, BANK], stack=s2)
                    SEG = 16
                    NSEG = T // SEG
                    SWEEPS = 3
                    UNROLL = 16
                    guess = sb(tag + "guess", [C, NSEG - 1, NB], stack=s2)
                    differ = sb(tag + "differ", [C, NSEG - 1, NB], stack=s2)
                    count = sb(tag + "count", [C, 1], stack=s2)
                    flag = sb(tag + "flag", [1, 1], I32, stack=s2)
                    ends = by_batch[0:C, SEG:T:SEG]

                    def flock(i, f, at):
                        total = NSEG - SWEEPS + 1 + i // SEG
                        first, end = (0, NSEG // 2) if f == 0 else (NSEG // 2, total)
                        return end - first, slice(SEG * first + at, SEG * (end - 1) + at + 1, SEG)

                    with nc.Block() as block:
                        @block.tensor
                        def _(pe):
                            for i in range(SWEEPS * SEG):
                                if i == 2 * SEG - 4:
                                    beside.pe_gram(pe, p_g)
                                for f in range(2):
                                    n, cols = flock(i, f, i % SEG)
                                    if i:
                                        pe.wait_ge(s("state"), 2 * i if i % SEG == 0 else 2 * i - 1 + f)
                                    pe.matmul(p_z[0:C, f, 0:NB * n], v[:, 0:C], by_batch[:, cols], start=True, stop=True).then_inc(s("preact"), 1)
                            pe.wait_ge(s("differ"), 1)
                            pe.matmul(p_f[:, 0:1], ones64[0:C, 0:C], count[:], start=True, stop=True).then_inc(s("differs"), 1)
                            pe.wait_ge(s("flag"), 1)
                            again = pe.value_load(flag[0:1, 0:1], min_val=0, max_val=1)
                            with pe.If(again != 0):
                                with pe.Fori(0, T, UNROLL) as t0:
                                    for u in range(UNROLL):
                                        pe.wait_ge(s("state_again"), t0 + u + 1)
                                        pe.matmul(p_z[:, u % 2, 0:NB], v[:], yx[:, bass.ds(NB * t0 + NB * u, NB)], start=True, stop=True).then_inc(s("preact_again"), 1)

                        @block.scalar
                        def _(act):
                            for i in range(SWEEPS * SEG):
                                for f in range(2):
                                    n, cols = flock(i, f, i % SEG + 1)
                                    act.wait_ge(s("preact"), 2 * i + f + 1)
                                    if i == SWEEPS * SEG - 1:
                                        act.wait_ge(s("guess"), 1)
                                    act.activation(by_batch[0:C, cols], p_z[0:C, f, 0:NB * n].rearrange("p (n b) -> p n b", b=NB), ACT.Sigmoid).then_inc(s("state"), 1)
                                if 4 <= i < 4 + NLEV:
                                    beside.act_sign(act, i - 4)
                            act.wait_ge(s("flag"), 1)
                            again = act.value_load(flag[0:1, 0:1], min_val=0, max_val=1)
                            with act.If(again != 0):
                                with act.Fori(0, T, UNROLL) as t0:
                                    for u in range(UNROLL):
                                        act.wait_ge(s("preact_again"), t0 + u + 1)
                                        act.activation(yx[0:C, bass.ds(NB * t0 + NB * (u + 1), NB)], p_z[0:C, u % 2, 0:NB], ACT.Sigmoid).then_inc(s("state_again"), 1)

                        @block.vector
                        def _(dve):
                            link = chain(dve, "dve")
                            dve.memset(count[:], 0.0).then_inc(s("state_again"), 1)
                            dve.wait_ge(s("state_again"), 1)
                            beside.dve_solve(dve, link, p_g)
                            dve.wait_ge(s("state"), 2 * (SWEEPS - 1) * SEG)
                            dve.tensor_copy(guess[:], ends).then_inc(s("guess"), 1)
                            dve.wait_ge(s("guess"), 1)
                            dve.wait_ge(s("state"), 2 * SWEEPS * SEG)
                            link(dve.tensor_tensor(differ[:], guess[:], ends, ALU.not_equal))
                            dve.tensor_reduce(count[:], differ[:].rearrange("p n b -> p (n b)"), AX_X, ALU.max).then_inc(s("differ"), 1)
                            dve.wait_ge(s("differs"), 1)
                            dve.tensor_scalar(flag[:], p_f[0:1, 0:1], 1.0, None, ALU.min).then_inc(s("flag"), 1)
                            unchain(link, "dve")
            if not swept:
                return
            with nc.Block() as block:
                @block.vector
                def _(dve):
                    dve.tensor_tensor(x[0:C], x[0:C], by_batch[0:C, 1:T + 1, 0], ALU.add)
                    dve.wait_ge(*at("moved", 1))
                    dve.tensor_tensor(x[C:R], x[C:R], xn[C:R], ALU.add)

                @block.scalar
                def _(act):
                    act.activation(xn[C:R], by_batch[0:C, 1:T + 1, 1], ACT.Copy).then_inc(s("moved"), 1)

    with ExitStack() as st:
        NT, K1 = 9, 3
        NPAIRS = 2 * K1
        wf = sb("wf", [R, NT * C], stack=st)
        sc = sb("sc", [R, 3 * NACT], stack=st)
        beta = lambda n: sc[:, n:n + 1]
        shift = lambda n: sc[:, NACT + n:NACT + n + 1]
        junk = sb("junk", [R, NT * C], stack=st)
        lev = sb("lev", [R, NLEV, NT * C], stack=st)
        weff = sb("weff", [R, NT * C], stack=st)
        wc = sb("wc", [128, NPAIRS, R], stack=st)
        pad1 = sb("pad1", [128, SIDE + 2, SIDE + 2], stack=st)
        sm = sb("sm", [R, 16], stack=st)
        gram = sb("gram", [R, NLEV, NLEV + 1], stack=st)
        tmp = sb("tmp", [R, NLEV, NLEV + 1], stack=st)
        row = sb("row", [R, NLEV + 1], stack=st)
        N_ALL = float(NB * C * NT * C)

        class Filter:

            def load(self, sp):
                sp.dma_start(wf[:], io["bin_w"]).then_inc(sig["load_bin"], 16)
                sp.dma_start(sc[:], io["bin_s"]).then_inc(sig["load_bin"], 16)

            def pe_sum(self, pe, p):
                pe.wait_ge(sig["w_sum"], 1)
                pe.matmul(p[0:R, BANK - 1:BANK], ones64[:], sm[:, 0:1], start=True, stop=True).then_inc(sig["w_total"], 1)

            def pe_square_sum(self, pe, p):
                pe.wait_ge(sig["w_sqsum"], 1)
                pe.matmul(p[0:R, T - 1:T], ones64[:], sm[:, 2:3], start=True, stop=True).then_inc(sig["w_sqtotal"], 1)

            def dve_spread(self, dve, link, p):
                dve.wait_ge(sig["load_bin"], 32)
                dve.tensor_reduce(sm[:, 0:1], wf[:], AX_X, ALU.add).then_inc(sig["w_sum"], 1)
                dve.wait_ge(sig["w_total"], 1)
                link(dve.tensor_scalar(sm[:, 1:2], p[0:R, BANK - 1:BANK], 1.0 / N_ALL, None, ALU.mult))
                link(dve.tensor_scalar(weff[:], wf[:], sm[:, 1:2], None, ALU.subtract))
                dve.tensor_tensor_reduce(junk[:], weff[:], weff[:], 1.0, 0.0, ALU.mult, ALU.add, sm[:, 2:3]).then_inc(sig["w_sqsum"], 1)

            def act_root(self, act, p):
                act.wait_ge(sig["w_sqtotal"], 1)
                act.activation(sm[:, 3:4], p[0:R, T - 1:T], ACT.Sqrt, scale=1.0 / N_ALL).then_inc(sig["w_sd"], 1)

            def act_sign(self, act, m):
                act.wait_ge(sig["levels"], 1)
                act.activation(lev[:, m], lev[:, m], ACT.Sign).then_inc(sig["lev_signs"], 1)

            def pe_gram(self, pe, p):
                pe.wait_ge(sig["gram_rows"], 1)
                pe.matmul(p[:, 0:30], ones64[:], gram[:].rearrange("p a b -> p (a b)"), start=True, stop=True).then_inc(sig["gram"], 1)

            def dve_solve(self, dve, link, p):
                dve.wait_ge(sig["w_sd"], 1)
                for m in range(NLEV):
                    link(dve.tensor_scalar(sm[:, 4 + m:5 + m], sm[:, 3:4], -1.0 + 2.0 * m / (NLEV - 1), None, ALU.mult))
                for m in range(NLEV):
                    ins = dve.tensor_scalar(lev[:, m], weff[:], sm[:, 4 + m:5 + m], None, ALU.add)
                ins.then_inc(sig["levels"], 1)
                dve.wait_ge(sig["lev_signs"], NLEV)
                for a in range(NLEV):
                    for b in range(a, NLEV + 1):
                        other = lev[:, b] if b < NLEV else wf[:]
                        link(dve.tensor_tensor_reduce(junk[:], lev[:, a], other, 1.0, 0.0, ALU.mult, ALU.add, gram[:, a, b:b + 1]))
                for a in range(NLEV - 1):
                    ins = dve.tensor_copy(gram[:, a + 1:NLEV, a], gram[:, a, a + 1:NLEV])
                ins.then_inc(sig["gram_rows"], 1)
                dve.wait_ge(sig["gram"], 1)
                link(dve.tensor_scalar(gram[:].rearrange("p a b -> p (a b)"), p[:, 0:30], 0.5, None, ALU.mult))
                for k in range(NLEV):
                    link(dve.reciprocal(sm[:, 10:11], gram[:, k, k:k + 1]))
                    link(dve.tensor_scalar(row[:], gram[:, k], sm[:, 10:11], None, ALU.mult))
                    col = gram[:, :, k:k + 1].broadcast_to([R, NLEV, NLEV + 1])
                    rows = row[:].rearrange("p (a b) -> p a b", a=1).broadcast_to([R, NLEV, NLEV + 1])
                    link(dve.tensor_tensor(tmp[:], col, rows, ALU.mult))
                    link(dve.tensor_tensor(gram[:], gram[:], tmp[:], ALU.subtract))
                    link(dve.tensor_copy(gram[:, k], row[:]))
                for m in range(NLEV):
                    if m == 0:
                        link(dve.tensor_scalar(weff[:], lev[:, 0], gram[:, 0, NLEV:NLEV + 1], None, ALU.mult))
                    else:
                        link(dve.scalar_tensor_tensor(weff[:], lev[:, m], gram[:, m, NLEV:NLEV + 1], weff[:], ALU.mult, ALU.add))
                link(dve.memset(wc[:], 0.0))
                taps = weff[:].rearrange("p (y x c) -> p y x c", y=K1, x=K1)
                for b in range(NB):
                    rr = slice(b * C, (b + 1) * C)
                    dve.tensor_copy(wc[rr, 0:K1, rr], taps[rr, :, 0])
                    dve.tensor_copy(wc[rr, K1:NPAIRS, rr], taps[rr, :, 2])
                    dve.tensor_copy(wc[R + b * C:R + (b + 1) * C, 0:K1, rr], taps[rr, :, 1])
                link(dve.tensor_reduce(sm[:, 11:12], gram[:, :, NLEV], AX_X, ALU.add))
                link(dve.tensor_tensor_reduce(junk[:, 0:NACT], sc[:, 0:NACT], sc[:, 2 * NACT:3 * NACT], 1.0, 0.0, ALU.mult, ALU.add, sm[:, 12:13]))
                link(dve.tensor_tensor(sm[:, 13:14], sm[:, 11:12], sm[:, 12:13], ALU.mult))

        recurrent("L0", True, 0, Filter())

        sg = sb("sg", [R, NACT, T], stack=st)
        p_a = ps("b1p_a", [128, T], stack=st)
        p_b = ps("b1p_b", [R, T], stack=st)
        p_c = ps("b1p_c", [R, T], stack=st)
        norm = Norm(p_a, p_b, eps6)
        inner = pad1[0:R, 1:1 + SIDE, 1:1 + SIDE]
        further = pad1[R:2 * R, 1:1 + SIDE, 0:SIDE]
        img = lambda t: t.rearrange("p (y x) -> p y x", x=SIDE)
        with nc.Block() as block:
            @block.gpsimd
            def _(pool):
                pool.memset(pad1[:], 0.0).then_inc(sig["bin_zero"], 1)

            @block.tensor
            def _(pe):
                norm.pe(pe)
                pe.wait_ge(sig["acts"], 1)
                pe.wait_ge(sig["acts_further"], 1)
                for h, c in halves():
                    for k in range(NPAIRS):
                        y0 = 16 * h + k % K1
                        x0 = 0 if k < K1 else 2
                        last = pe.matmul(p_c[:, c], wc[:, k], pad1[:, y0:y0 + 16, x0:x0 + SIDE], start=(k == 0), stop=(k == NPAIRS - 1))
                    last.then_inc(sig["bin_conv"], 1)

            @block.scalar
            def _(act):
                norm.act(act)
                for n in range(NACT):
                    act.wait_ge(sig["act_in"], n + 1)
                    act.activation(sg[:, n], sg[:, n], ACT.Sign).then_inc(sig["act_sign"], 1)
                act.wait_ge(sig["acts"], 1)
                act.copy(further, inner).then_inc(sig["acts_further"], 1)

            @block.vector
            def _(dve):
                link = chain(dve, "dve")
                norm.dve(dve)
                norm.wait_out(dve)
                for n in range(NACT):
                    dve.tensor_scalar(sg[:, n], xn[:], shift(n), -0.5, ALU.add, ALU.add).then_inc(sig["act_in"], 1)
                dve.wait_ge(sig["bin_zero"], 1)
                for n in range(NACT):
                    dve.wait_ge(sig["act_sign"], n + 1)
                    if n == 0:
                        link(dve.tensor_scalar(inner, img(sg[:, 0]), beta(0), None, ALU.mult))
                    else:
                        ins = dve.scalar_tensor_tensor(inner, img(sg[:, n]), beta(n), inner, ALU.mult, ALU.add)
                        if n < NACT - 1:
                            link(ins)
                ins.then_inc(sig["acts"], 1)
                for h, c in halves():
                    dve.wait_ge(sig["bin_conv"], h + 1)
                    dve.scalar_tensor_tensor(x[:, c], p_c[:, c], sm[:, 13:14], x[:, c], ALU.add, ALU.add)
                unchain(link, "dve")

    def experts(tag, use):
        per_use = {"load": 112, "logits": 2, "biased_logits": 2, "spread": 2}
        s = lambda name: sig["moe_" + name]
        at = lambda name, n: (s(name), use * per_use.get(name, 1) + n)
        G = NB * E
        NTG = T // 128
        with ExitStack() as st:
            gate = sb(tag + "gate", [R, G], stack=st)
            gate_b = sb(tag + "gate_b", [G, 1], stack=st)
            TRIOS = (E + 2) // 3
            w1 = sb(tag + "w1", [3 * C + 3, TRIOS, HID], stack=st)
            w2 = sb(tag + "w2", [HID, E, C], stack=st)
            b2 = sb(tag + "b2", [C, E], stack=st)
            own = sb(tag + "own", [G, NB], stack=st)
            lg = sb(tag + "lg", [G, T], stack=st)
            pr = sb(tag + "pr", [G, T], stack=st)
            left = sb(tag + "left", [G, T], stack=st)
            wt = sb(tag + "wt", [G, T], stack=st)
            top = sb(tag + "top", [G, 8], stack=st)
            small = sb(tag + "small", [G, 4], stack=st)
            wt_tok = sb(tag + "wt_tok", [128, NTG, G], stack=st)
            pooled = sb(tag + "pooled", [3 * C + 3, TRIOS, 3 * NB], stack=st)
            hid = sb(tag + "hid", [HID, G], stack=st)
            outs = sb(tag + "outs", [C, NB, E], stack=st)
            outb = sb(tag + "outb", [G, NB, C], stack=st)
            p_a = ps(tag + "p_a", [128, T], stack=st)
            p_b = ps(tag + "p_b", [R, T], stack=st)
            p_l2 = ps(tag + "p_l", [R, T], stack=st)
            p_l = p_l2[0:G]
            p_t = ps(tag + "p_t", [128, 2, BANK], stack=st)
            norm = Norm(p_a, p_b, eps5)
            p_pool, p_e, p_r = p_a[0:R, 0:G], p_b[0:C, BANK:BANK + G], p_a[0:G, BANK:BANK + C]
            p_x = p_l2
            with nc.Block() as block:
                @block.sync
                def _(sp):
                    for t, n in ((gate, tag + "_gate"), (gate_b, tag + "_gate_b"), (w1, tag + "_w1"), (w2, tag + "_w2"), (b2, tag + "_b2"), (own, "own")):
                        sp.dma_start(t[:], io[n]).then_inc(s("load"), 16)
                    sp.dma_start(pooled[3 * C:], io["own_one"]).then_inc(s("load"), 16)
                    sp.wait_ge(*at("load", 112))

                @block.gpsimd
                def _(pool):
                    pool.memset(pooled[0:3 * C], 0.0).then_inc(s("zeros"), 1)

                @block.tensor
                def _(pe):
                    norm.pe(pe)
                    pe.wait_ge(*at("load", 112))
                    for h, c in halves():
                        norm.wait_out(pe, h)
                        pe.matmul(p_l[:, c], gate[:], xn[:, c], start=True, stop=True).then_inc(s("logits"), 1)
                    pe.wait_ge(*at("weights", 1))
                    for j in range(NTG):
                        last = pe.transpose(p_t[:, 1, j * G:(j + 1) * G], wt[:, j * 128:(j + 1) * 128], ident[0:G, 0:G])
                    last.then_inc(s("w_turned"), 1)
                    pe.wait_ge(*at("w_tok", 1))
                    for j in range(NTG):
                        last = pe.matmul(p_pool, xn_tok[:, j], wt_tok[:, j], start=(j == 0), stop=(j == NTG - 1))
                    last.then_inc(s("pooled"), 1)
                    pe.wait_ge(*at("pool_read", 1))
                    for t in range(TRIOS):
                        last = pe.matmul(p_t[:, 0, 6 * t:6 * t + 6], w1[:, t], pooled[:, t], start=True, stop=True)
                    last.then_inc(s("hidden"), 1)
                    pe.wait_ge(*at("gelu", 1))
                    for e in range(E):
                        last = pe.matmul(p_e[:, 2 * e:2 * e + 2], w2[:, e], hid[:, 2 * e:2 * e + 2], start=True, stop=True)
                    last.then_inc(s("expert_out"), 1)
                    pe.wait_ge(*at("biased", 1))
                    pe.transpose(p_r, outs[:].rearrange("p b e -> p (b e)"), ident[0:C, 0:C]).then_inc(s("out_turned"), 1)
                    pe.wait_ge(*at("outb", 1))
                    for h, c in halves():
                        pe.matmul(p_x[:, c], outb[:].rearrange("p b c -> p (b c)"), wt[:, c], start=True, stop=True).then_inc(s("spread"), 1)

                @block.scalar
                def _(act):
                    norm.act(act)
                    act.wait_ge(*at("load", 112))
                    for h, c in halves():
                        act.wait_ge(*at("logits", h + 1))
                        act.activation(lg[:, c], p_l[:, c], ACT.Identity, bias=gate_b[:, 0:1]).then_inc(s("biased_logits"), 1)
                    act.wait_ge(*at("neg_max", 1))
                    act.activation(pr[:], lg[:], ACT.Exp, bias=small[:, 0:1], accum_out=small[:, 1:2]).then_inc(s("exp"), 1)
                    act.wait_ge(*at("hidden", 1))
                    act.activation(hid[:], p_t[:, 0, 0:G], ACT.Gelu).then_inc(s("gelu"), 1)

                @block.vector
                def _(dve):
                    link = chain(dve, "dve")
                    norm.dve(dve)
                    dve.wait_ge(*at("biased_logits", 2))
                    link(dve.max(top[:], lg[:]))
                    dve.tensor_scalar(small[:, 0:1], top[:, 0:1], -1.0, None, ALU.mult).then_inc(s("neg_max"), 1)
                    link(dve.match_replace(left[:], top[:], lg[:], MARK))
                    dve.wait_ge(*at("exp", 1))
                    link(dve.reciprocal(small[:, 2:3], small[:, 1:2]))
                    link(dve.scalar_tensor_tensor(wt[:], left[:], MARK, pr[:], ALU.is_equal, ALU.mult))
                    dve.tensor_scalar(wt[:], wt[:], small[:, 2:3], None, ALU.mult).then_inc(s("weights"), 1)
                    dve.wait_ge(*at("w_turned", 1))
                    dve.tensor_copy(wt_tok[:].rearrange("p j r -> p (j r)"), p_t[:, 1, 0:NTG * G]).then_inc(s("w_tok"), 1)
                    dve.wait_ge(*at("pooled", 1))
                    dve.wait_ge(*at("zeros", 1))
                    for b in range(NB):
                        for k in range(3):
                            n = (E - k + 2) // 3
                            ins = dve.tensor_copy(pooled[k * C:(k + 1) * C, 0:n, 2 * k + b], p_pool[b * C:(b + 1) * C, b * E + k:b * E + k + 3 * (n - 1) + 1:3])
                    ins.then_inc(s("pool_read"), 1)
                    dve.wait_ge(*at("expert_out", 1))
                    dve.wait_ge(*at("load", 112))
                    dve.tensor_tensor(outs[:], p_e.rearrange("p (e b) -> p b e", b=NB),
                                      b2[:].rearrange("p (a e) -> p a e", a=1).broadcast_to([C, NB, E]), ALU.add).then_inc(s("biased"), 1)
                    dve.wait_ge(*at("out_turned", 1))
                    for b in range(NB):
                        ins = dve.tensor_scalar(outb[:, b], p_r, own[:, b:b + 1], None, ALU.mult)
                    ins.then_inc(s("outb"), 1)
                    for h, c in halves():
                        dve.wait_ge(*at("spread", h + 1))
                        dve.tensor_tensor(x[:, c], x[:, c], p_x[:, c], ALU.add)
                    unchain(link, "dve")

    experts("L1", 0)

    with ExitStack() as st:
        ew = sb("ew", [R, NBASIS, R], stack=st)
        eb = sb("eb", [R, 2], stack=st)
        sr = sb("sr", [R, SIDE], stack=st)
        scl = sb("scl", [R, SIDE], stack=st)
        dg = sb("dg", [R, SIDE], stack=st)
        tot = sb("tot", [R, 2], stack=st)
        rc = sb("rc", [R, 3, SIDE], stack=st)
        acc = sb("eacc", [R, SIDE, SIDE], stack=st)
        low = sb("elow", [R, SIDE, SIDE], stack=st)
        p_a = ps("e2p_a", [128, T], stack=st)
        p_b = ps("e2p_b", [R, T], stack=st)
        p_c = ps("e2p_c", [R, T], stack=st)
        p_r = ps("e2p_r", [R, 2, BANK], stack=st)
        norm = Norm(p_a, p_b, eps6)
        xi = xn[:].rearrange("p (i j) -> p i j", j=SIDE)
        with nc.Block() as block:
            @block.sync
            def _(sp):
                sp.dma_start(ew[:], io["eq_w"]).then_inc(sig["load_eq"], 16)
                sp.dma_start(eb[:], io["eq_b"]).then_inc(sig["load_eq"], 16)
                sp.wait_ge(sig["load_eq"], 32)

            @block.tensor
            def _(pe):
                norm.pe(pe)
                pe.wait_ge(sig["load_eq"], 32)
                norm.wait_out(pe)
                turned = xn[:].rearrange("p (i j) -> p j i", j=SIDE)
                for h, c in halves():
                    pe.matmul(p_c[:, c], ew[:, 9], xn[:, c], start=True, stop=False)
                    pe.matmul(p_c[:, c], ew[:, 10], turned[:, 16 * h:16 * h + 16], start=False, stop=True).then_inc(sig["eq_full"], 1)
                pe.wait_ge(sig["eq_sums"], 1)
                sd = tot[:, 0:1].broadcast_to([R, SIDE])
                sa = tot[:, 1:2].broadcast_to([R, SIDE])
                groups = [[(8, sr[:]), (7, scl[:]), (11, dg[:]), (13, sd), (14, sa)],
                          [(5, scl[:]), (6, sr[:]), (12, dg[:])],
                          [(0, dg[:]), (1, sd), (2, sr[:]), (3, scl[:]), (4, sa)]]
                for g, terms in enumerate(groups):
                    for n, (k, src) in enumerate(terms):
                        last = pe.matmul(p_r[:, g % 2, (g // 2) * SIDE:(g // 2) * SIDE + SIDE], ew[:, k], src, start=(n == 0), stop=(n == len(terms) - 1))
                    last.then_inc(sig["eq_lines"], 1)

            @block.scalar
            def _(act):
                norm.act(act)

            @block.vector
            def _(dve):
                link = chain(dve, "dve")
                norm.dve(dve)
                norm.wait_out(dve)
                dve.tensor_reduce(scl[:], xn[:].rearrange("p (i j) -> p j i", j=SIDE), AX_X, ALU.add)
                link(dve.tensor_reduce(sr[:], xi, AX_X, ALU.add))
                link(dve.tensor_copy(dg[:], xn[:, 0:T:SIDE + 1]))
                link(dve.tensor_reduce(tot[:, 0:1], dg[:], AX_X, ALU.add))
                dve.tensor_reduce(tot[:, 1:2], sr[:], AX_X, ALU.add).then_inc(sig["eq_sums"], 1)
                dve.wait_ge(sig["eq_lines"], 3)
                dve.wait_ge(sig["load_eq"], 32)
                link(dve.tensor_scalar(rc[:, 0], p_r[:, 0, 0:SIDE], eb[:, 0:1], None, ALU.add))
                link(dve.tensor_copy(rc[:, 1], p_r[:, 1, 0:SIDE]))
                link(dve.tensor_scalar(rc[:, 2], p_r[:, 0, SIDE:2 * SIDE], eb[:, 1:2], None, ALU.add))
                dve.wait_ge(sig["eq_full"], 2)
                along = rc[:, 0].rearrange("p (i a) -> p i a", a=1).broadcast_to([R, SIDE, SIDE])
                down = rc[:, 1].rearrange("p (a j) -> p a j", a=1).broadcast_to([R, SIDE, SIDE])
                link(dve.tensor_tensor(acc[:], p_c[:].rearrange("p (i j) -> p i j", j=SIDE), along, ALU.add))
                link(dve.tensor_tensor(acc[:], acc[:], down, ALU.add))
                diag = acc[:].rearrange("p i j -> p (i j)")[:, 0:T:SIDE + 1]
                link(dve.tensor_tensor(diag, diag, rc[:, 2], ALU.add))
                link(dve.scalar_tensor_tensor(low[:], acc[:], 0.01, acc[:], ALU.mult, ALU.max))
                dve.tensor_tensor(x[:], x[:], low[:].rearrange("p i j -> p (i j)"), ALU.add)
                unchain(link, "dve")

    with ExitStack() as st:
        NTG = T // 128
        HEADS = 2
        HC = C // 4 // HEADS
        JC = NB * HEADS * HC
        W1, W3 = (SIDE // 8) ** 2, (SIDE // 16) ** 2
        WITHIN = {2: 0, 0: 1}
        aq = sb("aq", [R, 2, 128], stack=st)
        ak = sb("ak", [R, 2, 128], stack=st)
        av = sb("av", [R, 2, JC], stack=st)
        ae1 = sb("ae1", [R, NB, 3 * HEADS * HC], stack=st)
        ae3 = sb("ae3", [R, NB * 3 * HEADS * HC], stack=st)
        ao = sb("ao", [128, 2, BANK], stack=st)
        aow = sb("aow", [128, 2, R], stack=st)
        abo = sb("abo", [R, 1], stack=st)
        pos1 = sb("pos1", [128, 2, 128], stack=st)
        pos3 = sb("pos3", [128, 2, 2, 256], stack=st)
        pos2 = sb("pos2", [128, HEADS * W1 * W1], stack=st)
        pos4 = sb("pos4", [128, HEADS * W3 * W3], stack=st)
        EC = 3 * BANK // 4
        xo = sb("xo", [R, 4, T], stack=st)
        q = sb("q", [128, 2, NB * HEADS, T], stack=st)
        kk = sb("kk", [128, 2, T], stack=st)
        vv = sb("vv", [128, 2, NTG, NB * HEADS, 32], stack=st)
        units = [(g, j, range(t, t + n)) for h, quarters in ((0, (2, 0)), (1, (0, 2))) for g in quarters for n in (2 if g == 2 else 4,)
                 for t in range(4 * h, 4 * h + 4, n) for j in range(4)]
        NU, EARLY = len(units), len(units) // 2
        scored = sb("scored", [128, EARLY, BANK], stack=st)
        mx = sb("amx", [128, NU, 4], stack=st)
        nmx = sb("anmx", [128, NU, 4], stack=st)
        den = sb("aden", [128, NU, 4], stack=st)
        rden = sb("arden", [128, NU, 4], stack=st)
        e1 = sb("e1", [128, W1, 3, HEADS, HC], stack=st)
        e3 = sb("e3", [128, 2, W3, NB, 3, HEADS, HC], stack=st)

        def arranged(g, whole, image, half):
            side = 8 if g < 2 else 16
            n = SIDE // side
            src = image.rearrange("p (u y v x) -> p u y v x", u=n, y=side, v=n)
            for u in range(half * n // 2, (half + 1) * n // 2):
                if g % 2 == 0:
                    dst = whole.rearrange("p (u v y x) -> p u v y x", u=n, v=n, y=side)[:, u]
                    yield dst, src[:, u].rearrange("p y v x -> p v y x")
                else:
                    dst = whole.rearrange("p (y x u v) -> p u y x v", u=n, v=n, y=side)[:, u]
                    yield dst, src[:, u].rearrange("p y v x -> p y x v")

        def entries(u):
            g, j, ts = units[u]
            nk = BANK // len(ts)
            for e, t in enumerate(ts):
                yield e, t, nk, slice(e * nk, (e + 1) * nk)

        def score(pe, dst, u, e, t, part, width):
            g, j, _ = units[u]
            nk = BANK // len(units[u][2])
            k0 = (t * 128 if nk == 128 else (t // 2) * 256) + part * width
            c = e * nk + part * width
            return pe.matmul(dst[:, c:c + width], q[:, WITHIN[g], j, t * 128:(t + 1) * 128], kk[:, WITHIN[g], k0:k0 + width], start=True, stop=True)

        def biased(dve, src, i):
            g, j, ts = units[i]
            h = j % 2
            dve.wait_ge(sig["at_scores"], i + 1)
            if i >= EARLY:
                dve.wait_ge(sig["at_turned"], i - EARLY + 1)
            for e, t, nk, c in entries(i):
                bias = pos3[:, t % 2, h] if g == 2 else pos1[:, h]
                last = dve.tensor_tensor_reduce(scored[:, i % EARLY, c], src[:, c], bias, 1.0, -3e38, ALU.add, ALU.max, mx[:, i, e:e + 1])
            last.then_inc(sig["at_max"], 1)
            dve.wait_ge(sig["at_max"], i + 1)
            n = len(ts)
            dve.tensor_scalar(nmx[:, i, 0:n], mx[:, i, 0:n], -1.0, None, ALU.mult).then_inc(sig["at_nmax"], 1)

        def exponentials(act, i):
            g, j, _ = units[i]
            act.wait_ge(sig["at_nmax"], i + 1)
            for e, t, nk, c in entries(i):
                row = scored[:, i % EARLY, c]
                last = act.activation(row, row, ACT.Exp, bias=nmx[:, i, e:e + 1], accum_out=den[:, i, e:e + 1])
            last.then_inc(sig["at_exp"], 1)

        def normalised(dve, i):
            dve.wait_ge(sig["at_exp"], i + 1)
            n = len(units[i][2])
            dve.reciprocal(rden[:, i, 0:n], den[:, i, 0:n]).then_inc(sig["at_rden"], 1)
            dve.wait_ge(sig["at_rden"], i + 1)
            for e, t, nk, c in entries(i):
                row = scored[:, i % EARLY, c]
                last = dve.tensor_scalar(row, row, rden[:, i, e:e + 1], None, ALU.mult)
            last.then_inc(sig["at_probs"], 1)

        class Front:
            made = 0

            @staticmethod
            def load(sp):
                loads = [(aq, "at_q"), (ak, "at_k"), (av, "at_v"), (ae1, "at_e1"), (ae3, "at_e3"), (pos1, "pos1"), (pos2, "pos2"),
                         (pos3, "pos3"), (pos4, "pos4"), (abo, "at_bo"), (ao, "at_o"), (aow, "at_ow")]
                for t, n in loads:
                    sp.dma_start(t[:], io[n]).then_inc(sig["load_at"], 16)

            def __init__(self, stack):
                self.half = h = Front.made
                Front.made += 1
                if h == 0:
                    Front.banks = [ps("atp_tok", [128, BANK], stack=stack), ps("atp_back", [R, BANK], stack=stack),
                                   ps("atp_q", [128, 2, BANK], stack=stack), ps("atp_e", [128, 2, BANK], stack=stack)]
                p_tok, p_back, self.p_q, self.p_e = Front.banks
                self.norm = Norm(p_tok, p_back, eps6, apart=True, k=None if h == 0 else Front.k)
                Front.k = self.norm.k

            def pe(self, pe):
                half, norm, p_q, p_e = self.half, self.norm, self.p_q, self.p_e
                width = BANK if half else 32
                pe.wait_ge(sig["half_added"], 3 * half + 3)
                for j in range(4):
                    norm.turn(pe, half, j)
                    yield
                for _ in range(28):
                    yield
                for j in range(4):
                    norm.turn_back(pe, half, j)
                    yield
                for _ in range(20):
                    yield
                pe.wait_ge(sig["load_at"], 16 * 12)
                made = 4 * half
                for g in (2, 0):
                    pe.wait_ge(sig[f"arranged{g}"], half + 1)
                    for m, wgt in enumerate((aq, ak)):
                        if made >= 2:
                            pe.wait_ge(sig["qk_read"], made - 1)
                        if half and g == 2:
                            pe.wait_ge(sig["at_max"], EARLY)
                        for c in range(0, BANK, width):
                            ins = pe.matmul(p_q[:, m, c:c + width], wgt[:, WITHIN[g]], xo[:, g, half * BANK + c:half * BANK + c + width],
                                            start=True, stop=True)
                            if c + width == BANK:
                                ins.then_inc(sig["qk_made"], 1)
                            yield
                        made += 1
                        for _ in range(8):
                            yield
                for slot, g in enumerate((2, 0)):
                    for t in range(4 * half, 4 * half + 4):
                        pe.matmul(p_e[:, slot, EC + t * JC:EC + (t + 1) * JC], xo[:, g, t * 128:(t + 1) * 128], av[:, slot], start=True, stop=True)
                        yield
                pe.wait_ge(sig["arranged3"], half + 1)
                cols = NB * 3 * HEADS * HC
                for f in range(2):
                    for w in range(2 * half, 2 * half + 2):
                        n = f * W3 + w
                        start = f * 128 * W3 + w
                        last = pe.matmul(p_e[:, 0, n * cols:(n + 1) * cols], xo[:, 3, start:start + 127 * W3 + 1:W3], ae3[:], start=True, stop=True)
                        if (f, w) == (1, 2 * half + 1):
                            last.then_inc(sig["e_made"], 1)
                        yield
                pe.wait_ge(sig["arranged1"], half + 1)
                cols = 3 * HEADS * HC
                for w in range(8 * half, 8 * half + 8):
                    for b in range(NB):
                        last = pe.matmul(p_e[b * 64:(b + 1) * 64, 1, w * cols:(w + 1) * cols], xo[:, 1, w:w + 63 * W1 + 1:W1], ae1[:, b], start=True, stop=True)
                        if (w, b) == (8 * half + 7, 1):
                            last.then_inc(sig["e_made"], 1)
                        yield
                if half == 0:
                    pe.wait_ge(sig["qk_read"], 4)
                    for u in range(EARLY):
                        if u >= 2:
                            pe.wait_ge(sig["at_max"], u - 1)
                        for n in range(BANK // width):
                            e, part = divmod(n, BANK // width // len(units[u][2]))
                            ins = score(pe, p_q[:, u % 2], u, e, units[u][2][e], part, width)
                            if n == BANK // width - 1:
                                ins.then_inc(sig["at_scores"], 1)
                            yield

            def roots(self, act):
                self.norm.act_roots(act, self.half)

            def act(self, act):
                for i in range(EARLY):
                    exponentials(act, i)

            def pool(self, pool):
                if self.half == 0:
                    pool.memset(q[:], 0.0).then_inc(sig["at_zero"], 1)
                    pool.memset(vv[:], 0.0).then_inc(sig["at_zero"], 1)
                self.norm.wait_out(pool, self.half)
                for g in (0, 3):
                    for dst, src in arranged(g, xo[:, g], xn[:], self.half):
                        last = pool.tensor_copy(dst, src)
                    last.then_inc(sig[f"arranged{g}"], 1)

            def dve(self, dve):
                half, p_q, p_e = self.half, self.p_q, self.p_e
                self.norm.dve(dve, (half,))
                self.norm.wait_out(dve, half)
                for g in (2, 1):
                    for dst, src in arranged(g, xo[:, g], xn[:], half):
                        last = dve.tensor_copy(dst, src)
                    last.then_inc(sig[f"arranged{g}"], 1)
                c = slice(half * BANK, (half + 1) * BANK)
                n = 4 * half
                for g in (2, 0):
                    dve.wait_ge(sig["qk_made"], n + 1)
                    dve.wait_ge(sig["at_zero"], 2)
                    for j in range(NB * HEADS):
                        rr = slice(32 * j, 32 * (j + 1))
                        last = dve.tensor_scalar(q[rr, WITHIN[g], j, c], p_q[rr, 0], HC_SCALE, None, ALU.mult)
                    last.then_inc(sig["qk_read"], 1)
                    dve.wait_ge(sig["qk_made"], n + 2)
                    dve.tensor_copy(kk[:, WITHIN[g], c], p_q[:, 1]).then_inc(sig["qk_read"], 1)
                    n += 2
                    if half:
                        for u in range(0, EARLY // 2) if g == 2 else range(EARLY // 2, EARLY):
                            normalised(dve, u)
                groups, own = slice(4 * half, 4 * half + 4), slice(EC + 4 * half * JC, EC + (4 * half + 4) * JC)
                dve.wait_ge(sig["e_made"], 2 * half + 1)
                dve.tensor_copy(vv[:, 0, groups, :, 0:HC].rearrange("p t j c -> p (t j) c"), p_e[:, 0, own].rearrange("p (n c) -> p n c", c=HC))
                w = slice(2 * half, 2 * half + 2)
                dve.tensor_copy(e3[:, :, w].rearrange("p f w b n h c -> p f (w b n h c)"),
                                p_e[:, 0, 0:EC].rearrange("p (f w n) -> p f w n", f=2, w=W3)[:, :, w].rearrange("p f w n -> p f (w n)"))
                dve.wait_ge(sig["e_made"], 2 * half + 2)
                dve.tensor_copy(vv[:, 1, groups, :, 0:HC].rearrange("p t j c -> p (t j) c"), p_e[:, 1, own].rearrange("p (n c) -> p n c", c=HC))
                w = slice(8 * half, 8 * half + 8)
                dve.tensor_copy(e1[:, w].rearrange("p w n h c -> p (w n h c)"),
                                p_e[:, 1, 0:EC].rearrange("p (w n) -> p w n", w=W1)[:, w].rearrange("p w n -> p (w n)"))
                if half == 0:
                    for u in range(EARLY):
                        biased(dve, p_q[:, u % 2], u)

        recurrent("L2", False, 1, Front)

        with ExitStack() as s2:
            RUNS = ((2, 0, 0, 8), (0, 0, 8, 12), (0, 1, 12, 16), (2, 1, 16, 24))
            run_of = {u: k for k, r in enumerate(RUNS) for u in range(r[2], r[3])}
            EXP3, EXP1, FINISH3, FINISH1, TURN_OUT = 6, 11, EARLY + 3, EARLY + 6, 20
            COPY = {EARLY: 0, EARLY + 4: 1, EARLY + 8: 2}
            p_s = ps("atp_s", [128, 2, BANK], stack=s2)
            p_t = ps("atp_t", [128, 2, BANK], stack=s2)
            p_o = ps("atp_o", [128, 2, BANK], stack=s2)
            p_x = ps("atp_x", [128, T], stack=s2)
            p_turned = p_x[:, BANK:BANK + 256].rearrange("p (g n) -> p g n", g=2)
            pt = sb("apt", [128, 2, BANK], stack=s2)
            og = sb("og", [128, 2, T], stack=s2)
            o_tok = sb("ato_tok", [128, 2, 128], stack=s2)
            o_chan = sb("ato_chan", [128, 2, 128], stack=s2)
            prod1 = sb("prod1", [128, HEADS, W1 * W1 * HC], stack=s2)
            pv1 = sb("pv1", [128, HEADS, W1 * W1 * HC], stack=s2)
            sc1 = sb("sc1", [128, HEADS * W1, W1], stack=s2)
            st1 = sb("st1", [128, 3, HEADS * W1], stack=s2)
            NC3 = 2 * NB * HEADS
            prod3 = sb("prod3", [128, NC3, W3 * W3 * HC], stack=s2)
            pv3 = sb("pv3", [128, NC3, W3 * W3 * HC], stack=s2)
            sc3 = sb("sc3", [128, NC3 * W3, W3], stack=s2)
            st3 = sb("st3", [128, 3, NC3 * W3], stack=s2)
            with nc.Block() as block:
                @block.tensor
                def _(pe):
                    def mix_across():
                        pe.wait_ge(sig["at_chan"], 1)
                        image = p_x[0:R].rearrange("p (u y v x) -> p u v y x", y=16, x=16, v=2)
                        for t in range(NTG):
                            dst = image[:, t % 4 // 2, t % 2, 8 * (t // 4):8 * (t // 4) + 8]
                            pe.matmul(dst, ao[:, 0, t * R:(t + 1) * R], o_chan[:, 0], start=(t in (0, 2)), stop=False)
                            if t % 4 == 3:
                                yield
                        image = p_x[0:R].rearrange("p (u y v x) -> p u v y x", y=8, x=8, v=4)
                        for w in range(W1):
                            for b in range(NB):
                                pe.matmul(image[b * C:(b + 1) * C, w // 4, w % 4], ao[:, 1, w * C:(w + 1) * C], o_chan[:, 1, b * 64:(b + 1) * 64],
                                          start=False, stop=False)
                            if w % 4 == 3:
                                yield

                    def mix_run(k):
                        g, half, _, _ = RUNS[k]
                        pe.wait_ge(sig["at_og"], k + 1)
                        c = slice(half * BANK, (half + 1) * BANK)
                        pe.matmul(p_x[0:R, c], aow[:, WITHIN[g]], og[:, WITHIN[g], c], start=False, stop=(k % 2 == 1)).then_inc(sig["at_mixed"], 1)

                    across = mix_across()
                    for i in range(2, NU + 3):
                        if EARLY <= i < NU:
                            if i >= EARLY + 2:
                                pe.wait_ge(sig["at_max"], i - 1)
                            for e, t, nk, c in entries(i):
                                last = score(pe, p_s[:, i % 2], i, e, t, 0, nk)
                            last.then_inc(sig["at_scores"], 1)
                        if i < NU + 2:
                            u = i - 2
                            pe.wait_ge(sig["at_probs"], u + 1)
                            if u >= 2:
                                pe.wait_ge(sig["at_pt"], u - 1)
                            for n in range(4):
                                last = pe.transpose(p_t[:, u % 2, n * 128:(n + 1) * 128], scored[:, u % EARLY, n * 128:(n + 1) * 128], ident[:])
                            last.then_inc(sig["at_turned"], 1)
                        if i >= 3:
                            u = i - 3
                            g, j, _ = units[u]
                            k = run_of[u]
                            if u == RUNS[k][2] and k >= 2:
                                pe.wait_ge(sig["at_og"], k - 1)
                            pe.wait_ge(sig["at_pt"], u + 1)
                            for e, t, nk, c in entries(u):
                                nkb = nk // 128
                                for kb in range(nkb):
                                    kt = t if nkb == 1 else (t // 2) * 2 + kb
                                    last = pe.matmul(p_o[32 * j:32 * j + 32, k % 2, t % 4 * 128:(t % 4 + 1) * 128], vv[:, WITHIN[g], kt, j],
                                                     pt[:, u % 2, c.start + kb * 128:c.start + (kb + 1) * 128], start=(kb == 0), stop=(kb == nkb - 1))
                            last.then_inc(sig["at_out"], 1)
                        if i == TURN_OUT:
                            pe.wait_ge(sig["at_norm"], 2)
                            for n in range(2):
                                last = pe.transpose(p_turned[:, n], o_tok[:, n], ident[:])
                            last.then_inc(sig["at_turned_out"], 1)
                        if i > TURN_OUT:
                            next(across, None)
                    for k in range(len(RUNS)):
                        mix_run(k)

                @block.vector
                def _(dve):
                    link = chain(dve, "dve")

                    def scores(dst, stat, prod, pos_, scale, nth, lead):
                        rows, keys = dst.shape[1], dst.shape[2]
                        flat = dst[:].rearrange("p r k -> p (r k)")
                        dve.wait_ge(sig["at_prod"], nth)
                        link(dve.tensor_reduce(flat, prod[:].rearrange("p n (m c) -> p (n m) c", c=HC), AX_X, ALU.add))
                        folded = flat.rearrange("p (a m) -> p a m", a=lead)
                        bias = pos_[:].rearrange("p (a m) -> p a m", a=1).broadcast_to([128, lead, pos_.shape[1]])
                        link(dve.scalar_tensor_tensor(folded, folded, scale, bias, ALU.mult, ALU.add))
                        link(dve.tensor_reduce(stat[:, 0], dst[:], AX_X, ALU.max))
                        dve.tensor_tensor(dst[:], dst[:], stat[:, 0].rearrange("p (r a) -> p r a", a=1).broadcast_to([128, rows, keys]),
                                          ALU.subtract).then_inc(sig["at_shifted"], 1)

                    def sums(src, stat, nth):
                        dve.wait_ge(sig["at_exp_across"], nth)
                        link(dve.tensor_reduce(stat[:, 1], src[:], AX_X, ALU.add))
                        link(dve.reciprocal(stat[:, 2], stat[:, 1]))

                    def finish3():
                        sums(sc3, st3, 1)
                        dve.wait_ge(sig["at_prod"], 3)
                        link(dve.tensor_reduce(prod3[:].rearrange("p n m -> p (n m)")[:, 0:NC3 * W3 * HC], pv3[:].rearrange("p n (m j) -> p (n m) j", j=W3), AX_X, ALU.add))
                        made = prod3[:].rearrange("p n m -> p (n m)")[:, 0:NC3 * W3 * HC].rearrange("p (f x w c) -> p f x w c", f=2, w=W3, c=HC)
                        over = st3[:, 2].rearrange("p (f x w a) -> p f x w a", f=2, w=W3, a=1)
                        dst = o_tok[:, 0].rearrange("p (f w x c) -> p f x w c", f=2, w=W3, c=HC)
                        for f in range(2):
                            last = dve.tensor_tensor(dst[:, f], made[:, f], over[:, f].broadcast_to([128, NB * HEADS, W3, HC]), ALU.mult)
                        last.then_inc(sig["at_norm"], 1)

                    def finish1():
                        sums(sc1, st1, 2)
                        dve.wait_ge(sig["at_prod"], 4)
                        flat = prod1[:].rearrange("p n m -> p (n m)")[:, 0:HEADS * W1 * HC]
                        link(dve.tensor_reduce(flat, pv1[:].rearrange("p n (m j) -> p (n m) j", j=W1), AX_X, ALU.add))
                        made = flat.rearrange("p (h w c) -> p h w c", h=HEADS, w=W1)
                        over = st1[:, 2].rearrange("p (h w a) -> p h w a", h=HEADS, a=1)
                        dst = o_tok[:, 1].rearrange("p (w h c) -> p h w c", w=W1, h=HEADS)
                        dve.tensor_tensor(dst, made, over.broadcast_to([128, HEADS, W1, HC]), ALU.mult).then_inc(sig["at_norm"], 1)

                    def copy_run(k):
                        g, half, _, end = RUNS[k]
                        dve.wait_ge(sig["at_out"], end)
                        side = 8 if g == 0 else 16
                        src = p_o[:, k % 2].rearrange("p (u v y x) -> p u v y x", v=SIDE // side, y=side, x=side)
                        dst = og[:, WITHIN[g], half * BANK:(half + 1) * BANK].rearrange("p (u y v x) -> p u v y x", v=SIDE // side, y=side, x=side)
                        for u in range(16 // side):
                            last = dve.tensor_copy(dst[:, u], src[:, u])
                        last.then_inc(sig["at_og"], 1)

                    scores(sc3, st3, prod3, pos4, HC_SCALE, 1, 2 * NB)
                    scores(sc1, st1, prod1, pos2, HC_SCALE, 2, 1)
                    for i in range(EARLY, NU + 1):
                        if i < NU:
                            biased(dve, p_s[:, i % 2], i)
                        if i > EARLY:
                            normalised(dve, i - 1)
                        if i == FINISH3:
                            finish3()
                        if i == FINISH1:
                            finish1()
                        if i in COPY:
                            copy_run(COPY[i])
                    copy_run(3)
                    for h, c in halves():
                        dve.wait_ge(sig["at_mixed"], 2 * (h + 1))
                        dve.scalar_tensor_tensor(x[:, c], p_x[0:R, c], abo[:, 0:1], x[:, c], ALU.add, ALU.add)
                    unchain(link, "dve")

                @block.scalar
                def _(act):
                    for i in range(2, NU + 2):
                        if EARLY <= i < NU:
                            exponentials(act, i)
                        u = i - 2
                        act.wait_ge(sig["at_turned"], u + 1)
                        if u >= 2:
                            act.wait_ge(sig["at_out"], u - 1)
                        act.copy(pt[:, u % 2], p_t[:, u % 2]).then_inc(sig["at_pt"], 1)
                        if i == EXP3:
                            act.wait_ge(sig["at_shifted"], 1)
                            act.activation(sc3[:], sc3[:], ACT.Exp).then_inc(sig["at_exp_across"], 1)
                        if i == EXP1:
                            act.wait_ge(sig["at_shifted"], 2)
                            act.activation(sc1[:], sc1[:], ACT.Exp).then_inc(sig["at_exp_across"], 1)
                        if i == TURN_OUT:
                            act.wait_ge(sig["at_turned_out"], 1)
                            act.copy(o_chan[:], p_turned).then_inc(sig["at_chan"], 1)

                @block.gpsimd
                def _(pool):
                    for n in range(NC3):
                        f, b, h = n // 4, n // 2 % 2, n % 2
                        ours = e3[:, f, :, b, 0, h].rearrange("p (i a) c -> p i a c", a=1).broadcast_to([128, W3, W3, HC])
                        theirs = e3[:, f, :, b, 1, h].rearrange("p (a j) c -> p a j c", a=1).broadcast_to([128, W3, W3, HC])
                        last = pool.tensor_tensor(prod3[:, n].rearrange("p (i j c) -> p i j c", i=W3, j=W3), ours, theirs, ALU.mult)
                    last.then_inc(sig["at_prod"], 1)
                    for h in range(HEADS):
                        ours = e1[:, :, 0, h].rearrange("p (i a) c -> p i a c", a=1).broadcast_to([128, W1, W1, HC])
                        theirs = e1[:, :, 1, h].rearrange("p (a j) c -> p a j c", a=1).broadcast_to([128, W1, W1, HC])
                        last = pool.tensor_tensor(prod1[:, h].rearrange("p (i j c) -> p i j c", i=W1, j=W1), ours, theirs, ALU.mult)
                    last.then_inc(sig["at_prod"], 1)
                    pool.wait_ge(sig["at_exp_across"], 1)
                    for n in range(NC3):
                        f, b, h = n // 4, n // 2 % 2, n % 2
                        weight = sc3[:, n * W3:(n + 1) * W3].rearrange("p i (a j) -> p i a j", a=1).broadcast_to([128, W3, HC, W3])
                        value = e3[:, f, :, b, 2, h].rearrange("p j (a c) -> p a c j", a=1).broadcast_to([128, W3, HC, W3])
                        last = pool.tensor_tensor(pv3[:, n].rearrange("p (i c j) -> p i c j", i=W3, c=HC), weight, value, ALU.mult)
                    last.then_inc(sig["at_prod"], 1)
                    pool.wait_ge(sig["at_exp_across"], 2)
                    for h in range(HEADS):
                        weight = sc1[:, h * W1:(h + 1) * W1].rearrange("p i (a j) -> p i a j", a=1).broadcast_to([128, W1, HC, W1])
                        value = e1[:, :, 2, h].rearrange("p j (a c) -> p a c j", a=1).broadcast_to([128, W1, HC, W1])
                        last = pool.tensor_tensor(pv1[:, h].rearrange("p (i c j) -> p i c j", i=W1, c=HC), weight, value, ALU.mult)
                    last.then_inc(sig["at_prod"], 1)

    experts("L3", 1)

    with ExitStack() as st:
        o_tok = sb("o_tok", [128, T // 128, NB, C], stack=st)
        p_o = ps("fp_o", [128, T // 128 * R], stack=st)
        with nc.Block() as block:
            @block.tensor
            def _(pe):
                for j in range(T // 128):
                    last = pe.transpose(p_o[:, j * R:(j + 1) * R], x[:, j * 128:(j + 1) * 128], ident[0:R, 0:R])
                last.then_inc(sig["out_turned"], 1)

            @block.vector
            def _(dve):
                dve.wait_ge(sig["out_turned"], 1)
                dve.tensor_copy(o_tok[:].rearrange("p j b c -> p (j b c)"), p_o[:]).then_inc(sig["out_tok"], 1)

            @block.sync
            def _(sp):
                sp.wait_ge(sig["out_tok"], 1)
                for b in range(NB):
                    sp.dma_start(io["out"][b].rearrange("(j p) c -> p j c", p=128), o_tok[:, :, b, :]).then_inc(sig["stored"], 16)
                sp.wait_ge(sig["stored"], 32)
def scan_orders():
    def curve(n, px, py):
        d, s = 0, n // 2
        while s > 0:
            rx = 1 if px & s > 0 else 0
            ry = 1 if py & s > 0 else 0
            d += s * s * (3 * rx ^ ry)
            if ry == 0:
                if rx == 1:
                    px, py = s - 1 - px, s - 1 - py
                px, py = py, px
            s //= 2
        return d

    along = np.argsort(np.array([curve(WIN, i, j) for j in range(WIN) for i in range(WIN)]))
    rows = [(b, int(q)) for q in along for b in range(NB)]
    cols = [(b, int(q) % WIN * WIN + int(q) // WIN) for q in along for b in range(NB)]
    return [rows, cols, rows[::-1], cols[::-1]]


def constants():
    perm = np.zeros((L, 4, L), np.float32)
    for k, order in enumerate(scan_orders()):
        for l, (b, pos) in enumerate(order):
            perm[b * POS + pos, k, l] = 1.0
    pick = np.zeros((3, 2, NS, NS, 2, D), np.float32)
    for n in range(NS):
        for back in range(2):
            pick[:, back, n, n, back, :] = 1.0
    own = np.zeros((NB * E, NB), np.float32)
    for b in range(NB):
        own[b * E:(b + 1) * E, b] = 1.0
    own_one = np.zeros((3, 6, 6), np.float32)
    for k in range(3):
        own_one[k, :, 2 * k:2 * k + 2] = 1.0
    return {
        "ident": np.eye(128, dtype=np.float32),
        "perm": perm,
        "unperm": np.ascontiguousarray(perm.transpose(2, 1, 0)),
        "pick": pick.reshape(96, NS, 128),
        "own": own,
        "own_one": own_one,
    }


def two(w):
    k, m = w.shape[0], w.shape[-1]
    out = np.zeros((2, k) + w.shape[1:-1] + (2, m), np.float32)
    out[0, ..., 0, :] = w
    out[1, ..., 1, :] = w
    return out.reshape((2 * k,) + w.shape[1:-1] + (2 * m,))


def twice(v):
    return np.concatenate([v, v], axis=0)


def column(v, rows):
    return np.ascontiguousarray(np.broadcast_to(np.reshape(v, (1, -1)), (rows, np.size(v))))


def pack(i):
    a = dict(constants())
    a["x"] = i["x"].reshape(NB, T, C)
    p = "L0_conv_"
    w_in = i[p + "in_proj_w"]
    a["w_in"] = np.stack([two(w_in[:D].T), two(w_in[D:].T)], axis=1)
    a["w_conv"] = twice(i[p + "conv_w"].reshape(D, 9))
    a["b_conv"] = twice(i[p + "conv_b"].reshape(D, 1))
    xp = i[p + "x_proj_w"]
    w_bc = np.zeros((2, D, 2, 2, 2, NS), np.float32)
    for back in range(2):
        for kl in range(2):
            for t in range(2):
                w_bc[back, :, kl, t, back, :] = xp[2 * back + kl, RANK + t * NS:RANK + (t + 1) * NS].T
    a["w_bc"] = w_bc.reshape(2 * D, 2, 4 * NS)
    a["xw"] = xp[:, :RANK].transpose(1, 0, 2)
    a["dtw"] = i[p + "dt_projs_w"].transpose(2, 0, 1)
    a["b_dt"] = i[p + "dt_projs_b"].reshape(2, 2, D).transpose(0, 2, 1).reshape(128, 2)
    a["a_log"] = i[p + "A_logs"].reshape(2, 2, D, NS).transpose(0, 2, 1, 3).reshape(128, 2, NS)
    a["skip"] = i[p + "Ds"].reshape(2, 2, D).transpose(0, 2, 1).reshape(128, 2)
    a["w_out"] = two(i[p + "out_proj_w"].T)
    a["ln_w"] = twice(i[p + "ln_w"].reshape(D, 1))
    a["ln_b"] = twice(i[p + "ln_b"].reshape(D, 1))
    for l in ("L0", "L2"):
        a[l + "_W"] = twice(i[l + "_ffn_W"].T)
        v = np.zeros((2 * C, 128), np.float32)
        v[:C, :C] = i[l + "_ffn_V"].T
        v[C:, :C] = np.eye(C, dtype=np.float32)
        a[l + "_V"] = v
        gb = np.zeros((2 * C, 2), np.float32)
        gb[C:, 0] = i[l + "_ffn_gamma"]
        gb[C:, 1] = i[l + "_ffn_beta"]
        a[l + "_gb"] = gb
    a["bin_w"] = twice(i["L1_conv_W"].transpose(2, 0, 1, 3).reshape(C, 9 * C))
    a["bin_s"] = column(np.concatenate([i["L1_conv_beta"], i["L1_conv_v"], i["L1_conv_bias"]]), R)
    for l in ("L1", "L3"):
        a[l + "_gate"] = two(i[l + "_ffn_gate_w"].T)
        a[l + "_gate_b"] = twice(i[l + "_ffn_gate_b"].reshape(E, 1))
        w = i[l + "_ffn_weight1"]
        o = np.zeros((3 * C + 3, 6, HID), np.float32)
        for e in range(E):
            o[e % 3 * C:(e % 3 + 1) * C, e // 3] = w[e, :C]
            o[3 * C + e % 3, e // 3] = w[e, C]
        a[l + "_w1"] = o
        a[l + "_w2"] = i[l + "_ffn_weight2"][:, :HID].transpose(1, 0, 2)
        a[l + "_b2"] = i[l + "_ffn_weight2"][:, HID].T
    cf = i["L2_conv_coefs"]
    a["eq_w"] = two(cf.transpose(0, 2, 1))
    a["eq_b"] = twice(np.stack([i["L2_conv_bias"].reshape(C), i["L2_conv_diag_bias"].reshape(C)], axis=1))
    w = {n: i["L3_conv_W" + n].reshape(C, 4, 2, 4) for n in "qkv"}
    for n in "qk":
        o = np.zeros((2, C, 2, 2, 2, 32), np.float32)
        for b in range(2):
            o[b, :, :, b, :, :4] = w[n][:, [2, 0]]
        a["at_" + n] = o.reshape(2 * C, 2, 128)
    o = np.zeros((2, C, 2, 2, 8), np.float32)
    e1 = np.zeros((2, C, 2, 3, 8), np.float32)
    for b in range(2):
        o[b, :, :, b] = w["v"][:, [2, 0]].reshape(C, 2, 8)
        for t, n in enumerate("qkv"):
            e1[b, :, b, t] = w[n][:, 1].reshape(C, 8)
    a["at_v"] = o.reshape(2 * C, 2, 16)
    a["at_e1"] = e1.reshape(2 * C, 2, 24)
    e3 = np.zeros((2, C, 2, 3, 8), np.float32)
    for b in range(2):
        for t, n in enumerate("qkv"):
            e3[b, :, b, t] = w[n][:, 3].reshape(C, 8)
    a["at_e3"] = e3.reshape(2 * C, 48)
    wo = i["L3_conv_Wo"].reshape(4, 8, C)
    o = np.zeros((2, 128, 512), np.float32)
    for n in range(8):
        for b in range(2):
            o[0, n * 16 + b * 8:n * 16 + b * 8 + 8, n * 2 * C + b * C:n * 2 * C + (b + 1) * C] = wo[3]
    for n in range(16):
        o[1, n * 8:(n + 1) * 8, n * C:(n + 1) * C] = wo[1]
    a["at_o"] = o.transpose(1, 0, 2)
    o = np.zeros((2, 2, 32, 2, 2, C), np.float32)
    for b in range(2):
        for n, g in enumerate((2, 0)):
            o[b, :, :4, n, b, :] = wo[g].reshape(2, 4, C)
    a["at_ow"] = o.reshape(128, 2, 2 * C)
    a["at_bo"] = twice(i["L3_conv_bo"].reshape(C, 1))
    pos = i["L3_conv_pos1"].reshape(2, 64, 64)
    o = np.full((128, 2, 128), MASKED, np.float32)
    for s in range(2):
        o[s * 64:(s + 1) * 64, :, s * 64:(s + 1) * 64] = pos.transpose(1, 0, 2)
    a["pos1"] = o
    a["pos2"] = column(i["L3_conv_pos2"], 128)
    a["pos3"] = i["L3_conv_pos3"].reshape(2, 2, 128, 256).transpose(2, 1, 0, 3)
    a["pos4"] = column(i["L3_conv_pos4"], 128)
    return {k: np.ascontiguousarray(v) for k, v in a.items()}


def kernel(**inputs):
    import concourse.bacc as bacc
    from concourse.bass_utils import run_bass_kernel_spmd

    nc = bacc.Bacc("TRN2", target_bir_lowering=False, num_devices=1)
    arrays = pack({k: np.asarray(v) for k, v in inputs.items()})
    io = {n: nc.dram_tensor(f"in_{n}", a.shape, mybir.dt.from_np(a.dtype), kind="ExternalInput").ap()
          for n, a in arrays.items()}
    io["out"] = nc.dram_tensor("out_x", (NB, T, C), F32, kind="ExternalOutput").ap()
    build_program(nc, io)
    r = run_bass_kernel_spmd(nc, [{f"in_{n}": a for n, a in arrays.items()}], core_ids=[0])
    return r.results[0]["out_x"].reshape(NB, SIDE, SIDE, C)
```
